# Optimizing a Trainium2 kernel written in Bass

```python
import numpy as np
import jax
import jax.numpy as jnp

def _softmax(x, axis=-1):
    return jax.nn.softmax(x, axis=axis)

def _gelu(x):
    return jax.nn.gelu(x, approximate=True)

def _silu(x):
    return jax.nn.silu(x)

def _sigmoid(x):
    return jax.nn.sigmoid(x)

def _layernorm(x, axis=-1, eps=1e-05):
    m = jnp.mean(x, axis=axis, keepdims=True)
    v = jnp.var(x, axis=axis, keepdims=True)
    return (x - m) / jnp.sqrt(v + eps)

def _scatter_add(tgt, idx, src, axis=0):
    return tgt.at[idx].add(src)

def _segment_sum(src, seg, n):
    return jax.ops.segment_sum(src, seg, n)
kernel_name = 'mk_gnn_resnorm_d4_gnn_r8_a2a342'

def setup_inputs(seed: int=0):
    np.random.seed(seed)
    _w = jnp.asarray

    def _rec_inputs():
        import jax
        import jax.numpy as jnp
        _gk = jax.random.key(seed)
        x = -0.0003713 + 1 * jax.random.normal(jax.random.fold_in(_gk, 1), (6250, 256), jnp.float32)
        src = jax.random.randint(jax.random.fold_in(_gk, 2), (100000,), 0, 6250, jnp.int32)
        dst = jax.random.randint(jax.random.fold_in(_gk, 3), (100000,), 0, 6250, jnp.int32)
        _o = jnp.argsort(dst, stable=True)
        src = src[_o]
        dst = dst[_o]
        edge_attr_64 = 0.000283511 + 1.00007 * jax.random.normal(jax.random.fold_in(_gk, 12), (100000, 64), jnp.float32)
        edge_type_8 = jax.random.randint(jax.random.fold_in(_gk, 14), (100000,), 0, 8, jnp.int32)
        node_type_4 = jax.random.randint(jax.random.fold_in(_gk, 15), (6250,), 0, 4, jnp.int32)
        return (x, src, dst, edge_attr_64, edge_type_8, node_type_4)
    x, src, dst, edge_attr_64, edge_type_8, node_type_4 = _rec_inputs()

    def _L0_gnn_setup():
        import jax, jax.numpy as jnp
        import numpy as np
        N, E = (6250, 100000)
        IN_DIM = OUT_DIM = 256
        T, R, H = (4, 8, 8)
        DK = OUT_DIM // H

        def typed_linear(x, node_type, W, b):
            out = jnp.zeros((x.shape[0], W.shape[2]), dtype=x.dtype)
            for t in range(W.shape[0]):
                y = x @ W[t] + b[t]
                out = jnp.where((node_type == t)[:, None], y, out)
            return out
        key = jax.random.key(seed)
        ks = jax.random.split(key, 16)
        x = jax.random.normal(ks[0], (N, IN_DIM), dtype=jnp.float32)
        node_type = jax.random.randint(ks[1], (N,), 0, T, dtype=jnp.int32)
        src = jax.random.randint(ks[2], (E,), 0, N, dtype=jnp.int32)
        dst = jnp.arange(E, dtype=jnp.int32) % N
        etype = jax.random.randint(ks[3], (E,), 0, R, dtype=jnp.int32)
        w_scale = np.sqrt(2.0 / (IN_DIM + OUT_DIM)).astype(np.float32)
        r_scale = np.sqrt(2.0 / (DK + DK)).astype(np.float32)

        def lin(k):
            return jax.random.normal(k, (T, IN_DIM, OUT_DIM), dtype=jnp.float32) * w_scale
        return {'x': x, 'node_type': node_type, 'src': src, 'dst': dst, 'etype': etype, 'Wk': lin(ks[4]), 'bk': jnp.zeros((T, OUT_DIM), jnp.float32), 'Wq': lin(ks[5]), 'bq': jnp.zeros((T, OUT_DIM), jnp.float32), 'Wv': lin(ks[6]), 'bv': jnp.zeros((T, OUT_DIM), jnp.float32), 'Wa': lin(ks[7]), 'ba': jnp.zeros((T, OUT_DIM), jnp.float32), 'rel_att': jax.random.normal(ks[8], (R, H, DK, DK), jnp.float32) * r_scale, 'rel_msg': jax.random.normal(ks[9], (R, H, DK, DK), jnp.float32) * r_scale, 'rel_pri': jnp.ones((R, H), jnp.float32), 'skip': jnp.ones((T,), jnp.float32)}
    _L0_gnn_all = _L0_gnn_setup()
    _L0_gnn_in = {k: v for k, v in _L0_gnn_all.items() if k in ('Wk', 'bk', 'Wq', 'bq', 'Wv', 'bv', 'Wa', 'ba', 'rel_att', 'rel_msg', 'rel_pri', 'skip')}
    del _L0_gnn_all

    def _L1_gnn_setup():
        import jax, jax.numpy as jnp
        import numpy as np
        N_NODES = 3125
        HEADS = 4
        HID = 64
        NEG_SLOPE = 0.2
        EPS = 1e-16

        def _gat_conv(x, src, dst, W, a_src, a_dst, b):
            N = x.shape[0]
            h = (x @ W).reshape(N, HEADS, HID)
            e_src = jnp.einsum('nhd,hd->nh', h, a_src)
            e_dst = jnp.einsum('nhd,hd->nh', h, a_dst)
            e = jax.nn.leaky_relu(e_src[src] + e_dst[dst], NEG_SLOPE)
            m = jax.ops.segment_max(e, dst, num_segments=N)
            ex = jnp.exp(e - m[dst])
            denom = jax.ops.segment_sum(ex, dst, num_segments=N)
            alpha = ex / (denom[dst] + EPS)
            msg = h[src] * alpha[:, :, None]
            out = jax.ops.segment_sum(msg, dst, num_segments=N)
            return out.reshape(N, HEADS * HID) + b
        key = jax.random.key(seed)
        ks = jax.random.split(key, 10)
        E = 50000
        F_in = 256
        x = jax.random.normal(ks[0], (N_NODES, F_in), dtype=jnp.float32)
        edge_index = jax.random.randint(ks[1], (2, E), 0, N_NODES, dtype=jnp.int64)
        s = 0.1
        return {'x': x, 'edge_index': edge_index, 'W0': s * jax.random.normal(ks[2], (F_in, HEADS * HID), dtype=jnp.float32), 'a_src0': s * jax.random.normal(ks[3], (HEADS, HID), dtype=jnp.float32), 'a_dst0': s * jax.random.normal(ks[4], (HEADS, HID), dtype=jnp.float32), 'b0': jnp.zeros((HEADS * HID,), dtype=jnp.float32), 'W1': s * jax.random.normal(ks[5], (HEADS * HID, HEADS * HID), dtype=jnp.float32), 'a_src1': s * jax.random.normal(ks[6], (HEADS, HID), dtype=jnp.float32), 'a_dst1': s * jax.random.normal(ks[7], (HEADS, HID), dtype=jnp.float32), 'b1': jnp.zeros((HEADS * HID,), dtype=jnp.float32)}
    _L1_gnn_all = _L1_gnn_setup()
    _L1_gnn_in = {k: v for k, v in _L1_gnn_all.items() if k in ('W0', 'a_src0', 'a_dst0', 'b0', 'W1', 'a_src1', 'a_dst1', 'b1')}
    del _L1_gnn_all

    def _L2_gnn_setup():
        import jax, jax.numpy as jnp
        import numpy as np
        N_NODES = 3125
        N_EDGES = 37500
        D_NODE = 256
        D_EDGE = 64
        LN_EPS = 0.001
        key = jax.random.key(seed)
        k1, k2, k3, k4 = jax.random.split(key, 4)
        node_features = jax.random.normal(k1, (N_NODES, D_NODE), dtype=jnp.float32)
        edge_index = jax.random.randint(k2, (2, N_EDGES), 0, N_NODES, dtype=jnp.int32)
        edge_features = jax.random.normal(k3, (N_EDGES, D_EDGE), dtype=jnp.float32)
        W = jax.random.normal(k4, (D_NODE + D_EDGE, D_NODE), dtype=jnp.float32) * (1.0 / np.sqrt(D_NODE + D_EDGE))
        b = jnp.zeros((D_NODE,), dtype=jnp.float32)
        gamma = jnp.ones((D_NODE,), dtype=jnp.float32)
        beta = jnp.zeros((D_NODE,), dtype=jnp.float32)
        return {'node_features': node_features, 'edge_index': edge_index, 'edge_features': edge_features, 'W': W, 'b': b, 'gamma': gamma, 'beta': beta}
    _L2_gnn_all = _L2_gnn_setup()
    _L2_gnn_in = {k: v for k, v in _L2_gnn_all.items() if k in ('W', 'b', 'gamma', 'beta')}
    del _L2_gnn_all

    def _L3_gnn_setup():
        import jax, jax.numpy as jnp
        import numpy as np
        N_NODES = 2500
        N_EDGES = 40000
        NUM_RELS = 8
        DIM = 256
        BN_EPS = 1e-05
        key = jax.random.key(seed)
        k1, k2, k3, k4, k5 = jax.random.split(key, 5)
        h = jax.random.normal(k1, (N_NODES, DIM), dtype=jnp.float32)
        weight = jax.random.normal(k2, (NUM_RELS, DIM, DIM), dtype=jnp.float32) * 0.05
        gamma = jnp.ones((DIM,), dtype=jnp.float32)
        beta = jnp.zeros((DIM,), dtype=jnp.float32)
        src = jax.random.randint(k3, (N_EDGES,), 0, N_NODES, dtype=jnp.int32)
        dst = jax.random.randint(k4, (N_EDGES,), 0, N_NODES, dtype=jnp.int32)
        rel = jax.random.randint(k5, (N_EDGES,), 0, NUM_RELS, dtype=jnp.int32)
        return {'h': h, 'weight': weight, 'gamma': gamma, 'beta': beta, 'src': src, 'dst': dst, 'rel': rel}
    _L3_gnn_all = _L3_gnn_setup()
    _L3_gnn_in = {k: v for k, v in _L3_gnn_all.items() if k in ('weight', 'gamma', 'beta')}
    del _L3_gnn_all
    return {'x': x, 'src': src, 'dst': dst, 'edge_attr_64': edge_attr_64, 'edge_type_8': edge_type_8, 'node_type_4': node_type_4, 'L0_gnn_Wk': _L0_gnn_in['Wk'], 'L0_gnn_bk': _L0_gnn_in['bk'], 'L0_gnn_Wq': _L0_gnn_in['Wq'], 'L0_gnn_bq': _L0_gnn_in['bq'], 'L0_gnn_Wv': _L0_gnn_in['Wv'], 'L0_gnn_bv': _L0_gnn_in['bv'], 'L0_gnn_Wa': _L0_gnn_in['Wa'], 'L0_gnn_ba': _L0_gnn_in['ba'], 'L0_gnn_rel_att': _L0_gnn_in['rel_att'], 'L0_gnn_rel_msg': _L0_gnn_in['rel_msg'], 'L0_gnn_rel_pri': _L0_gnn_in['rel_pri'], 'L0_gnn_skip': _L0_gnn_in['skip'], 'L1_gnn_W0': _L1_gnn_in['W0'], 'L1_gnn_a_src0': _L1_gnn_in['a_src0'], 'L1_gnn_a_dst0': _L1_gnn_in['a_dst0'], 'L1_gnn_b0': _L1_gnn_in['b0'], 'L1_gnn_W1': _L1_gnn_in['W1'], 'L1_gnn_a_src1': _L1_gnn_in['a_src1'], 'L1_gnn_a_dst1': _L1_gnn_in['a_dst1'], 'L1_gnn_b1': _L1_gnn_in['b1'], 'L2_gnn_W': _L2_gnn_in['W'], 'L2_gnn_b': _L2_gnn_in['b'], 'L2_gnn_gamma': _L2_gnn_in['gamma'], 'L2_gnn_beta': _L2_gnn_in['beta'], 'L3_gnn_weight': _L3_gnn_in['weight'], 'L3_gnn_gamma': _L3_gnn_in['gamma'], 'L3_gnn_beta': _L3_gnn_in['beta']}

def reference(x, src, dst, edge_attr_64, edge_type_8, node_type_4, L0_gnn_Wk, L0_gnn_bk, L0_gnn_Wq, L0_gnn_bq, L0_gnn_Wv, L0_gnn_bv, L0_gnn_Wa, L0_gnn_ba, L0_gnn_rel_att, L0_gnn_rel_msg, L0_gnn_rel_pri, L0_gnn_skip, L1_gnn_W0, L1_gnn_a_src0, L1_gnn_a_dst0, L1_gnn_b0, L1_gnn_W1, L1_gnn_a_src1, L1_gnn_a_dst1, L1_gnn_b1, L2_gnn_W, L2_gnn_b, L2_gnn_gamma, L2_gnn_beta, L3_gnn_weight, L3_gnn_gamma, L3_gnn_beta):
    import jax
    import jax.numpy as jnp

    def _L0_gnn_ref(x, node_type, src, dst, etype, Wk, bk, Wq, bq, Wv, bv, Wa, ba, rel_att, rel_msg, rel_pri, skip):
        import jax, jax.numpy as jnp
        import numpy as np
        N, E = (6250, 100000)
        IN_DIM = OUT_DIM = 256
        T, R, H = (4, 8, 8)
        DK = OUT_DIM // H

        def typed_linear(x, node_type, W, b):
            out = jnp.zeros((x.shape[0], W.shape[2]), dtype=x.dtype)
            for t in range(W.shape[0]):
                y = x @ W[t] + b[t]
                out = jnp.where((node_type == t)[:, None], y, out)
            return out
        n = x.shape[0]
        r = rel_att.shape[0]
        h, dk = (rel_att.shape[1], rel_att.shape[2])
        sqrt_dk = jnp.asarray(np.sqrt(dk), x.dtype)
        k = typed_linear(x, node_type, Wk, bk).reshape(n, h, dk)
        q = typed_linear(x, node_type, Wq, bq).reshape(n, h, dk)
        v = typed_linear(x, node_type, Wv, bv).reshape(n, h, dk)
        k_r = jnp.einsum('nhd,rhde->rnhe', k, rel_att)
        v_r = jnp.einsum('nhd,rhde->rnhe', v, rel_msg)
        key_e = k_r[etype, src]
        val_e = v_r[etype, src]
        att = (q[dst] * key_e).sum(-1) * rel_pri[etype] / sqrt_dk
        seg = dst * r + etype
        s = n * r
        m = jax.ops.segment_max(att, seg, num_segments=s)
        ex = jnp.exp(att - m[seg])
        den = jax.ops.segment_sum(ex, seg, num_segments=s)
        alpha = ex / den[seg]
        hmsg = jax.ops.segment_sum(alpha[..., None] * val_e, seg, num_segments=s)
        hmsg = hmsg.reshape(n, r, h * dk)
        cnt = jax.ops.segment_sum(jnp.ones((att.shape[0],), x.dtype), seg, num_segments=s)
        present = (cnt.reshape(n, r) > 0).astype(x.dtype)
        t = hmsg.sum(1) / jnp.maximum(present.sum(1, keepdims=True), 1.0)
        trans = typed_linear(t, node_type, Wa, ba)
        a = jax.nn.sigmoid(skip)[node_type][:, None]
        return trans * a + x * (1.0 - a)

    def _L1_gnn_ref(x, edge_index, W0, a_src0, a_dst0, b0, W1, a_src1, a_dst1, b1):
        import jax, jax.numpy as jnp
        import numpy as np
        N_NODES = 3125
        HEADS = 4
        HID = 64
        NEG_SLOPE = 0.2
        EPS = 1e-16

        def _gat_conv(x, src, dst, W, a_src, a_dst, b):
            N = x.shape[0]
            h = (x @ W).reshape(N, HEADS, HID)
            e_src = jnp.einsum('nhd,hd->nh', h, a_src)
            e_dst = jnp.einsum('nhd,hd->nh', h, a_dst)
            e = jax.nn.leaky_relu(e_src[src] + e_dst[dst], NEG_SLOPE)
            m = jax.ops.segment_max(e, dst, num_segments=N)
            ex = jnp.exp(e - m[dst])
            denom = jax.ops.segment_sum(ex, dst, num_segments=N)
            alpha = ex / (denom[dst] + EPS)
            msg = h[src] * alpha[:, :, None]
            out = jax.ops.segment_sum(msg, dst, num_segments=N)
            return out.reshape(N, HEADS * HID) + b
        N = x.shape[0]
        loops = jnp.arange(N, dtype=edge_index.dtype)
        src = jnp.concatenate([edge_index[0], loops])
        dst = jnp.concatenate([edge_index[1], loops])
        h = jax.nn.relu(_gat_conv(x, src, dst, W0, a_src0, a_dst0, b0))
        h = jax.nn.relu(_gat_conv(h, src, dst, W1, a_src1, a_dst1, b1))
        return h

    def _L2_gnn_ref(node_features, edge_index, edge_features, W, b, gamma, beta):
        import jax, jax.numpy as jnp
        import numpy as np
        N_NODES = 3125
        N_EDGES = 37500
        D_NODE = 256
        D_EDGE = 64
        LN_EPS = 0.001
        source = edge_index[0]
        target = edge_index[1]
        msgs = jnp.concatenate([node_features[source], edge_features], axis=-1)
        msgs = jax.nn.silu(msgs @ W + b)
        out = jax.ops.segment_sum(msgs, target, num_segments=node_features.shape[0])
        mean = jnp.mean(out, axis=-1, keepdims=True)
        var = jnp.mean(jnp.square(out - mean), axis=-1, keepdims=True)
        out = (out - mean) * jax.lax.rsqrt(var + LN_EPS) * gamma + beta
        return out

    def _L3_gnn_ref(h, weight, gamma, beta, src, dst, rel):
        import jax, jax.numpy as jnp
        import numpy as np
        N_NODES = 2500
        N_EDGES = 40000
        NUM_RELS = 8
        DIM = 256
        BN_EPS = 1e-05
        all_h = jnp.einsum('ni,rio->nro', h, weight)
        msg = all_h[src, rel]
        agg = jax.ops.segment_sum(msg, dst, num_segments=h.shape[0])
        mean = jnp.mean(agg, axis=0)
        var = jnp.mean(jnp.square(agg - mean), axis=0)
        out = (agg - mean) * jax.lax.rsqrt(var + BN_EPS) * gamma + beta
        return out
    edge_index = jnp.stack([src, dst])
    x = _layernorm(x + _L0_gnn_ref(x, node_type_4, src, dst, edge_type_8, L0_gnn_Wk, L0_gnn_bk, L0_gnn_Wq, L0_gnn_bq, L0_gnn_Wv, L0_gnn_bv, L0_gnn_Wa, L0_gnn_ba, L0_gnn_rel_att, L0_gnn_rel_msg, L0_gnn_rel_pri, L0_gnn_skip), axis=-1)
    x = _layernorm(x + _L1_gnn_ref(x, edge_index, L1_gnn_W0, L1_gnn_a_src0, L1_gnn_a_dst0, L1_gnn_b0, L1_gnn_W1, L1_gnn_a_src1, L1_gnn_a_dst1, L1_gnn_b1), axis=-1)
    x = _layernorm(x + _L2_gnn_ref(x, edge_index, edge_attr_64, L2_gnn_W, L2_gnn_b, L2_gnn_gamma, L2_gnn_beta), axis=-1)
    x = _layernorm(x + _L3_gnn_ref(x, L3_gnn_weight, L3_gnn_gamma, L3_gnn_beta, src, dst, edge_type_8), axis=-1)
    return x

_drawn_inputs = setup_inputs


def setup_inputs(seed=0):
    import zlib

    import numpy as np

    out = dict(_drawn_inputs(seed))
    spreads = {'L0_gnn_bk': (0.0, 0.8),
     'L0_gnn_bq': (0.0, 0.8),
     'L0_gnn_bv': (0.0, 0.417),
     'L0_gnn_ba': (0.0, 0.1),
     'L0_gnn_rel_pri': (1.0, 0.6),
     'L0_gnn_skip': (1.0, 0.6),
     'L1_gnn_b0': (0.0, 0.1),
     'L1_gnn_b1': (0.0, 0.1),
     'L2_gnn_b': (0.0, 0.1),
     'L2_gnn_gamma': (1.0, 0.2),
     'L2_gnn_beta': (0.0, 0.1),
     'L3_gnn_gamma': (1.0, 0.2),
     'L3_gnn_beta': (0.0, 0.1)}
    factors = {'L1_gnn_a_dst1': 6.307}
    for name, (base, spread) in spreads.items():
        noise = np.random.default_rng([zlib.crc32(name.encode()), seed]).standard_normal(out[name].shape)
        drawn = base * np.exp(spread * noise) if base else spread * noise
        out[name] = jnp.asarray(drawn.astype(out[name].dtype))
    for name, factor in factors.items():
        out[name] = (out[name] * factor).astype(out[name].dtype)
    return out
```

```python
from contextlib import ExitStack

import concourse.bass as bass
from concourse import mybir

fp32 = mybir.dt.float32
i32 = mybir.dt.int32
ALU = mybir.AluOpType
ACT = mybir.ActivationFunctionType
AX = mybir.AxisListType

P = 128
N, E = 6250, 100000
D = 256
TYPES, RELS, HEADS = 4, 8, 8
DK = D // HEADS
GHEADS = 4
GHID = D // GHEADS
DE = 64
T = -(-N // P)
NP = T * P
C = -(-E // P)
EP = C * P
J = C
S = -(-(C + T) // 8) * 8
CB = -(-C // P)
SH = S // 2
GW = 4
HROW = D + 8
BIG = 1e30
ds = bass.ds


class Shared:

    def __init__(self, nc):
        self.nc = nc
        self.used = []

    def semaphore(self, name):
        self.used.append(self.nc.alloc_semaphore(name))
        return self.used[-1]

    def recycle(self):
        self.nc.clear_and_free_semaphores(self.used)
        self.used = []
        self.nc.all_engine_barrier()


def col(ap2, w):
    return ap2.unsqueeze(2).to_broadcast([ap2.shape[0], ap2.shape[1], w])


def grouped(eng, groups, body, last=0):
    pairs = max(1, (groups - last) // 2)
    for kk in range(min(2, groups)):
        body(kk, kk, 0)
    if pairs > 1:
        with eng.Fori(1, pairs) as i:
            body(i * 2, 0, i)
            body(i * 2 + 1, 1, i)
    for kk in range(2 * pairs, groups):
        body(kk, kk % 2, kk // 2)


def after(k, count):
    return not isinstance(k, int) or k >= count


def before(k, end):
    return not isinstance(k, int) or k < end


def chained(eng, sem):
    count = [0]

    def link(ins):
        count[0] += 1
        ins.then_inc(sem, 1)
        eng.wait_ge(sem, count[0])
    link.count = count
    return link



def segmented_scan(nc, k, ctx, name, items, step_op, join_op, init):
    Q = len(items)
    sb = lambda n, s: ctx.enter_context(nc.sbuf_tensor(f"{name}_{n}", s, fp32))
    last = sb("last", [P, 2, Q])
    lastT = sb("lastT", [Q, 2, P])
    carryT = sb("carryT", [Q, P + 1])
    carry = sb("carry", [P, Q])
    ps = ctx.enter_context(nc.psum_tensor(f"{name}_ps", [P, 512], fp32))
    s_last = (k.semaphore(f"{name}_s_last"))
    s_turned = (k.semaphore(f"{name}_s_turned"))
    s_carryT = (k.semaphore(f"{name}_s_carryT"))
    s_back = (k.semaphore(f"{name}_s_back"))
    assert len({b for *_, b in items}) == 1
    backward = items[0][3]

    def way(v):
        return v[:, ::-1] if backward else v

    def dve_part(link):
        for q, (out, x, gate, _) in enumerate(items):
            link(nc.vector.tensor_tensor_scan(way(out), way(gate), way(x), init, step_op, join_op))
            end = out[:, 0:1] if backward else out[:, J - 1:J]
            link(nc.vector.tensor_copy(last[:, 0, q:q + 1], end))
            link(nc.vector.tensor_reduce(last[:, 1, q:q + 1], gate, AX.X, ALU.min))
        link(nc.vector.tensor_copy(last[:, 0, 0:1], last[:, 0, 0:1]))
        nc.vector.tensor_copy(last[:, 1, 0:1], last[:, 1, 0:1]).then_inc(s_last, 1)
        nc.vector.wait_ge(s_turned, 1)
        link(nc.vector.tensor_copy(lastT[:], ps[0:Q, 0:2 * P].rearrange("q (a p) -> q a p", a=2)))
        if backward:
            link(nc.vector.memset(carryT[:, P:P + 1], init))
            link(nc.vector.tensor_tensor_scan(carryT[:, 0:P][:, ::-1], lastT[:, 1, :][:, ::-1],
                                              lastT[:, 0, :][:, ::-1], init, step_op, join_op))
        else:
            link(nc.vector.memset(carryT[:, 0:1], init))
            link(nc.vector.tensor_tensor_scan(carryT[:, 1:P + 1], lastT[:, 1, :], lastT[:, 0, :],
                                              init, step_op, join_op))
        nc.vector.tensor_copy(lastT[:, 0, :], carryT[:, 1:P + 1] if backward else carryT[:, 0:P])\
            .then_inc(s_carryT, 1)
        nc.vector.wait_ge(s_back, 1)
        link(nc.vector.tensor_copy(carry[:], ps[:, 256:256 + Q]))
        for q, (out, x, gate, _) in enumerate(items):
            link(nc.vector.tensor_tensor_scan(way(out), way(gate), way(x), carry[:, q:q + 1],
                                              step_op, join_op))

    def pe_part(ident):
        nc.tensor.wait_ge(s_last, 1)
        nc.tensor.transpose(ps[0:Q, 0:P], last[:, 0, :], ident)
        nc.tensor.transpose(ps[0:Q, P:2 * P], last[:, 1, :], ident).then_inc(s_turned, 1)
        nc.tensor.wait_ge(s_carryT, 1)
        nc.tensor.transpose(ps[:, 256:256 + Q], lastT[:, 0, :], ident[0:Q, 0:Q]).then_inc(s_back, 1)

    return dve_part, pe_part



def constants(nc, k):
    with ExitStack() as ctx:
        sem = lambda n: (k.semaphore(n))
        s_zero, s_ident = sem("c_zero"), sem("c_ident")
        block = ctx.enter_context(nc.Block())

        @block.gpsimd
        def _(pool):
            pool.memset(k.ident[:], 0.0).then_inc(s_zero, 1)
            pool.iota(k.window_iota[:], [[0, GW], [1, P]], 0, 0, allow_small_or_imprecise_dtypes=True)
            pool.wait_ge(s_zero, 1)
            pool.affine_select(out=k.ident[:], in_=k.ident[:], compare_op=ALU.not_equal, fill=1.0,
                               base=0, pattern=[[-1, P]], channel_multiplier=1).then_inc(s_ident, 1)

        @block.vector
        def _(dve):
            nc.vector.memset(k.ones[:], 1.0)



def plan_steps(nc, k):
    with ExitStack() as ctx:
        sb = lambda n, s, d=fp32: ctx.enter_context(nc.sbuf_tensor(n, s, d))
        sem = lambda n: (k.semaphore(n))
        last_dst = sb("p_last", [P, CB], i32)
        last_win = sb("p_lastwin", [P, CB], i32)
        key = sb("p_key", [P, CB])
        tile_id = sb("p_tile", [P, CB])
        step_iota = sb("p_step", [P, S])
        before = sb("p_before", [P, CB, S])
        tile_of = sb("p_tileof", [P, S])
        window_of = sb("p_windowof", [P, S])
        tile_int = sb("p_tileint", [1, S], i32)
        s_tile, s_stored = sem("p_tile_ready"), sem("p_stored")
        ps = ctx.enter_context(nc.psum_tensor("p_ps", [P, 2, 512], fp32))
        s_in, s_iota, s_ch, s_before, s_sum, s_z = (sem("p_" + n) for n in
                                                    ("in", "iota", "ch", "before", "sum", "z"))
        block = ctx.enter_context(nc.Block())

        @block.gpsimd
        def _(pool):
            pool.iota(step_iota[:], [[1, S]], 0, 0, allow_small_or_imprecise_dtypes=True).then_inc(s_iota, 1)
            pool.iota(tile_id[:], [[P, CB]], 0, 1, allow_small_or_imprecise_dtypes=True).then_inc(s_iota, 1)

        @block.sync
        def _(sp):
            sp.wait_ge(s_z, 1)
            full = C // P
            every = k.dst_ext[1:1 + EP].rearrange("(c p) -> c p", p=P)[:, P - 1:P]
            with nc.allow_non_contiguous_dma(reason="one element of every tile"):
                for b in range(full):
                    sp.dma_start(last_dst[:, b:b + 1], every[b * P:(b + 1) * P, :]).then_inc(s_in, 16)
                sp.dma_start(last_dst[0:C - full * P, full:full + 1],
                             every[full * P:C, :]).then_inc(s_in, 16)
            sp.wait_ge(s_tile, 1)
            sp.dma_start(k.step_tile, tile_int[:]).then_inc(s_stored, 16)
            sp.wait_ge(s_stored, 16)

        @block.vector
        def _(dve):
            link = chained(dve, s_ch)
            nc.vector.memset(last_dst[:], P * 4 * S).then_inc(s_z, 1)
            dve.wait_ge(s_in, 16 * CB)
            dve.wait_ge(s_iota, 2)
            link(nc.vector.tensor_scalar(last_win[:], last_dst[:], 7, None, ALU.arith_shift_right))
            link(nc.vector.tensor_tensor(key[:], last_win[:], tile_id[:], ALU.add))
            for b in range(CB):
                ins = nc.vector.tensor_scalar(before[:, b, :], step_iota[:], key[:, b:b + 1], None, ALU.is_gt)
            ins.then_inc(s_before, 1)
            dve.wait_ge(s_sum, 1)
            link(nc.vector.tensor_copy(tile_of[:].rearrange("p (a s) -> p a s", a=2), ps[:, :, 0:SH]))
            link(nc.vector.tensor_tensor(window_of[:], step_iota[:], tile_of[:], ALU.subtract))
            link(nc.vector.tensor_scalar(window_of[:], window_of[:], float(T - 1), None, ALU.min))
            link(nc.vector.tensor_copy(k.step_window[:], window_of[0:1, :]))
            nc.vector.tensor_scalar(tile_int[:], tile_of[0:1, :], float(C - 1), None, ALU.min).then_inc(s_tile, 1)
            for b in range(CB):
                link(nc.vector.tensor_scalar(k.pick[:, b, :], tile_of[:], tile_id[:, b:b + 1], None,
                                             ALU.is_equal))
            link(nc.vector.tensor_scalar(k.place[:], window_of[:], float(P), 1.0, ALU.mult, ALU.add))

        @block.tensor
        def _(pe):
            pe.wait_ge(s_before, 1)
            for h in range(2):
                for b in range(CB):
                    ins = nc.tensor.matmul(ps[:, h, 0:SH], k.ones[:], before[:, b, h * SH:(h + 1) * SH],
                                           start=(b == 0), stop=(b == CB - 1))
            ins.then_inc(s_sum, 1)


def to_steps(nc, k, name, source, width, picked, integer):
    with ExitStack() as ctx:
        sem = lambda n: (k.semaphore(f"{name}_{n}"))
        dt = i32 if integer else fp32
        raw = ctx.enter_context(nc.sbuf_tensor(name + "_raw", [P, CB, P * width], dt))
        rows = raw
        if integer:
            rows = ctx.enter_context(nc.sbuf_tensor(name + "_rows", [P, CB, P * width], fp32))
        ps = ctx.enter_context(nc.psum_tensor(name + "_ps", [P, 4, 512], fp32))
        s_zero, s_in, s_rows, s_out, s_kept, s_ch = (sem(n) for n in ("zero", "in", "rows", "out", "kept", "ch"))
        block = ctx.enter_context(nc.Block())
        full = C // P

        @block.sync
        def _(sp):
            sp.wait_ge(s_zero, 1)
            sp.dma_start(raw[:, 0:full, :], source[0:full * P, :].rearrange("(b c) w -> c b w", c=P))\
                .then_inc(s_in, 16)
            sp.dma_start(raw[0:C - full * P, full, :], source[full * P:C, :]).then_inc(s_in, 16)

        @block.vector
        def _(dve):
            link = chained(dve, s_ch)
            nc.vector.memset(raw[:, full, :], 0).then_inc(s_zero, 1)
            dve.wait_ge(s_in, 32)
            if integer:
                nc.vector.tensor_copy(rows[:], raw[:]).then_inc(s_rows, 1)
            for n, (q, out, add) in enumerate(picked):
                dve.wait_ge(s_out, n + 1)
                half = ps[:, 2 * (n % 2):2 * (n % 2) + 2, 0:SH]
                o = out.rearrange("p (a s) -> p a s", a=2)
                nc.vector.tensor_scalar(o, half, float(add), None, ALU.add).then_inc(s_kept, 1)

        @block.tensor
        def _(pe):
            if integer:
                pe.wait_ge(s_rows, 1)
            else:
                pe.wait_ge(s_in, 32)
            for n, (q, _, _) in enumerate(picked):
                if n >= 2:
                    pe.wait_ge(s_kept, n - 1)
                for h in range(2):
                    for b in range(CB):
                        lhs = rows[:, b, :].rearrange("c (p w) -> c p w", w=width)[:, :, q]
                        ins = nc.tensor.matmul(ps[:, 2 * (n % 2) + h, 0:SH], lhs,
                                               k.pick[:, b, h * SH:(h + 1) * SH],
                                               start=(b == 0), stop=(b == CB - 1))
                ins.then_inc(s_out, 1)


def steps_of_graph(nc, k):
    to_steps(nc, k, "ts_src", k.src.rearrange("(c p) -> c p", p=P), 1, [(0, k.src_step[:], 0.0)], True)
    with ExitStack() as ctx:
        dst = ctx.enter_context(nc.sbuf_tensor("sg_dst", [P, S], fp32))
        to_steps(nc, k, "ts_dst", k.dst_ext[1:1 + EP].rearrange("(c p) -> c p", p=P), 1,
                 [(0, dst[:], 0.0)], True)
        sem = lambda n: (k.semaphore(n))
        s_ch, s_ps = sem("sg_ch"), sem("sg_ps")
        ps = ctx.enter_context(nc.psum_tensor("sg_ps", [P, 2, 512], fp32))
        block = ctx.enter_context(nc.Block())

        @block.tensor
        def _(pe):
            for h in range(2):
                for b in range(CB):
                    ins = nc.tensor.matmul(ps[:, h, 0:SH], k.ones[:], k.pick[:, b, h * SH:(h + 1) * SH],
                                           start=(b == 0), stop=(b == CB - 1))
            ins.then_inc(s_ps, 1)

        @block.vector
        def _(dve):
            link = chained(dve, s_ch)
            link(nc.vector.tensor_tensor(k.place[:], dst[:], k.place[:], ALU.subtract))
            dve.wait_ge(s_ps, 1)
            o = k.place[:].rearrange("p (a s) -> p a s", a=2)
            link(nc.vector.tensor_tensor(o, o, ps[:, :, 0:SH], ALU.add))



def sort_positions(nc, k):
    with ExitStack() as ctx:
        sb = lambda n, s, d=fp32: ctx.enter_context(nc.sbuf_tensor("so_" + n, s, d))
        sem = lambda n: (k.semaphore("so_" + n))
        vals = sb("vals", [P, 5, J])
        same = sb("same", [P, 2, J])
        hot = sb("hot", [P, RELS + 1, J])
        fwd = sb("fwd", [P, RELS + 1, J])
        bwd = sb("bwd", [P, RELS, J])
        ints = fwd[:, 0:5, :].bitcast(i32)
        tmp = sb("tmp", [P, J])
        sum_ = sb("sum", [P, J])
        s_in, s_ch, s_iota, s_out = sem("in"), sem("ch"), sem("iota"), sem("out")
        scan_f = segmented_scan(nc, k, ctx, "so_f", [(fwd[:, q, :], hot[:, q, :], same[:, 0, :], False)
                                                  for q in range(RELS + 1)], ALU.mult, ALU.add, 0.0)
        scan_b = segmented_scan(nc, k, ctx, "so_b", [(bwd[:, q, :], hot[:, q, :], same[:, 1, :], True)
                                                  for q in range(RELS)], ALU.mult, ALU.add, 0.0)
        block = ctx.enter_context(nc.Block())
        here, prev, nxt, rel, src = range(5)

        @block.gpsimd
        def _(pool):
            pool.iota(hot[:, RELS, :], [[1, J]], 0, J, allow_small_or_imprecise_dtypes=True).then_inc(s_iota, 1)

        @block.sync
        def _(sp):
            for q, view in ((here, k.dst_ext[1:1 + EP]), (prev, k.dst_ext[0:EP]), (nxt, k.dst_ext[2:2 + EP]),
                            (rel, k.rel), (src, k.src)):
                sp.dma_start(ints[:, q, :], view.rearrange("(p j) -> p j", j=J)).then_inc(s_in, 16)

        @block.tensor
        def _(pe):
            scan_f[1](k.ident[:])
            scan_b[1](k.ident[:])

        @block.vector
        def _(dve):
            link = chained(dve, s_ch)
            dve.wait_ge(s_in, 80)
            dve.wait_ge(s_iota, 1)
            v = nc.vector
            link(v.tensor_copy(vals[:], ints))
            link(v.tensor_tensor(same[:, 0, :], vals[:, here, :], vals[:, prev, :], ALU.is_equal))
            link(v.tensor_tensor(same[:, 1, :], vals[:, here, :], vals[:, nxt, :], ALU.is_equal))
            for r in range(RELS):
                link(v.tensor_scalar(hot[:, r, :], vals[:, rel, :], float(r), None, ALU.is_equal))
            link(v.tensor_tensor(tmp[:], hot[:, RELS, :], same[:, 0, :], ALU.mult))
            link(v.tensor_tensor(hot[:, RELS, :], hot[:, RELS, :], tmp[:], ALU.subtract))
            scan_f[0](link)
            scan_b[0](link)
            link(v.tensor_tensor(bwd[:], bwd[:], fwd[:, 0:RELS, :], ALU.add))
            link(v.tensor_tensor(bwd[:], bwd[:], hot[:, 0:RELS, :], ALU.subtract))
            link(v.tensor_copy(sum_[:], fwd[:, RELS, :]))
            link(v.memset(k.rows[:, :, 2], 0.0))
            for r in range(RELS):
                link(v.tensor_tensor(tmp[:], hot[:, r, :], fwd[:, r, :], ALU.mult))
                link(v.tensor_tensor(sum_[:], sum_[:], tmp[:], ALU.add))
                link(v.scalar_tensor_tensor(tmp[:], vals[:, rel, :], float(r), bwd[:, r, :], ALU.is_gt, ALU.mult))
                link(v.tensor_tensor(sum_[:], sum_[:], tmp[:], ALU.add))
                link(v.scalar_tensor_tensor(k.rows[:, :, 2], bwd[:, r, :], 0.0, k.rows[:, :, 2], ALU.is_gt, ALU.add))
            link(v.tensor_copy(k.position[:], sum_[:]))
            link(v.scalar_tensor_tensor(k.rows[:, :, 0], vals[:, src, :], float(RELS), vals[:, rel, :], ALU.mult, ALU.add))
            link(v.scalar_tensor_tensor(k.rows[:, :, 1], vals[:, here, :], float(RELS), vals[:, rel, :], ALU.mult, ALU.add))
            v.tensor_copy(k.rows[:, :, 3], vals[:, here, :])


def scatter_sorted(nc, k, ctx):
    sb = lambda n, s, d=fp32: ctx.enter_context(nc.sbuf_tensor("sc_" + n, s, d))
    sem = lambda n: (k.semaphore("sc_" + n))
    at = sb("at", [P, 2, GW], i32)
    row = sb("row", [P, 2, GW, 4])
    edge = sb("edge", [1, 4])
    s_staged, s_edge, s_ends, s_go = sem("staged"), sem("edge"), sem("ends"), sem("go")
    s_wrote = [sem(f"wrote{g}") for g in range(2)]
    groups, rest = J // GW, J % GW

    def sp_part():
        nc.sync.wait_ge(s_edge, 1)
        nc.sync.dma_start(k.sorted_rows[0:1, :], edge[:]).then_inc(s_ends, 16)
        nc.sync.dma_start(k.sorted_rows[EP + 1:EP + 2, :], edge[:]).then_inc(s_ends, 16)
        nc.sync.wait_ge(s_ends, 32)

    def pool_part():
        pool = nc.gpsimd
        pool.memset(edge[:], -1.0).then_inc(s_edge, 1)

        def write(kk, g, turn, n=GW):
            if after(kk, 2):
                pool.wait_ge(s_wrote[g], turn * (16 * GW))
            pool.tensor_copy(at[:, g, 0:n], k.position[:, ds(kk * GW, n)])
            pool.tensor_copy(row[:, g, 0:n, :], k.rows[:, ds(kk * GW, n), :]).then_inc(s_staged, 1)
            pool.wait_ge(s_staged, kk + 1)
            pool.sem_inc(s_go, 1)
            for q in range(n):
                pool.indirect_dma_start(k.sorted_rows, bass.IndirectOffsetOnAxis(ap=at[:, g, q:q + 1], axis=0),
                                        row[:, g, q, :], None).then_inc(s_wrote[g], 16)

        grouped(pool, groups, write)
        write(groups, groups % 2, groups // 2, rest)
        turns = [(groups + 1 - g) // 2 for g in range(2)]
        for g in range(2):
            extra = 16 * rest if groups % 2 == g else 0
            pool.wait_ge(s_wrote[g], 16 * GW * turns[g] + extra)

    return sp_part, pool_part



def hgt_tables(nc, k):
    FQ = 3 * D
    with ExitStack() as ctx:
        sb = lambda n, s, d=fp32: ctx.enter_context(nc.sbuf_tensor("ht_" + n, s, d))
        ps = lambda n, s: ctx.enter_context(nc.psum_tensor("ht_" + n, s, fp32))
        sem = lambda n: (k.semaphore("ht_" + n))
        scatter_sp, scatter_pool = scatter_sorted(nc, k, ctx)
        w = sb("w", [P, 2 * TYPES, FQ])
        bias = sb("bias", [TYPES, FQ])
        rel_w = sb("rel_w", [P, 2, 2, RELS, P])
        pri = sb("pri", [P, RELS, HEADS])
        xt = sb("xt", [P, 2, D])
        s_xt = [sem(f"xt{g}") for g in range(2)]
        xm = sb("xm", [P, 2, TYPES, D])
        hot = sb("hot", [P, 2, TYPES])
        xT = sb("xT", [P, 2, 2 * TYPES, P])
        maskT = sb("maskT", [TYPES, 2, P])
        q_out = sb("q_out", [P, 2, D])
        kv = sb("kv", [P, 2, 2 * D])
        kvT = sb("kvT", [P, 2, 4, P])
        rel_out = sb("rel_out", [P, 2, 2, RELS, D])
        p_turn = ps("p_turn", [P, 2, 512])
        p_hot = ps("p_hot", [P, 512])
        p_qkv = ps("p_qkv", [P, 2, 512])
        p_kvT = ps("p_kvT", [P, 512])
        p_rel = ps("p_rel", [P, 2, 512])
        s_x, s_zero, s_w, s_ch = (sem(n) for n in ("x", "zero", "w", "ch"))
        s_xm, s_turn, s_xT, s_qkv, s_q, s_kv, s_kvT, s_kvTs, s_rel, s_even, s_odd = (
            sem(n) for n in ("xm", "turn", "xT", "qkv", "q", "kv", "kvT", "kvTs", "rel", "even", "odd"))
        s_qout = [sem(f"qout{g}") for g in range(2)]
        s_relout = [sem(f"relout{g}") for g in range(2)]
        block = ctx.enter_context(nc.Block())

        def rel_piece(g, m):
            kind, half, rh = m // 4, (m // 2) % 2, m % 2
            return rel_out[:, g, kind, 4 * rh:4 * rh + 4, half * P:(half + 1) * P]

        @block.gpsimd
        def _(pool):
            scatter_pool()

        @block.sync
        def _(sp):
            def load(u, g, turn):
                if after(u, 2):
                    sp.wait_ge(s_xm, u - 1)
                sp.dma_start(xt[:, g, :], k.x[ds(u * P, P), :]).then_inc(s_xt[g], 16)

            load(0, 0, 0)
            load(1, 1, 0)
            with nc.allow_non_contiguous_dma(reason="a type for each node"):
                sp.dma_start(k.type_int[:], k.node_type.rearrange("(t p) -> p t", p=P)).then_inc(s_x, 16)
            for n, (wt, bt) in enumerate(((k.L0_Wk, k.L0_bk), (k.L0_Wv, k.L0_bv), (k.L0_Wq, k.L0_bq))):
                sp.dma_start(w[:, :, n * D:(n + 1) * D], wt.rearrange("t (h i) o -> i (t h) o", i=P)).then_inc(s_w, 16)
                sp.dma_start(bias[:, n * D:(n + 1) * D], bt).then_inc(s_w, 16)
            sp.wait_ge(s_zero, 1)
            for m, mat in enumerate((k.L0_rel_att, k.L0_rel_msg)):
                for h in range(HEADS):
                    b = DK * (h % 4)
                    sp.dma_start(rel_w[b:b + DK, m, h // 4, :, b:b + DK],
                                 mat[:, h, :, :].rearrange("r d e -> d r e")).then_inc(s_w, 16)
            sp.dma_start(pri[:], k.L0_rel_pri.partition_broadcast(P)).then_inc(s_w, 16)
            scatter_sp()

            def store(u, g, turn):
                if before(u, T - 2):
                    load(u + 2, g, turn + 1)
                sp.wait_ge(s_q, u + 1)
                sp.dma_start(k.q_table[ds(u * P, P), :], q_out[:, g, :]).then_inc(s_qout[g], 16)
                sp.wait_ge(s_even, u * 4 + 4)
                sp.wait_ge(s_odd, u * 4 + 4)
                for m, table in enumerate((k.kr_table, k.vr_table)):
                    sp.dma_start(table.rearrange("(n r) d -> n r d", r=RELS)[ds(u * P, P), :, :],
                                 rel_out[:, g, m, :, :]).then_inc(s_relout[g], 16)

            grouped(sp, T, store, last=3)
            for g in range(2):
                sp.wait_ge(s_qout[g], 16 * ((T + 1 - g) // 2))
                sp.wait_ge(s_relout[g], 32 * ((T + 1 - g) // 2))

        @block.vector
        def _(dve):
            v = nc.vector
            link = chained(dve, s_ch)
            v.memset(rel_w[:], 0.0).then_inc(s_zero, 1)
            dve.wait_ge(s_x, 16)
            link(v.tensor_copy(k.type_mask[:, :, 0], k.type_int[:]))
            for t in range(TYPES - 1, -1, -1):
                link(v.tensor_scalar(k.type_mask[:, :, t], k.type_mask[:, :, 0], float(t), None, ALU.is_equal))
            dve.wait_ge(s_w, 16 * (6 + 2 * HEADS + 1))
            for half in range(2):
              for r in range(RELS):
                a = rel_w[:, 0, half, r, :].rearrange("p (h e) -> p h e", e=DK)
                f = col(pri[:, r, 4 * half:4 * half + 4], DK)
                link(v.scalar_tensor_tensor(a, a, float(DK) ** -0.5, f, ALU.mult, ALU.mult))

            def mask(u, g, turn):
                if after(u, 2):
                    dve.wait_ge(s_turn, u - 1)
                dve.wait_ge(s_xt[g], turn * 16 + 16)
                v.tensor_copy(hot[:, g, :], k.type_mask[:, ds(u, 1), :].squeeze(1))
                for t in range(TYPES):
                    ins = v.tensor_scalar(xm[:, g, t, :], xt[:, g, :],
                                          k.type_mask[:, ds(u, 1), t:t + 1].squeeze(1), None, ALU.mult)
                ins.then_inc(s_xm, 1)

            mask(0, 0, 0)

            def tile(u, g, turn):
                if before(u, T - 1):
                    mask(u + 1, 1 - g, turn + g)
                if before(u, T):
                    dve.wait_ge(s_qkv, u + 1)
                    if after(u, 2):
                        dve.wait_ge(s_kvT, u - 1)
                    v.tensor_copy(kv[:, g, :], p_qkv[:, 0, :]).then_inc(s_kv, 1)
                if after(u, 1):
                    o = 1 - g
                    if after(u, 3):
                        dve.wait_ge(s_relout[o], (turn if g == 1 else turn - 1) * 32)
                    for m in range(0, 8, 2):
                        dve.wait_ge(s_rel, u * 8 + (m - 7))
                        v.tensor_copy(rel_piece(o, m), p_rel[:, m % 2, :].rearrange("p (r e) -> p r e", e=P)).then_inc(s_even, 1)

            grouped(dve, T + 1, tile, last=2)

        @block.scalar
        def _(act):
            def copy(o, i):
                return nc.scalar.activation(o, i, ACT.Copy)

            def turned(u, g):
                act.wait_ge(s_turn, u + 1)
                if after(u, 2):
                    act.wait_ge(s_qkv, u - 1)
                copy(maskT[:, g, :], p_hot[0:TYPES, 0:P])
                for h in range(2):
                    ins = copy(xT[:, g, 4 * h:4 * h + 4, :], p_turn[:, h, :].rearrange("p (c n) -> p c n", n=P))
                ins.then_inc(s_xT, 1)

            turned(0, 0)

            def tile(u, g, turn):
                if before(u, T):
                    act.wait_ge(s_qkv, u + 1)
                    if after(u, 2):
                        act.wait_ge(s_qout[g], turn * 16)
                    copy(q_out[:, g, :], p_qkv[:, 1, 0:D]).then_inc(s_q, 1)
                if after(u, 1):
                    o = 1 - g
                    if after(u, 3):
                        act.wait_ge(s_relout[o], (turn if g == 1 else turn - 1) * 32)
                    for m in range(1, 8, 2):
                        act.wait_ge(s_rel, u * 8 + (m - 7))
                        copy(rel_piece(o, m), p_rel[:, m % 2, :].rearrange("p (r e) -> p r e", e=P)).then_inc(s_odd, 1)
                if before(u, T - 1):
                    turned(u + 1, 1 - g)
                if before(u, T):
                    act.wait_ge(s_kvT, u + 1)
                    if after(u, 2):
                        act.wait_ge(s_rel, u * 8 - 8)
                    copy(kvT[:, g, :, :], p_kvT[:].rearrange("p (c n) -> p c n", n=P)).then_inc(s_kvTs, 1)

            grouped(act, T + 1, tile, last=2)

        @block.tensor
        def _(pe):
            mm, tr = nc.tensor.matmul, nc.tensor.transpose

            def turn_x(u, g):
                pe.wait_ge(s_xm, u + 1)
                if after(u, 1):
                    pe.wait_ge(s_xT, u)
                tr(p_hot[0:TYPES, 0:P], hot[:, g, :], k.ident[:])
                for c in range(2 * TYPES):
                    ins = tr(p_turn[:, c // 4, (c % 4) * P:(c % 4 + 1) * P],
                             xm[:, g, c // 2, (c % 2) * P:(c % 2 + 1) * P], k.ident[:])
                ins.then_inc(s_turn, 1)

            pe.wait_ge(s_w, 16 * (6 + 2 * HEADS + 1))
            turn_x(0, 0)

            def tile(u, g, turn):
                if before(u, T):
                    pe.wait_ge(s_xT, u + 1)
                    if after(u, 1):
                        pe.wait_ge(s_q, u)
                        pe.wait_ge(s_kv, u)
                    for lo, hi in ((0, 512), (512, FQ)):
                        o = p_qkv[:, lo // 512, 0:hi - lo]
                        for c in range(2 * TYPES):
                            mm(o, xT[:, g, c, :], w[:, c, lo:hi], start=(c == 0), stop=False)
                        ins = mm(o, maskT[:, g, :], bias[:, lo:hi], start=False, stop=True)
                    ins.then_inc(s_qkv, 1)
                if after(u, 1):
                    o = 1 - g
                    pe.wait_ge(s_kvTs, u)
                    for m in range(8):
                        if after(u, 2) or m >= 2:
                            pe.wait_ge(s_odd if m % 2 else s_even, u * 4 + (m // 2 - 4))
                        kind, half, rh = m // 4, (m // 2) % 2, m % 2
                        mm(p_rel[:, m % 2, :], kvT[:, o, 2 * kind + half, :],
                           rel_w[:, kind, half, 4 * rh:4 * rh + 4, :].rearrange("p r e -> p (r e)"),
                           start=True, stop=True).then_inc(s_rel, 1)
                if before(u, T - 1):
                    turn_x(u + 1, 1 - g)
                if before(u, T):
                    pe.wait_ge(s_kv, u + 1)
                    if after(u, 1):
                        pe.wait_ge(s_kvTs, u)
                    for c in range(4):
                        ins = tr(p_kvT[:, c * P:(c + 1) * P], kv[:, g, c * P:(c + 1) * P], k.ident[:])
                    ins.then_inc(s_kvT, 1)

            grouped(pe, T + 1, tile, last=2)





def hgt_scores(nc, k, score):
    with ExitStack() as ctx:
        sb = lambda n, s, d=fp32: ctx.enter_context(nc.sbuf_tensor("hs_" + n, s, d))
        sem = lambda n: (k.semaphore("hs_" + n))
        rows = sb("rows", [P, J, 4])
        at = sb("at", [P, 2, GW, 2], i32)
        key = sb("key", [P, 2, GW, D])
        query = sb("query", [P, 2, GW, D])
        product = sb("product", [P, GW, D])
        s_rows, s_staged, s_go, s_product, s_score = (sem(n) for n in ("rows", "staged", "go", "product", "score"))
        s_got = [sem(f"got{g}") for g in range(2)]
        block = ctx.enter_context(nc.Block())
        groups, rest = J // GW, J % GW

        @block.sync
        def _(sp):
            sp.dma_start(rows[:], k.sorted_rows[1:1 + EP, :].rearrange("(p j) w -> p j w", j=J)).then_inc(s_rows, 16)

        @block.gpsimd
        def _(pool):
            def gather(kk, g, turn, n=GW):
                pool.wait_ge(s_staged, kk + 1)
                pool.sem_inc(s_go, 1)
                for q in range(n):
                    pool.indirect_dma_start(key[:, g, q, :], None, k.kr_table,
                                            bass.IndirectOffsetOnAxis(ap=at[:, g, q, 0:1], axis=0)).then_inc(s_got[g], 16)
                    pool.indirect_dma_start(query[:, g, q, :], None, k.q_table,
                                            bass.IndirectOffsetOnAxis(ap=at[:, g, q, 1:2], axis=0)).then_inc(s_got[g], 16)

            grouped(pool, groups, gather)
            gather(groups, groups % 2, groups // 2, rest)

        @block.vector
        def _(dve):
            v = nc.vector
            dve.wait_ge(s_rows, 16)

            def stage(kk, g, n=GW):
                v.tensor_copy(at[:, g, 0:n, :], rows[:, ds(kk * GW, n), 0:4:3]).then_inc(s_staged, 1)

            stage(0, 0)
            stage(1, 1)

            def dot(kk, g, turn, n=GW):
                dve.wait_ge(s_got[g], turn * (32 * GW) + 32 * n)
                if after(kk, 1):
                    dve.wait_ge(s_score, kk)
                v.tensor_tensor(product[:, 0:n, :], key[:, g, 0:n, :], query[:, g, 0:n, :], ALU.mult).then_inc(s_product, 1)
                dve.wait_ge(s_product, kk + 1)
                v.tensor_reduce(score[:, ds(kk * GW, n), :],
                                product[:, 0:n, :].rearrange("p n (h d) -> p n h d", d=DK), AX.X, ALU.add).then_inc(s_score, 1)
                if before(kk, groups - 2):
                    stage(kk + 2, g)
                elif kk == groups - 2:
                    stage(kk + 2, g, rest)

            grouped(dve, groups, dot, last=3)
            dot(groups, groups % 2, groups // 2, rest)


def hgt_softmax(nc, k, score):
    with ExitStack() as ctx:
        sb = lambda n, s, d=fp32: ctx.enter_context(nc.sbuf_tensor("sm_" + n, s, d))
        sem = lambda n: (k.semaphore("sm_" + n))
        rows = sb("rows", [P, 3, J, 4])
        fwd = sb("fwd", [P, J, HEADS])
        bwd = rows[:].rearrange("p a j w -> p (a j w)")[:, 0:J * HEADS].rearrange("p (j h) -> p j h", h=HEADS)
        present = sb("present", [P, J])
        same = sb("same", [P, 2, J])
        gate = sb("gate", [P, 2, J])
        s_in, s_ch, s_shift, s_exp, s_w, s_out = (sem(n) for n in ("in", "ch", "shift", "exp", "w", "out"))
        heads = range(HEADS)
        scans = []
        for name, g, ops, init in (("m", gate, (ALU.add, ALU.max), -BIG), ("s", same, (ALU.mult, ALU.add), 0.0)):
            for way, out, back in ((0, fwd, False), (1, bwd, True)):
                scans.append(segmented_scan(nc, k, ctx, f"sm_{name}{way}",
                             [(out[:, :, h], score[:, :, h], g[:, way, :], back) for h in heads], *ops, init))
        block = ctx.enter_context(nc.Block())

        @block.sync
        def _(sp):
            for q, first in enumerate((1, 0, 2)):
                sp.dma_start(rows[:, q, :, :], k.sorted_rows[first:first + EP, :].rearrange("(p j) w -> p j w", j=J)).then_inc(s_in, 16)
            sp.wait_ge(s_w, 1)
            sp.dma_start(k.weight_dram.rearrange("(p j) h -> p j h", j=J), score).then_inc(s_out, 16)
            sp.wait_ge(s_out, 16)

        @block.tensor
        def _(pe):
            for s in scans:
                s[1](k.ident[:])

        @block.scalar
        def _(act):
            act.wait_ge(s_shift, 1)
            nc.scalar.activation(score, score, ACT.Exp).then_inc(s_exp, 1)

        @block.vector
        def _(dve):
            v = nc.vector
            link = chained(dve, s_ch)
            dve.wait_ge(s_in, 48)
            for way in range(2):
                link(v.tensor_tensor(same[:, way, :], rows[:, 0, :, 1], rows[:, 1 + way, :, 1], ALU.is_equal))
            link(v.tensor_scalar(gate[:], same[:], -1.0, BIG, ALU.add, ALU.mult))
            link(v.tensor_scalar(present[:], rows[:, 0, :, 2], 1.0, None, ALU.max))
            scans[0][0](link)
            scans[1][0](link)
            link(v.tensor_tensor(fwd[:], fwd[:], bwd, ALU.max))
            v.tensor_tensor(score, score, fwd[:], ALU.subtract).then_inc(s_shift, 1)
            dve.wait_ge(s_exp, 1)
            scans[2][0](link)
            scans[3][0](link)
            link(v.tensor_tensor(fwd[:], fwd[:], bwd, ALU.add))
            link(v.tensor_tensor(fwd[:], fwd[:], score, ALU.subtract))
            link(v.tensor_tensor(fwd[:], fwd[:], col(present[:], HEADS), ALU.mult))
            link(v.reciprocal(fwd[:], fwd[:]))
            v.tensor_tensor(score, score, fwd[:], ALU.mult).then_inc(s_w, 1)



def aggregate(nc, k, name, table, table_row, numbers, width, weights=None, heads=0, extra=0, count=False):
    row = D + extra + count
    with ExitStack() as ctx:
        sb = lambda n, s, d=fp32: ctx.enter_context(nc.sbuf_tensor(f"{name}_{n}", s, d))
        sem = lambda n: (k.semaphore(f"{name}_{n}"))
        at = sb("at", [P, 2, GW], i32)
        got = sb("got", [P, 2, GW, table_row])
        message = sb("message", [P, 2, GW, row]) if weights is not None else got
        hot = sb("hot", [P, 2, GW, P])
        p_sum = ctx.enter_context(nc.psum_tensor(f"{name}_sum", [P, 2, GW, 512], fp32))
        s_staged, s_go, s_ready, s_summed, s_added = (sem(n) for n in ("staged", "go", "ready", "summed", "added"))
        s_zero = sem("zero")
        s_got = [sem(f"got{g}") for g in range(2)]
        block = ctx.enter_context(nc.Block())
        groups = S // GW

        @block.gpsimd
        def _(pool):
            def gather(kk, g, turn):
                pool.wait_ge(s_staged, kk + 1)
                pool.sem_inc(s_go, 1)
                for q in range(GW):
                    pool.indirect_dma_start(got[:, g, q, :], None, table,
                                            bass.IndirectOffsetOnAxis(ap=at[:, g, q:q + 1], axis=0)).then_inc(s_got[g], 16)

            grouped(pool, groups, gather)

        @block.scalar
        def _(act):
            def stage(kk, g, turn):
                if after(kk, 2):
                    if weights is not None:
                        act.wait_ge(s_ready, kk - 1)
                    else:
                        act.wait_ge(s_summed, kk * GW - GW)
                nc.scalar.activation(at[:, g, :], numbers[:, ds(kk * GW, GW)], ACT.Copy).then_inc(s_staged, 1)

            grouped(act, groups, stage)

        @block.tensor
        def _(pe):
            def sums(kk, g, turn):
                pe.wait_ge(s_ready, kk + 1)
                if weights is None:
                    pe.wait_ge(s_got[g], turn * (16 * GW) + 16 * GW)
                if after(kk, 2):
                    pe.wait_ge(s_added, kk * GW - GW)
                for q in range(GW):
                    nc.tensor.matmul(p_sum[:, g, q, 0:row], hot[:, g, q, :], message[:, g, q, 0:row],
                                     start=True, stop=True).then_inc(s_summed, 1)

            grouped(pe, groups, sums)

        @block.vector
        def _(dve):
            v = nc.vector
            if count:
                v.memset(message[:, :, :, D:D + 1], 1.0)
            v.memset(k.acc[:], 0.0).then_inc(s_zero, 1)
            dve.wait_ge(s_zero, 1)

            def ready(kk, g, turn):
                if after(kk, 2):
                    dve.wait_ge(s_summed, kk * GW - GW)
                ins = v.tensor_tensor(hot[:, g, :, :], k.window_iota[:],
                                      col(k.place[:, ds(kk * GW, GW)], P), ALU.is_equal)
                if weights is not None:
                    if extra:
                        v.tensor_copy(message[:, g, :, D:row], weights[:, ds(kk * GW, GW), 0:extra])
                    dve.wait_ge(s_got[g], turn * (16 * GW) + 16 * GW)
                    hd = D // heads
                    for q in range(0, GW):
                        ins = v.tensor_tensor(message[:, g, q, 0:D].rearrange("p (h d) -> p h d", d=hd),
                                              got[:, g, q, 0:D].rearrange("p (h d) -> p h d", d=hd),
                                              weights[:, ds(kk * GW + q, 1), 0:heads].squeeze(1).unsqueeze(2).to_broadcast([P, heads, hd]),
                                              ALU.mult)
                ins.then_inc(s_ready, 1)

            def add(kk, g):
                for q in range(GW):
                    w = v.value_load(k.step_window[0:1, ds(kk * GW + q, 1)], min_val=0, max_val=T - 1)
                    dve.wait_ge(s_summed, kk * GW + (q + 1))
                    if after(kk, 1) or q:
                        dve.wait_ge(s_added, kk * GW + q)
                    o = k.acc[:, ds(w, 1), 0:row].squeeze(1)
                    v.tensor_tensor(o, o, p_sum[:, g, q, 0:row], ALU.add).then_inc(s_added, 1)

            def body(kk, g, turn):
                ready(kk, g, turn)
                if after(kk, 1):
                    add(kk - 1, 1 - g)

            grouped(dve, groups, body)
            add(groups - 1, (groups - 1) % 2)



def hgt_update(nc, k):
    with ExitStack() as ctx:
        sb = lambda n, s, d=fp32: ctx.enter_context(nc.sbuf_tensor("hu_" + n, s, d))
        ps = lambda n, s: ctx.enter_context(nc.psum_tensor("hu_ps_" + n, s, fp32))
        sem = lambda n: (k.semaphore("hu_" + n))
        w = sb("w", [P, 2 * TYPES, D])
        bias = sb("bias", [TYPES, D])
        skip = sb("skip", [P, TYPES])
        share = sb("share", [P, T])
        rest = sb("rest", [P, T])
        xm = sb("xm", [P, 2, TYPES, D])
        hot = sb("hot", [P, 2, TYPES])
        xT = sb("xT", [P, 2, 2 * TYPES, P])
        maskT = sb("maskT", [TYPES, 2, P])
        p_turn, p_hot, p_out = ps("turn", [P, 2, 512]), ps("hot", [P, 512]), ps("out", [P, 2, 512])
        s_x, s_w, s_ch, s_skip, s_sig = (sem(n) for n in ("x", "w", "ch", "skip", "sig"))
        s_xm, s_turn, s_xT, s_out, s_added = (sem(n) for n in ("xm", "turn", "xT", "out", "added"))
        block = ctx.enter_context(nc.Block())

        @block.sync
        def _(sp):
            sp.dma_start(skip[:], k.L0_skip.partition_broadcast(P)).then_inc(s_skip, 16)
            sp.dma_start(w[:], k.L0_Wa.rearrange("t (h i) o -> i (t h) o", i=P)).then_inc(s_w, 16)
            sp.dma_start(bias[:], k.L0_ba).then_inc(s_w, 16)
            sp.dma_start(k.x_now[:], k.x.rearrange("(t p) d -> p t d", p=P)).then_inc(s_x, 16)

        @block.vector
        def _(dve):
            v = nc.vector
            link = chained(dve, s_ch)
            dve.wait_ge(s_sig, 1)
            link(v.tensor_scalar(share[:], k.type_mask[:, :, 0], skip[:, 0:1], None, ALU.mult))
            for t in range(1, TYPES):
                link(v.scalar_tensor_tensor(share[:], k.type_mask[:, :, t], skip[:, t:t + 1], share[:], ALU.mult, ALU.add))
            link(v.tensor_scalar(rest[:], share[:], -1.0, 2.0, ALU.mult, ALU.add))
            dve.wait_ge(s_x, 16)
            link(v.tensor_tensor(k.x_now[:], k.x_now[:], col(rest[:], D), ALU.mult))

            def mask(u, g):
                if after(u, 2):
                    dve.wait_ge(s_turn, u - 1)
                v.tensor_copy(hot[:, g, :], k.type_mask[:, ds(u, 1), :].squeeze(1))
                for t in range(TYPES):
                    ins = v.tensor_scalar(xm[:, g, t, :], k.acc[:, ds(u, 1), 0:D].squeeze(1),
                                          k.type_mask[:, ds(u, 1), t:t + 1].squeeze(1), None, ALU.mult)
                ins.then_inc(s_xm, 1)

            mask(0, 0)

            def tile(u, g, turn):
                if before(u, T - 1):
                    mask(u + 1, 1 - g)
                dve.wait_ge(s_out, u + 1)
                o = k.x_now[:, ds(u, 1), :].squeeze(1)
                v.scalar_tensor_tensor(o, p_out[:, g, 0:D], share[:, ds(u, 1)], o, ALU.mult, ALU.add).then_inc(s_added, 1)

            grouped(dve, T, tile, last=1)

        @block.scalar
        def _(act):
            act.wait_ge(s_skip, 16)
            nc.scalar.activation(skip[:], skip[:], ACT.Sigmoid).then_inc(s_sig, 1)

            def turned(u, g, turn):
                act.wait_ge(s_turn, u + 1)
                if after(u, 2):
                    act.wait_ge(s_out, u - 1)
                nc.scalar.activation(maskT[:, g, :], p_hot[0:TYPES, 0:P], ACT.Copy)
                for h in range(2):
                    ins = nc.scalar.activation(xT[:, g, 4 * h:4 * h + 4, :],
                                               p_turn[:, h, :].rearrange("p (c n) -> p c n", n=P), ACT.Copy)
                ins.then_inc(s_xT, 1)

            grouped(act, T, turned)

        @block.tensor
        def _(pe):
            mm, tr = nc.tensor.matmul, nc.tensor.transpose

            def turn_x(u, g):
                pe.wait_ge(s_xm, u + 1)
                if after(u, 1):
                    pe.wait_ge(s_xT, u)
                tr(p_hot[0:TYPES, 0:P], hot[:, g, :], k.ident[:])
                for c in range(2 * TYPES):
                    ins = tr(p_turn[:, c // 4, (c % 4) * P:(c % 4 + 1) * P],
                             xm[:, g, c // 2, (c % 2) * P:(c % 2 + 1) * P], k.ident[:])
                ins.then_inc(s_turn, 1)

            pe.wait_ge(s_w, 32)
            turn_x(0, 0)

            def tile(u, g, turn):
                if before(u, T - 1):
                    turn_x(u + 1, 1 - g)
                pe.wait_ge(s_xT, u + 1)
                if after(u, 2):
                    pe.wait_ge(s_added, u - 1)
                for c in range(2 * TYPES):
                    mm(p_out[:, g, 0:D], xT[:, g, c, :], w[:, c, :], start=(c == 0), stop=False)
                mm(p_out[:, g, 0:D], maskT[:, g, :], bias[:], start=False, stop=True).then_inc(s_out, 1)

            grouped(pe, T, tile, last=1)


def node_products(nc, k, name, x, weight, cols, table, bias=None, attention=None):
    W = 512
    pieces = -(-cols // W)
    width = min(W, cols)
    extra = 2 * GHEADS if attention else 0
    with ExitStack() as ctx:
        sb = lambda n, s, d=fp32: ctx.enter_context(nc.sbuf_tensor(f"{name}_{n}", s, d))
        ps = lambda n, s: ctx.enter_context(nc.psum_tensor(f"{name}_ps_{n}", s, fp32))
        sem = lambda n: (k.semaphore(f"{name}_{n}"))
        w = sb("w", [P, 2, cols])
        xs = sb("xs", [P, 2, D])
        xT = sb("xT", [P, 2, 2, P])
        out = sb("out", [P, 2, cols + extra])
        b = sb("b", [1, cols]) if bias is not None else None
        if attention:
            vecs = sb("vecs", [P, 2, D])
            product = sb("product", [P, 2, D])
        p_turn, p_out = ps("turn", [P, 512]), ps("out_ps", [P, 2, 512])
        s_w, s_xs, s_turn, s_xT, s_out, s_kept, s_prod, s_row = (
            sem(n) for n in ("s_w", "s_xs", "s_turn", "s_xT", "s_out", "s_kept", "s_prod", "s_row"))
        s_stored = [sem(f"s_stored{g}") for g in range(2)]
        loads = len(weight) * 2 + (bias is not None) + (2 if attention else 0)
        block = ctx.enter_context(nc.Block())

        @block.sync
        def _(sp):
            for view, first in weight:
                for h in range(2):
                    sp.dma_start(w[:, h, first:first + view.shape[1]], view[h * P:(h + 1) * P, :]).then_inc(s_w, 16)
            if bias is not None:
                sp.dma_start(b[:], bias.unsqueeze(0)).then_inc(s_w, 16)
            if attention:
                for m, a in enumerate(attention):
                    sp.dma_start(vecs[:, m, :], a.rearrange("h d -> (h d)").partition_broadcast(P)).then_inc(s_w, 16)

            def store(u, g, turn):
                if attention:
                    sp.wait_ge(s_row, u + 1)
                else:
                    sp.wait_ge(s_kept, u * pieces + pieces)
                sp.dma_start(table[ds(u * P, P), :], out[:, g, :]).then_inc(s_stored[g], 16)

            grouped(sp, T, store)
            for g in range(2):
                sp.wait_ge(s_stored[g], 16 * ((T + 1 - g) // 2))

        @block.scalar
        def _(act):
            copy = lambda o, i: nc.scalar.activation(o, i, ACT.Copy)

            def take(u, g):
                if after(u, 2):
                    act.wait_ge(s_turn, u - 1)
                copy(xs[:, g, :], x[:, ds(u, 1), :].squeeze(1)).then_inc(s_xs, 1)

            take(0, 0)

            def tile(u, g, turn):
                if before(u, T - 1):
                    take(u + 1, 1 - g)
                act.wait_ge(s_turn, u + 1)
                if after(u, 2):
                    act.wait_ge(s_out, u * pieces - pieces)
                copy(xT[:, g, :, :], p_turn[:, 0:2 * P].rearrange("p (c n) -> p c n", n=P)).then_inc(s_xT, 1)
                if after(u, 2):
                    act.wait_ge(s_stored[g], turn * 16)
                for m in range(pieces):
                    bank = m % 2 if pieces > 1 else g
                    act.wait_ge(s_out, u * pieces + (m + 1))
                    copy(out[:, g, m * W:m * W + width], p_out[:, bank, 0:width]).then_inc(s_kept, 1)

            grouped(act, T, tile, last=1)

        @block.vector
        def _(dve):
            if not attention:
                return
            v = nc.vector
            dve.wait_ge(s_w, 16 * loads)

            def tile(u, g, turn):
                dve.wait_ge(s_kept, u + 1)
                if after(u, 1):
                    dve.wait_ge(s_row, u)
                v.tensor_tensor(product[:], out[:, g, 0:D].unsqueeze(1).to_broadcast([P, 2, D]), vecs[:], ALU.mult).then_inc(s_prod, 1)
                dve.wait_ge(s_prod, u + 1)
                heads = product[:].rearrange("p a (h d) -> p (a h) d", d=GHID)
                v.tensor_reduce(k.node8[:, ds(u, 1), :].squeeze(1), heads, AX.X, ALU.add)
                v.tensor_reduce(out[:, g, D:D + extra], heads, AX.X, ALU.add).then_inc(s_row, 1)

            grouped(dve, T, tile)

        @block.tensor
        def _(pe):
            def turn_x(u, g):
                pe.wait_ge(s_xs, u + 1)
                if after(u, 1):
                    pe.wait_ge(s_xT, u)
                for c in range(2):
                    ins = nc.tensor.transpose(p_turn[:, c * P:(c + 1) * P], xs[:, g, c * P:(c + 1) * P], k.ident[:])
                ins.then_inc(s_turn, 1)

            pe.wait_ge(s_w, 16 * loads)
            turn_x(0, 0)

            def tile(u, g, turn):
                if before(u, T - 1):
                    turn_x(u + 1, 1 - g)
                pe.wait_ge(s_xT, u + 1)
                for m in range(pieces):
                    bank = m % 2 if pieces > 1 else g
                    if after(u, 1) or m >= 2:
                        if pieces > 1 or after(u, 2):
                            pe.wait_ge(s_kept, u * pieces + (m - 1))
                    o = p_out[:, bank, 0:width]
                    for c in range(2):
                        ins = nc.tensor.matmul(o, xT[:, g, c, :], w[:, c, m * W:m * W + width],
                                               start=(c == 0), stop=(c == 1 and bias is None))
                    if bias is not None:
                        ins = nc.tensor.matmul(o, k.ones[0:1, :], b[:, m * W:m * W + width], start=False, stop=True)
                    ins.then_inc(s_out, 1)

            grouped(pe, T, tile, last=1)


def norm_rows(nc, k, name, x, eps, other=None, scale=None, store=None):
    CH = 7
    chunks = T // CH
    with ExitStack() as ctx:
        sb = lambda n, s, d=fp32: ctx.enter_context(nc.sbuf_tensor(f"{name}_{n}", s, d))
        sem = lambda n: (k.semaphore(f"{name}_{n}"))
        square = sb("square", [P, 2, CH, D])
        total = sb("total", [P, T])
        var = sb("var", [P, T])
        eps_col = sb("eps", [P, 1])
        s_ch, s_centred, s_square, s_var, s_root, s_scale, s_done, s_stored, s_eps = (
            sem(n) for n in ("ch", "centred", "squared", "vars", "root", "sc", "done", "stored", "epss"))
        if scale:
            both = sb("both", [P, 2, D])
        block = ctx.enter_context(nc.Block())

        @block.sync
        def _(sp):
            if scale:
                for m, a in enumerate(scale):
                    sp.dma_start(both[:, m, :], a.partition_broadcast(P)).then_inc(s_scale, 16)
            if store is not None:
                full = N // P
                for c in range(chunks):
                    sp.wait_ge(s_done, c + 1)
                    lo, hi = c * CH, min((c + 1) * CH, full)
                    sp.dma_start(store[lo * P:hi * P, :].rearrange("(t p) d -> p t d", p=P), x[:, lo:hi, :]).then_inc(s_stored, 16)
                sp.dma_start(store[full * P:N, :], x[0:N - full * P, full, :]).then_inc(s_stored, 16)
                sp.wait_ge(s_stored, 16 * (chunks + 1))

        @block.scalar
        def _(act):
            for c in range(chunks):
                act.wait_ge(s_centred, c + 1)
                if c >= 2:
                    act.wait_ge(s_var, c - 1)
                nc.scalar.activation(square[:, c % 2, :, :], x[:, c * CH:(c + 1) * CH, :], ACT.Square).then_inc(s_square, 1)
            act.wait_ge(s_var, chunks)
            act.wait_ge(s_eps, 1)
            nc.scalar.activation(var[:], var[:], ACT.Sqrt, bias=eps_col[:], scale=1.0 / D).then_inc(s_root, 1)

        @block.vector
        def _(dve):
            v = nc.vector
            link = chained(dve, s_ch)
            v.memset(eps_col[:], eps).then_inc(s_eps, 1)

            def variance(c):
                dve.wait_ge(s_square, c + 1)
                v.tensor_reduce(var[:, c * CH:(c + 1) * CH], square[:, c % 2, :, :], AX.X, ALU.add).then_inc(s_var, 1)

            for c in range(chunks):
                t = slice(c * CH, (c + 1) * CH)
                if other is not None:
                    link(v.tensor_tensor(x[:, t, :], x[:, t, :], other[:, t, :], ALU.add))
                link(v.tensor_reduce(total[:, t], x[:, t, :], AX.X, ALU.add))
                link(v.tensor_scalar(total[:, t], total[:, t], 1.0 / D, None, ALU.mult))
                v.tensor_tensor(x[:, t, :], x[:, t, :], col(total[:, t], D), ALU.subtract).then_inc(s_centred, 1)
                if c:
                    variance(c - 1)
            variance(chunks - 1)
            dve.wait_ge(s_root, 1)
            link(v.reciprocal(var[:], var[:]))
            if scale:
                dve.wait_ge(s_scale, 32)
            for c in range(chunks):
                t = slice(c * CH, (c + 1) * CH)
                ins = v.tensor_tensor(x[:, t, :], x[:, t, :], col(var[:, t], D), ALU.mult)
                if scale:
                    link(ins)
                    for m, op in ((0, ALU.mult), (1, ALU.add)):
                        ins = v.tensor_tensor(x[:, t, :], x[:, t, :], both[:, m, :].unsqueeze(1).to_broadcast([P, CH, D]), op)
                        if m == 0:
                            link(ins)
                ins.then_inc(s_done, 1)



def segment_starts(nc, k):
    with ExitStack() as ctx:
        sb = lambda n, s, d=fp32: ctx.enter_context(nc.sbuf_tensor("st_" + n, s, d))
        sem = lambda n: (k.semaphore("st_" + n))
        part = sb("part", [P, 1])
        node = sb("node", [P, T])
        lower = sb("lower", [P, P])
        degree = sb("degree", [P, T])
        whole = sb("whole", [P, T])
        upto = sb("upto", [P, T])
        tmp = sb("tmp", [P, T])
        zeros = sb("zeros", [P, J])
        ps = ctx.enter_context(nc.psum_tensor("st_ps", [P, 512], fp32))
        s_iota, s_in, s_ps, s_ch, s_zero, s_clear = (sem(n) for n in ("iota", "in", "ps", "ch", "zero", "clear"))
        block = ctx.enter_context(nc.Block())

        @block.gpsimd
        def _(pool):
            pool.iota(part[:], [[0, 1]], 0, 1, allow_small_or_imprecise_dtypes=True).then_inc(s_iota, 1)
            pool.iota(node[:], [[P, T]], EP, 1, allow_small_or_imprecise_dtypes=True).then_inc(s_iota, 1)

        @block.sync
        def _(sp):
            sp.wait_ge(s_zero, 1)
            to = k.edge_node[0:EP, :].rearrange("(p j) h -> p (j h)", j=J)
            for h in range(8):
                sp.dma_start(to[:, h * J:(h + 1) * J], zeros[:]).then_inc(s_clear, 16)
            sp.wait_ge(s_clear, 128)

        @block.tensor
        def _(pe):
            pe.wait_ge(s_in, 1)
            nc.tensor.matmul(ps[:, 0:T], lower[:], degree[:], start=True, stop=True)
            nc.tensor.matmul(ps[:, 64:64 + T], k.ones[:], degree[:], start=True, stop=True).then_inc(s_ps, 1)

        @block.vector
        def _(dve):
            v = nc.vector
            link = chained(dve, s_ch)
            v.memset(zeros[:], 0.0).then_inc(s_zero, 1)
            dve.wait_ge(s_iota, 2)
            link(v.tensor_scalar(lower[:], k.window_iota[:, 0, :], part[:, 0:1], None, ALU.is_gt))
            v.tensor_copy(degree[:], k.acc[:, :, D]).then_inc(s_in, 1)
            dve.wait_ge(s_ps, 1)
            link(v.tensor_copy(whole[:], ps[:, 64:64 + T]))
            link(v.tensor_tensor_scan(upto[:], k.ones[:, 0:T], whole[:], 0.0, ALU.mult, ALU.add))
            link(v.tensor_tensor(upto[:], upto[:], whole[:], ALU.subtract))
            link(v.tensor_tensor(upto[:], upto[:], ps[:, 0:T], ALU.add))
            link(v.tensor_scalar(k.alone[:], degree[:], 0.0, None, ALU.is_equal))
            link(v.tensor_tensor(tmp[:], node[:], upto[:], ALU.subtract))
            link(v.tensor_tensor(tmp[:], tmp[:], k.alone[:], ALU.mult))
            link(v.tensor_tensor(k.first_edge[:], upto[:], tmp[:], ALU.add))


def gat_gather(nc, k, name, es):
    with ExitStack() as ctx:
        sb = lambda n, s, d=fp32: ctx.enter_context(nc.sbuf_tensor(f"{name}_{n}", s, d))
        sem = lambda n: (k.semaphore(f"{name}_{n}"))
        src = sb("src", [P, J], i32)
        at = sb("at", [P, 2, GW], i32)
        got = sb("got", [P, 2, GW, 8])
        to = sb("to", [P, 2, 1], i32)
        node = sb("node", [P, 2, 8])
        s_src, s_staged, s_go, s_table, s_node = (sem(n) for n in ("s_src", "s_staged", "s_go", "s_table", "s_node"))
        s_got = [sem(f"s_got{g}") for g in range(2)]
        s_put = [sem(f"s_put{g}") for g in range(2)]
        block = ctx.enter_context(nc.Block())
        groups, rest = J // GW, J % GW

        @block.sync
        def _(sp):
            sp.dma_start(src[:], k.src.rearrange("(p j) -> p j", j=J)).then_inc(s_src, 16)
            sp.dma_start(k.att_table.rearrange("(t p) h -> p t h", p=P), k.node8[:]).then_inc(s_table, 16)

        @block.gpsimd
        def _(pool):
            def put(u, g, turn):
                if after(u, 2):
                    pool.wait_ge(s_put[g], turn * 16)
                pool.tensor_copy(to[:, g, :], k.first_edge[:, ds(u, 1)])
                pool.tensor_copy(node[:, g, :], k.node8[:, ds(u, 1), :].squeeze(1)).then_inc(s_node, 1)
                pool.wait_ge(s_node, u + 1)
                pool.sem_inc(s_go, 1)
                pool.indirect_dma_start(k.edge_node, bass.IndirectOffsetOnAxis(ap=to[:, g, 0:1], axis=0),
                                        node[:, g, :], None).then_inc(s_put[g], 16)

            grouped(pool, T, put)
            for g in range(2):
                pool.wait_ge(s_put[g], 16 * ((T + 1 - g) // 2))
            pool.wait_ge(s_table, 16)

            def gather(kk, g, turn, n=GW):
                pool.wait_ge(s_staged, kk + 1)
                pool.sem_inc(s_go, 1)
                for q in range(n):
                    pool.indirect_dma_start(got[:, g, q, :], None, k.att_table,
                                            bass.IndirectOffsetOnAxis(ap=at[:, g, q:q + 1], axis=0)).then_inc(s_got[g], 16)

            grouped(pool, groups, gather)
            gather(groups, groups % 2, groups // 2, rest)

        @block.vector
        def _(dve):
            v = nc.vector
            dve.wait_ge(s_src, 16)

            def stage(kk, g, n=GW):
                v.tensor_copy(at[:, g, 0:n], src[:, ds(kk * GW, n)]).then_inc(s_staged, 1)

            stage(0, 0)
            stage(1, 1)

            def keep(kk, g, turn, n=GW):
                dve.wait_ge(s_got[g], turn * (16 * GW) + 16 * n)
                v.tensor_copy(es[:, ds(kk * GW, n), :], got[:, g, 0:n, 0:GHEADS])
                if before(kk, groups - 2):
                    stage(kk + 2, g)
                elif kk == groups - 2:
                    stage(kk + 2, g, rest)

            grouped(dve, groups, keep, last=3)
            keep(groups, groups % 2, groups // 2, rest)


def gat_softmax(nc, k, name, es):
    H = GHEADS
    with ExitStack() as ctx:
        sb = lambda n, s, d=fp32: ctx.enter_context(nc.sbuf_tensor(f"{name}_{n}", s, d))
        sem = lambda n: (k.semaphore(f"{name}_{n}"))
        flat = k.acc[:].rearrange("p t w -> p (t w)")
        cut = lambda lo, w: flat[:, lo * J:(lo + w) * J].rearrange("p (j w) -> p j w", w=w)
        out, fwd, bwd = cut(0, 8), cut(8, H), cut(12, H)
        ints = k.step_w[:].rearrange("p s h -> p (s h)")[:, 0:3 * J].rearrange("p (q j) -> p q j", j=J).bitcast(i32)
        node = k.step_w[:].rearrange("p s h -> p (s h)")[:, 0:8 * J].rearrange("p (j w) -> p j w", w=8)
        tmp = sb("tmp", [P, J, H])
        same = sb("same", [P, 2, J])
        gate = tmp[:].rearrange("p j h -> p (j h)")[:, 0:2 * J].rearrange("p (w j) -> p w j", j=J)
        s_in, s_ch, s_shift, s_exp, s_w, s_out = (sem(n) for n in ("s_in", "s_ch", "s_shift", "s_exp", "s_w", "s_out"))
        spread = segmented_scan(nc, k, ctx, name + "_n", [(node[:, :, q], out[:, :, q], same[:, 0, :], False) for q in range(8)],
                                ALU.mult, ALU.add, 0.0)
        tops = [segmented_scan(nc, k, ctx, f"{name}_m{way}", [(o[:, :, h], es[:, :, h], gate[:, way, :], way == 1) for h in range(H)],
                               ALU.add, ALU.max, -BIG) for way, o in enumerate((fwd, bwd))]
        block = ctx.enter_context(nc.Block())

        @block.sync
        def _(sp):
            for q, first in enumerate((1, 0, 2)):
                sp.dma_start(ints[:, q, :], k.dst_ext[first:first + EP].rearrange("(p j) -> p j", j=J)).then_inc(s_in, 16)
            sp.dma_start(out, k.edge_node[0:EP, :].rearrange("(p j) h -> p j h", j=J)).then_inc(s_in, 16)
            sp.wait_ge(s_w, 1)
            sp.dma_start(k.weight_dram.rearrange("(p j) h -> p j h", j=J), out).then_inc(s_out, 16)
            sp.wait_ge(s_out, 16)

        @block.tensor
        def _(pe):
            spread[1](k.ident[:])
            for s in tops:
                s[1](k.ident[:])

        @block.scalar
        def _(act):
            act.wait_ge(s_shift, 1)
            nc.scalar.activation(out, out, ACT.Exp).then_inc(s_exp, 1)

        @block.vector
        def _(dve):
            v = nc.vector
            link = chained(dve, s_ch)
            dve.wait_ge(s_in, 64)
            for way in range(2):
                link(v.tensor_tensor(same[:, way, :], ints[:, 0, :], ints[:, 1 + way, :], ALU.is_equal))
            link(v.tensor_scalar(gate, same[:], -1.0, BIG, ALU.add, ALU.mult))
            spread[0](link)
            for s in tops:
                s[0](link)
            own, to = node[:, :, 0:H], node[:, :, H:2 * H]

            def leaky(o, a):
                link(v.tensor_tensor(tmp[:], a, to, ALU.add))
                link(v.scalar_tensor_tensor(o, tmp[:], 0.2, tmp[:], ALU.mult, ALU.max))

            link(v.tensor_tensor(fwd, fwd, bwd, ALU.max))
            link(v.tensor_tensor(fwd, fwd, own, ALU.max))
            leaky(bwd, fwd)
            leaky(fwd, es)
            link(v.tensor_tensor(out[:, :, 0:H], fwd, bwd, ALU.subtract))
            leaky(fwd, own)
            v.tensor_tensor(out[:, :, H:2 * H], fwd, bwd, ALU.subtract).then_inc(s_shift, 1)
            link(v.tensor_scalar(same[:, 1, :], same[:, 1, :], -1.0, 1.0, ALU.mult, ALU.add))
            dve.wait_ge(s_exp, 1)
            v.tensor_tensor(out[:, :, H:2 * H], out[:, :, H:2 * H], col(same[:, 1, :], H), ALU.mult).then_inc(s_w, 1)


def gat_update(nc, k, name, bias, residual):
    H = GHEADS
    with ExitStack() as ctx:
        sb = lambda n, s, d=fp32: ctx.enter_context(nc.sbuf_tensor(f"{name}_{n}", s, d))
        sem = lambda n: (k.semaphore(f"{name}_{n}"))
        own = sb("own", [P, T, H])
        inverse = sb("inverse", [P, T, H])
        b = sb("b", [P, D])
        row = sb("row", [P, 2, D])
        s_b, s_ch, s_done = sem("s_b"), sem("s_ch"), sem("s_done")
        s_row = [sem(f"s_row{g}") for g in range(2)]
        s_step = sem("s_step")
        block = ctx.enter_context(nc.Block())

        @block.sync
        def _(sp):
            sp.dma_start(b[:], bias.partition_broadcast(P)).then_inc(s_b, 16)

            def load(u, g, turn):
                if after(u, 2):
                    sp.wait_ge(s_done, u - 1)
                sp.dma_start(row[:, g, :], k.h_table[ds(u * P, P), 0:D]).then_inc(s_row[g], 16)

            grouped(sp, T, load)

        @block.vector
        def _(dve):
            v = nc.vector
            link = chained(dve, s_ch)
            link(v.tensor_tensor(own[:], k.acc[:, :, D + H:D + 2 * H], col(k.alone[:], H), ALU.add))
            link(v.tensor_tensor(inverse[:], own[:], k.acc[:, :, D:D + H], ALU.add))
            link(v.tensor_scalar(inverse[:], inverse[:], 1e-16, None, ALU.add))
            link(v.reciprocal(inverse[:], inverse[:]))
            dve.wait_ge(s_b, 16)

            def tile(u, g, turn):
                n = [0]

                def step(ins):
                    n[0] += 1
                    ins.then_inc(s_step, 1)
                    dve.wait_ge(s_step, u * 4 + n[0])

                heads = lambda a: a.rearrange("p (h d) -> p h d", d=GHID)
                per = lambda a: a[:, ds(u, 1), :].squeeze(1).unsqueeze(2).to_broadcast([P, H, GHID])
                dve.wait_ge(s_row[g], turn * 16 + 16)
                r = row[:, g, :]
                step(v.tensor_tensor(heads(r), heads(r), per(own[:]), ALU.mult))
                step(v.tensor_tensor(r, r, k.acc[:, ds(u, 1), 0:D].squeeze(1), ALU.add))
                step(v.tensor_tensor(heads(r), heads(r), per(inverse[:]), ALU.mult))
                step(v.tensor_tensor(r, r, b[:], ALU.add))
                if residual:
                    o = k.x_now[:, ds(u, 1), :].squeeze(1)
                    v.scalar_tensor_tensor(o, r, 0.0, o, ALU.max, ALU.add).then_inc(s_done, 1)
                else:
                    v.tensor_scalar(k.acc[:, ds(u, 1), 0:D].squeeze(1), r, 0.0, None, ALU.max).then_inc(s_done, 1)

            grouped(dve, T, tile)



def mlp_aggregate(nc, k):
    with ExitStack() as ctx:
        sb = lambda n, s, d=fp32: ctx.enter_context(nc.sbuf_tensor("ml_" + n, s, d))
        ps = lambda n, s: ctx.enter_context(nc.psum_tensor("ml_ps_" + n, s, fp32))
        sem = lambda n: (k.semaphore("ml_" + n))
        w = sb("w", [DE, D])
        s_go_sp, s_go_pe = sem("go_sp"), sem("go_pe")
        at = sb("at", [P, 2, GW], i32)
        got = sb("got", [P, 2, GW, D])
        attr = sb("attr", [P, 2, GW, DE])
        attrT = sb("attrT", [DE, 2, GW, P])
        message = sb("message", [P, 2, GW, D])
        hot = sb("hot", [P, 2, GW, P])
        p_turn = ps("turn", [P, 512])
        p_edge = ps("edge", [P, GW, D])
        p_sum = ps("sum", [P, 2, GW, D])
        s_w, s_staged, s_go, s_turn, s_turned, s_edge, s_pre, s_hot, s_message, s_summed, s_added, s_zero = (
            sem(n) for n in ("s_w", "staged", "go", "turn_s", "turned", "edge_s", "pre", "hot_s", "message_s", "summed", "added", "zero"))
        s_got = [sem(f"got{g}") for g in range(2)]
        s_attr = [sem(f"attr{g}") for g in range(2)]
        block = ctx.enter_context(nc.Block())
        groups = S // GW

        @block.sync
        def _(sp):
            sp.dma_start(w[:], k.L2_W[D:D + DE, :]).then_inc(s_w, 16)

            def load(kk, g, turn):
                if after(kk, 2):
                    sp.wait_ge(s_turn, kk - 1)
                    sp.sem_inc(s_go_sp, 1)
                for q in range(GW):
                    c = sp.value_load(k.step_tile[0:1, ds(kk * GW + q, 1)], min_val=0, max_val=C - 1)
                    sp.dma_start(attr[:, g, q, :], k.edge_attr[ds(c * P, P), :]).then_inc(s_attr[g], 16)

            grouped(sp, groups, load)

        @block.gpsimd
        def _(pool):
            def gather(kk, g, turn):
                pool.wait_ge(s_staged, kk + 1)
                pool.sem_inc(s_go, 1)
                for q in range(GW):
                    pool.indirect_dma_start(got[:, g, q, :], None, k.p_table,
                                            bass.IndirectOffsetOnAxis(ap=at[:, g, q:q + 1], axis=0)).then_inc(s_got[g], 16)

            grouped(pool, groups, gather)

        @block.scalar
        def _(act):
            def stage(kk, g):
                nc.scalar.activation(at[:, g, :], k.src_step[:, ds(kk * GW, GW)], ACT.Copy).then_inc(s_staged, 1)

            def turned(kk, g):
                act.wait_ge(s_turn, kk + 1)
                if after(kk, 2):
                    act.wait_ge(s_edge, kk - 1)
                nc.scalar.activation(attrT[:, g, :, :], p_turn[0:DE, :].rearrange("p (q n) -> p q n", n=P), ACT.Copy).then_inc(s_turned, 1)

            stage(0, 0)
            stage(1, 1)
            turned(0, 0)

            def silu(kk, g, turn):
                if before(kk, groups - 1):
                    turned(kk + 1, 1 - g)
                act.wait_ge(s_pre, kk + 1)
                if after(kk, 2):
                    act.wait_ge(s_summed, kk * GW - GW)
                nc.scalar.activation(message[:, g, :, :], got[:, g, :, :], ACT.Silu).then_inc(s_message, 1)
                if before(kk, groups - 2):
                    act.wait_ge(s_message, kk + 1)
                    stage(kk + 2, g)

            grouped(act, groups, silu, last=2)

        @block.tensor
        def _(pe):
            def turn_attr(kk, g, turn):
                pe.wait_ge(s_attr[g], turn * (16 * GW) + 16 * GW)
                if after(kk, 1):
                    pe.wait_ge(s_turned, kk)
                pe.sem_inc(s_go_pe, 1)
                for q in range(GW):
                    ins = nc.tensor.transpose(p_turn[0:DE, q * P:(q + 1) * P], attr[:, g, q, :], k.ident[:])
                ins.then_inc(s_turn, 1)

            def edge(kk, g):
                pe.wait_ge(s_turned, kk + 1)
                if after(kk, 1):
                    pe.wait_ge(s_pre, kk)
                for q in range(GW):
                    ins = nc.tensor.matmul(p_edge[:, q, :], attrT[:, g, q, :], w[:], start=True, stop=True)
                ins.then_inc(s_edge, 1)

            def sums(kk, g):
                pe.wait_ge(s_message, kk + 1)
                pe.wait_ge(s_hot, kk + 1)
                if after(kk, 2):
                    pe.wait_ge(s_added, kk * GW - GW)
                for q in range(GW):
                    nc.tensor.matmul(p_sum[:, g, q, :], hot[:, g, q, :], message[:, g, q, :],
                                     start=True, stop=True).then_inc(s_summed, 1)

            pe.wait_ge(s_w, 16)
            turn_attr(0, 0, 0)

            def body(kk, g, turn):
                edge(kk, g)
                if before(kk, groups - 1):
                    turn_attr(kk + 1, 1 - g, turn + g)
                if after(kk, 1):
                    sums(kk - 1, 1 - g)

            grouped(pe, groups, body, last=2)
            sums(groups - 1, (groups - 1) % 2)

        @block.vector
        def _(dve):
            v = nc.vector
            v.memset(k.acc[:], 0.0).then_inc(s_zero, 1)
            dve.wait_ge(s_zero, 1)

            def pre(kk, g, turn):
                if after(kk, 2):
                    dve.wait_ge(s_summed, kk * GW - GW)
                v.tensor_tensor(hot[:, g, :, :], k.window_iota[:],
                                col(k.place[:, ds(kk * GW, GW)], P), ALU.is_equal).then_inc(s_hot, 1)
                dve.wait_ge(s_edge, kk + 1)
                dve.wait_ge(s_got[g], turn * (16 * GW) + 16 * GW)
                v.tensor_tensor(got[:, g, :, :], got[:, g, :, :], p_edge[:], ALU.add).then_inc(s_pre, 1)

            def add(kk, g):
                for q in range(GW):
                    w_ = v.value_load(k.step_window[0:1, ds(kk * GW + q, 1)], min_val=0, max_val=T - 1)
                    dve.wait_ge(s_summed, kk * GW + (q // 2 * 2 + 2))
                    if after(kk, 1) or q:
                        dve.wait_ge(s_added, kk * GW + q)
                    o = k.acc[:, ds(w_, 1), 0:D].squeeze(1)
                    v.tensor_tensor(o, o, p_sum[:, g, q, :], ALU.add).then_inc(s_added, 1)

            def body(kk, g, turn):
                pre(kk, g, turn)
                if after(kk, 1):
                    add(kk - 1, 1 - g)

            grouped(dve, groups, body)
            add(groups - 1, (groups - 1) % 2)



def norm_columns(nc, k):
    CH = 7
    chunks = T // CH
    full = N // P
    with ExitStack() as ctx:
        sb = lambda n, s, d=fp32: ctx.enter_context(nc.sbuf_tensor("bn_" + n, s, d))
        sem = lambda n: (k.semaphore("bn_" + n))
        square = sb("square", [P, 2, CH, D])
        both = sb("both", [P, 2, D])
        mean = sb("mean", [P, D])
        factor = sb("factor", [P, D])
        eps_col = sb("eps", [P, 1])
        ps = ctx.enter_context(nc.psum_tensor("bn_ps", [P, 2, 512], fp32))
        s_scale, s_ch, s_sum, s_var, s_centred, s_square, s_squares, s_root, s_eps = (
            sem(n) for n in ("scale", "ch", "sum", "var", "centred", "squared", "squares", "root", "epss"))
        acc = k.acc[:, :, 0:D]
        block = ctx.enter_context(nc.Block())

        @block.sync
        def _(sp):
            sp.dma_start(both[:, 0, :], k.L3_gamma.partition_broadcast(P)).then_inc(s_scale, 16)
            sp.dma_start(both[:, 1, :], k.L3_beta.partition_broadcast(P)).then_inc(s_scale, 16)

        @block.tensor
        def _(pe):
            def add(o, view, t):
                rows = N - full * P if t == full else P
                return nc.tensor.matmul(o, k.ones[0:rows, :], view[0:rows, :], start=(t == 0), stop=(t == T - 1))

            for t in range(T):
                ins = add(ps[:, 0, 0:D], acc[:, t, :], t)
            ins.then_inc(s_sum, 1)
            for c in range(chunks):
                pe.wait_ge(s_square, c + 1)
                for t in range(CH):
                    ins = add(ps[:, 1, 0:D], square[:, c % 2, t, :], c * CH + t)
                ins.then_inc(s_squares, 1)

        @block.scalar
        def _(act):
            for c in range(chunks):
                act.wait_ge(s_centred, c + 1)
                if c >= 2:
                    act.wait_ge(s_squares, c - 1)
                nc.scalar.activation(square[:, c % 2, :, :], acc[:, c * CH:(c + 1) * CH, :], ACT.Square).then_inc(s_square, 1)
            act.wait_ge(s_squares, chunks)
            act.wait_ge(s_eps, 1)
            nc.scalar.activation(factor[:], ps[:, 1, 0:D], ACT.Sqrt, bias=eps_col[:], scale=1.0 / N).then_inc(s_root, 1)

        @block.vector
        def _(dve):
            v = nc.vector
            link = chained(dve, s_ch)
            v.memset(eps_col[:], 1e-5).then_inc(s_eps, 1)
            wide = lambda a: a.unsqueeze(1).to_broadcast([P, CH, D])
            dve.wait_ge(s_sum, 1)
            link(v.tensor_scalar(mean[:], ps[:, 0, 0:D], 1.0 / N, None, ALU.mult))
            for c in range(chunks):
                t = slice(c * CH, (c + 1) * CH)
                v.tensor_tensor(acc[:, t, :], acc[:, t, :], wide(mean[:]), ALU.subtract).then_inc(s_centred, 1)
            dve.wait_ge(s_root, 1)
            link(v.reciprocal(factor[:], factor[:]))
            dve.wait_ge(s_scale, 32)
            link(v.tensor_tensor(factor[:], factor[:], both[:, 0, :], ALU.mult))
            dve.wait_ge(s_squares, chunks)
            for c in range(chunks):
                t = slice(c * CH, (c + 1) * CH)
                link(v.tensor_tensor(acc[:, t, :], acc[:, t, :], wide(factor[:]), ALU.mult))
                link(v.tensor_tensor(acc[:, t, :], acc[:, t, :], wide(both[:, 1, :]), ALU.add))


def build(nc, a, out, upto=99):
    k = Shared(nc)
    with ExitStack() as ctx:
        sb = lambda n, s, d=fp32: ctx.enter_context(nc.sbuf_tensor(n, s, d))
        dram = lambda n, s, d=fp32: nc.dram_tensor(n, s, d, kind="Internal").ap()
        k.x = a["x"]
        k.dst_ext = a["dst_ext"]
        k.src = a["src"]
        k.rel = a["rel"]
        k.node_type = a["node_type"]
        k.edge_attr = a["edge_attr"]
        k.L0_Wk = a["L0_Wk"]
        k.L0_bk = a["L0_bk"]
        k.L0_Wq = a["L0_Wq"]
        k.L0_bq = a["L0_bq"]
        k.L0_Wv = a["L0_Wv"]
        k.L0_bv = a["L0_bv"]
        k.L0_Wa = a["L0_Wa"]
        k.L0_ba = a["L0_ba"]
        k.L0_rel_att = a["L0_rel_att"]
        k.L0_rel_msg = a["L0_rel_msg"]
        k.L0_rel_pri = a["L0_rel_pri"]
        k.L0_skip = a["L0_skip"]
        k.L1_W0 = a["L1_W0"]
        k.L1_a_src0 = a["L1_a_src0"]
        k.L1_a_dst0 = a["L1_a_dst0"]
        k.L1_b0 = a["L1_b0"]
        k.L1_W1 = a["L1_W1"]
        k.L1_a_src1 = a["L1_a_src1"]
        k.L1_a_dst1 = a["L1_a_dst1"]
        k.L1_b1 = a["L1_b1"]
        k.L2_W = a["L2_W"]
        k.L2_b = a["L2_b"]
        k.L2_gamma = a["L2_gamma"]
        k.L2_beta = a["L2_beta"]
        k.L3_weight = a["L3_weight"]
        k.L3_gamma = a["L3_gamma"]
        k.L3_beta = a["L3_beta"]
        k.out = out
        k.ident = sb("ident", [P, P])
        k.ones = sb("ones", [P, P])
        k.window_iota = sb("window_iota", [P, GW, P])
        k.pick = sb("pick", [P, CB, S])
        k.step_window = sb("step_window", [1, S], i32)
        k.src_step = sb("src_step", [P, S])
        k.pair_step = sb("pair_step", [P, S])
        k.place = sb("place", [P, S])
        k.type_int = sb("type_int", [P, T], i32)
        k.type_mask = sb("type_mask", [P, T, TYPES])
        k.step_w = sb("step_w", [P, S, HEADS])
        flat = k.step_w[:].rearrange("p s h -> p (s h)")
        k.rows = flat[:, 0:4 * J].rearrange("p (j w) -> p j w", w=4)
        k.position = flat[:, 4 * J:5 * J]
        k.sorted_rows = dram("sorted_rows", [EP + 2, 4])
        k.step_tile = dram("step_tile", [1, S], i32)
        k.q_table = dram("q_table", [NP, D])
        k.kr_table = dram("kr_table", [NP * RELS, D])
        k.vr_table = dram("vr_table", [NP * RELS, D])
        k.weight_dram = dram("weight_dram", [EP, HEADS])

        for stage in (constants, plan_steps, steps_of_graph, sort_positions, hgt_tables):
            stage(nc, k)
        if upto < 1: return
        with ExitStack() as scan:
            score = scan.enter_context(nc.sbuf_tensor("score", [P, J, HEADS], fp32))[:]
            hgt_scores(nc, k, score)
            hgt_softmax(nc, k, score)
        to_steps(nc, k, "ts_w", k.weight_dram.rearrange("(c p) h -> c (p h)", p=P), HEADS,
                 [(h, k.step_w[:, :, h], 0.0) for h in range(HEADS)], False)
        to_steps(nc, k, "ts_pair", k.sorted_rows[1:1 + EP, :].rearrange("(c p) w -> c (p w)", p=P), 4,
                 [(0, k.pair_step[:], 0.0)], False)
        if upto < 2: return
        k.acc = sb("acc", [P, T, HROW])
        aggregate(nc, k, "ag0", k.vr_table, D, k.pair_step[:], D, k.step_w[:], HEADS, count=True)
        if upto < 3: return
        k.x_now = sb("x_now", [P, T, D])
        k.node8 = sb("node8", [P, T, 8])
        k.first_edge = sb("first_edge", [P, T])
        k.alone = sb("alone", [P, T])
        k.h_table = dram("h_table", [NP, HROW])
        k.p_table = dram("p_table", [NP, D])
        k.att_table = dram("att_table", [NP, 8])
        k.edge_node = dram("edge_node", [EP + NP, 8])
        acc = k.acc[:, :, 0:D]
        k.recycle()
        hgt_update(nc, k)
        if upto < 3.5: return
        segment_starts(nc, k)
        norm_rows(nc, k, "n0", k.x_now[:], 1e-5)
        if upto < 4: return
        for n, (x, w, a_src, a_dst, bias) in enumerate(((k.x_now[:], k.L1_W0, k.L1_a_src0, k.L1_a_dst0, k.L1_b0),
                                                         (acc, k.L1_W1, k.L1_a_src1, k.L1_a_dst1, k.L1_b1))):
            node_products(nc, k, f"gp{n}", x, [(w, 0)], D, k.h_table, attention=(a_src, a_dst))
            with ExitStack() as scan:
                es = scan.enter_context(nc.sbuf_tensor(f"es{n}", [P, J, GHEADS], fp32))[:]
                gat_gather(nc, k, f"gg{n}", es)
                gat_softmax(nc, k, f"gs{n}", es)
            to_steps(nc, k, f"tw{n}", k.weight_dram.rearrange("(c p) h -> c (p h)", p=P), HEADS,
                     [(h, k.step_w[:, :, h], 0.0) for h in range(HEADS)], False)
            aggregate(nc, k, f"ag{n + 1}", k.h_table, HROW, k.src_step[:], D, k.step_w[:], GHEADS, extra=8)
            gat_update(nc, k, f"gu{n}", bias, n == 1)
            if upto < 5 + n: return
            k.recycle()
        norm_rows(nc, k, "n1", k.x_now[:], 1e-5)
        node_products(nc, k, "mp", k.x_now[:], [(k.L2_W[0:D, :], 0)], D, k.p_table, bias=k.L2_b)
        mlp_aggregate(nc, k)
        if upto < 7: return
        norm_rows(nc, k, "n2", acc, 1e-3, scale=(k.L2_gamma, k.L2_beta))
        norm_rows(nc, k, "n3", k.x_now[:], 1e-5, other=acc)
        if upto < 8: return
        node_products(nc, k, "rp", k.x_now[:], [(k.L3_weight[r], r * D) for r in range(RELS)], RELS * D,
                      k.kr_table.rearrange("(n r) d -> n (r d)", r=RELS))
        aggregate(nc, k, "ag3", k.kr_table, D, k.pair_step[:], D)
        norm_columns(nc, k)
        norm_rows(nc, k, "n4", k.x_now[:], 1e-5, other=acc, store=k.out)


def lay_out(inputs):
    import numpy as np
    a = {n: np.ascontiguousarray(np.asarray(v)) for n, v in inputs.items()}
    ints = lambda v: np.ascontiguousarray(v, dtype=np.int32) if v.dtype == np.int32 else v
    pad = lambda v, n, fill: np.concatenate([v, np.full((n - v.shape[0],) + v.shape[1:], fill, v.dtype)])
    one = lambda x: np.full((1,), x, a["dst"].dtype)
    out = {
        "x": pad(a["x"], NP, 0),
        "dst_ext": np.concatenate([one(-1), pad(a["dst"], EP, NP - 1), one(-2)]),
        "src": pad(a["src"], EP, 0),
        "rel": pad(a["edge_type_8"], EP, 0),
        "node_type": pad(a["node_type_4"], NP, 0),
        "edge_attr": pad(a["edge_attr_64"], EP, 0),
    }
    for n, v in a.items():
        if n.startswith("L"):
            out[n.replace("_gnn_", "_")] = v
    return out


def kernel(**inputs):
    import concourse.bacc as bacc
    from concourse.bass_utils import run_bass_kernel_spmd as run

    nc = bacc.Bacc("TRN2", target_bir_lowering=False, num_devices=1)
    arrays = {"in_" + n: v for n, v in lay_out(inputs).items()}
    aps = {n[3:]: nc.dram_tensor(n, v.shape, mybir.dt.from_np(v.dtype), kind="ExternalInput").ap()
           for n, v in arrays.items()}
    out = nc.dram_tensor("out_0", (N, D), fp32, kind="ExternalOutput").ap()
    build(nc, aps, out)
    r = run(nc, [arrays], core_ids=[0])
    return r.results[0]["out_0"]
```

```python
from contextlib import ExitStack

import concourse.bass as bass
from concourse import mybir

fp32 = mybir.dt.float32
i32 = mybir.dt.int32
bf16 = mybir.dt.bfloat16
ALU = mybir.AluOpType
ACT = mybir.ActivationFunctionType
AX = mybir.AxisListType

P = 128
N, E = 6250, 100000
D = 256
TYPES, RELS, HEADS = 4, 8, 8
DK = D // HEADS
GHEADS = 4
GHID = D // GHEADS
DE = 64
T = -(-N // P)
NP = T * P
C = -(-E // P)
EP = C * P
J = C
S = -(-(C + T) // 8) * 8
CB = -(-C // P)
SH = S // 2
GW = 4
WAYS = 4
HROW = D + 8
BIG = 1e30
ds = bass.ds


class Shared:

    def __init__(self, nc):
        self.nc = nc
        self.used = []

    def semaphore(self, name):
        self.used.append(self.nc.alloc_semaphore(name))
        return self.used[-1]

    def recycle(self):
        self.nc.clear_and_free_semaphores(self.used)
        self.used = []
        self.nc.all_engine_barrier()


def col(ap2, w):
    return ap2.unsqueeze(2).to_broadcast([ap2.shape[0], ap2.shape[1], w])


def grouped(eng, groups, body, last=0, ways=2):
    turns = max(1, (groups - last) // ways)
    for kk in range(min(ways, groups)):
        body(kk, kk, 0)
    if turns > 1:
        with eng.Fori(1, turns) as i:
            for g in range(ways):
                body(i * ways + g, g, i)
    for kk in range(ways * turns, groups):
        body(kk, kk % ways, kk // ways)


def after(k, count):
    return not isinstance(k, int) or k >= count


def before(k, end):
    return not isinstance(k, int) or k < end


def chained(eng, sem):
    count = [0]

    def link(ins):
        count[0] += 1
        ins.then_inc(sem, 1)
        eng.wait_ge(sem, count[0])
    link.count = count
    return link


def four(eng, registers, row, kk, top):
    eng.reg_load(registers, row[0:1, ds(kk * GW, GW)])
    return [eng.snap(r, min_val=0, max_val=top) for r in registers]



def segmented_scan(nc, k, ctx, name, items, step_op, join_op, init):
    Q = len(items)
    sb = lambda n, s: ctx.enter_context(nc.sbuf_tensor(f"{name}_{n}", s, fp32))
    last = sb("last", [P, 2, Q])
    lastT = sb("lastT", [Q, 2, P])
    carryT = sb("carryT", [Q, P + 1])
    carry = sb("carry", [P, Q])
    ps = ctx.enter_context(nc.psum_tensor(f"{name}_ps", [P, 512], fp32))
    s_last = (k.semaphore(f"{name}_s_last"))
    s_turned = (k.semaphore(f"{name}_s_turned"))
    s_carryT = (k.semaphore(f"{name}_s_carryT"))
    s_back = (k.semaphore(f"{name}_s_back"))
    assert len({b for *_, b in items}) == 1
    backward = items[0][3]

    def way(v):
        return v[:, ::-1] if backward else v

    def dve_part(link):
        for q, (out, x, gate, _) in enumerate(items):
            link(nc.vector.tensor_tensor_scan(way(out), way(gate), way(x), init, step_op, join_op))
            end = out[:, 0:1] if backward else out[:, J - 1:J]
            link(nc.vector.tensor_copy(last[:, 0, q:q + 1], end))
            link(nc.vector.tensor_reduce(last[:, 1, q:q + 1], gate, AX.X, ALU.min))
        link(nc.vector.tensor_copy(last[:, 0, 0:1], last[:, 0, 0:1]))
        nc.vector.tensor_copy(last[:, 1, 0:1], last[:, 1, 0:1]).then_inc(s_last, 1)
        nc.vector.wait_ge(s_turned, 1)
        link(nc.vector.tensor_copy(lastT[:], ps[0:Q, 0:2 * P].rearrange("q (a p) -> q a p", a=2)))
        if backward:
            link(nc.vector.memset(carryT[:, P:P + 1], init))
            link(nc.vector.tensor_tensor_scan(carryT[:, 0:P][:, ::-1], lastT[:, 1, :][:, ::-1],
                                              lastT[:, 0, :][:, ::-1], init, step_op, join_op))
        else:
            link(nc.vector.memset(carryT[:, 0:1], init))
            link(nc.vector.tensor_tensor_scan(carryT[:, 1:P + 1], lastT[:, 1, :], lastT[:, 0, :],
                                              init, step_op, join_op))
        nc.vector.tensor_copy(lastT[:, 0, :], carryT[:, 1:P + 1] if backward else carryT[:, 0:P])\
            .then_inc(s_carryT, 1)
        nc.vector.wait_ge(s_back, 1)
        link(nc.vector.tensor_copy(carry[:], ps[:, 256:256 + Q]))
        for q, (out, x, gate, _) in enumerate(items):
            link(nc.vector.tensor_tensor_scan(way(out), way(gate), way(x), carry[:, q:q + 1],
                                              step_op, join_op))

    def pe_part(ident):
        nc.tensor.wait_ge(s_last, 1)
        nc.tensor.transpose(ps[0:Q, 0:P], last[:, 0, :], ident)
        nc.tensor.transpose(ps[0:Q, P:2 * P], last[:, 1, :], ident).then_inc(s_turned, 1)
        nc.tensor.wait_ge(s_carryT, 1)
        nc.tensor.transpose(ps[:, 256:256 + Q], lastT[:, 0, :], ident[0:Q, 0:Q]).then_inc(s_back, 1)

    return dve_part, pe_part



def constants(nc, k):
    with ExitStack() as ctx:
        sem = lambda n: (k.semaphore(n))
        s_zero, s_ident = sem("c_zero"), sem("c_ident")
        block = ctx.enter_context(nc.Block())

        @block.gpsimd
        def _(pool):
            pool.memset(k.ident[:], 0.0).then_inc(s_zero, 1)
            pool.iota(k.window_iota[:], [[0, GW], [1, P]], 0, 0, allow_small_or_imprecise_dtypes=True)
            pool.iota(k.part[:], [[0, 1]], 0, 1, allow_small_or_imprecise_dtypes=True)
            pool.wait_ge(s_zero, 1)
            pool.affine_select(out=k.ident[:], in_=k.ident[:], compare_op=ALU.not_equal, fill=1.0,
                               base=0, pattern=[[-1, P]], channel_multiplier=1).then_inc(s_ident, 1)

        @block.vector
        def _(dve):
            nc.vector.memset(k.ones[:], 1.0)



def plan_steps(nc, k):
    with ExitStack() as ctx:
        sb = lambda n, s, d=fp32: ctx.enter_context(nc.sbuf_tensor(n, s, d))
        sem = lambda n: (k.semaphore(n))
        last_dst = sb("p_last", [P, CB], i32)
        last_win = sb("p_lastwin", [P, CB], i32)
        key = sb("p_key", [P, CB])
        tile_id = sb("p_tile", [P, CB])
        step_iota = sb("p_step", [P, S])
        before = sb("p_before", [P, CB, S])
        tile_of = sb("p_tileof", [P, S])
        window_of = sb("p_windowof", [P, S])
        tile_int = sb("p_tileint", [1, S], i32)
        s_tile, s_stored = sem("p_tile_ready"), sem("p_stored")
        ps = ctx.enter_context(nc.psum_tensor("p_ps", [P, 2, 512], fp32))
        s_in, s_iota, s_ch, s_before, s_sum, s_z = (sem("p_" + n) for n in
                                                    ("in", "iota", "ch", "before", "sum", "z"))
        block = ctx.enter_context(nc.Block())

        @block.gpsimd
        def _(pool):
            pool.iota(step_iota[:], [[1, S]], 0, 0, allow_small_or_imprecise_dtypes=True).then_inc(s_iota, 1)
            pool.iota(tile_id[:], [[P, CB]], 0, 1, allow_small_or_imprecise_dtypes=True).then_inc(s_iota, 1)

        @block.sync
        def _(sp):
            sp.wait_ge(s_z, 1)
            full = C // P
            every = k.dst_ext[1:1 + EP].rearrange("(c p) -> c p", p=P)[:, P - 1:P]
            with nc.allow_non_contiguous_dma(reason="one element of every tile"):
                for b in range(full):
                    sp.dma_start(last_dst[:, b:b + 1], every[b * P:(b + 1) * P, :]).then_inc(s_in, 16)
                sp.dma_start(last_dst[0:C - full * P, full:full + 1],
                             every[full * P:C, :]).then_inc(s_in, 16)
            sp.wait_ge(s_tile, 1)
            sp.dma_start(k.step_tile, tile_int[:]).then_inc(s_stored, 16)
            sp.wait_ge(s_stored, 16)

        @block.vector
        def _(dve):
            link = chained(dve, s_ch)
            nc.vector.memset(last_dst[:], P * 4 * S).then_inc(s_z, 1)
            dve.wait_ge(s_in, 16 * CB)
            dve.wait_ge(s_iota, 2)
            link(nc.vector.tensor_scalar(last_win[:], last_dst[:], 7, None, ALU.arith_shift_right))
            link(nc.vector.tensor_tensor(key[:], last_win[:], tile_id[:], ALU.add))
            for b in range(CB):
                ins = nc.vector.tensor_scalar(before[:, b, :], step_iota[:], key[:, b:b + 1], None, ALU.is_gt)
            ins.then_inc(s_before, 1)
            dve.wait_ge(s_sum, 1)
            link(nc.vector.tensor_copy(tile_of[:].rearrange("p (a s) -> p a s", a=2), ps[:, :, 0:SH]))
            link(nc.vector.tensor_tensor(window_of[:], step_iota[:], tile_of[:], ALU.subtract))
            link(nc.vector.tensor_scalar(window_of[:], window_of[:], float(T - 1), None, ALU.min))
            link(nc.vector.tensor_copy(k.step_window[:], window_of[0:1, :]))
            nc.vector.tensor_scalar(tile_int[:], tile_of[0:1, :], float(C - 1), None, ALU.min).then_inc(s_tile, 1)
            for b in range(CB):
                link(nc.vector.tensor_scalar(k.pick[:, b, :], tile_of[:], tile_id[:, b:b + 1], None,
                                             ALU.is_equal))
            link(nc.vector.tensor_scalar(k.place[:], window_of[:], float(P), 1.0, ALU.mult, ALU.add))

        @block.tensor
        def _(pe):
            pe.wait_ge(s_before, 1)
            for h in range(2):
                for b in range(CB):
                    ins = nc.tensor.matmul(ps[:, h, 0:SH], k.ones[:], before[:, b, h * SH:(h + 1) * SH],
                                           start=(b == 0), stop=(b == CB - 1))
            ins.then_inc(s_sum, 1)


def to_steps(nc, k, name, source, width, picked, integer):
    with ExitStack() as ctx:
        sem = lambda n: (k.semaphore(f"{name}_{n}"))
        dt = i32 if integer else fp32
        raw = ctx.enter_context(nc.sbuf_tensor(name + "_raw", [P, CB, P * width], dt))
        rows = raw
        if integer:
            rows = ctx.enter_context(nc.sbuf_tensor(name + "_rows", [P, CB, P * width], fp32))
        ps = ctx.enter_context(nc.psum_tensor(name + "_ps", [P, 4, 512], fp32))
        s_zero, s_in, s_rows, s_out, s_kept, s_ch = (sem(n) for n in ("zero", "in", "rows", "out", "kept", "ch"))
        block = ctx.enter_context(nc.Block())
        full = C // P

        @block.sync
        def _(sp):
            sp.wait_ge(s_zero, 1)
            sp.dma_start(raw[:, 0:full, :], source[0:full * P, :].rearrange("(b c) w -> c b w", c=P))\
                .then_inc(s_in, 16)
            sp.dma_start(raw[0:C - full * P, full, :], source[full * P:C, :]).then_inc(s_in, 16)

        @block.vector
        def _(dve):
            link = chained(dve, s_ch)
            nc.vector.memset(raw[:, full, :], 0).then_inc(s_zero, 1)
            dve.wait_ge(s_in, 32)
            if integer:
                nc.vector.tensor_copy(rows[:], raw[:]).then_inc(s_rows, 1)
            for n, (q, out, add) in enumerate(picked):
                dve.wait_ge(s_out, n + 1)
                half = ps[:, 2 * (n % 2):2 * (n % 2) + 2, 0:SH]
                o = out.rearrange("p (a s) -> p a s", a=2)
                nc.vector.tensor_scalar(o, half, float(add), None, ALU.add).then_inc(s_kept, 1)

        @block.tensor
        def _(pe):
            if integer:
                pe.wait_ge(s_rows, 1)
            else:
                pe.wait_ge(s_in, 32)
            for n, (q, _, _) in enumerate(picked):
                if n >= 2:
                    pe.wait_ge(s_kept, n - 1)
                for h in range(2):
                    first, end = max(0, (h * SH - T + 1) // P), min(CB, ((h + 1) * SH - 1) // P + 1)
                    for b in range(first, end):
                        lhs = rows[:, b, :].rearrange("c (p w) -> c p w", w=width)[:, :, q]
                        ins = nc.tensor.matmul(ps[:, 2 * (n % 2) + h, 0:SH], lhs,
                                               k.pick[:, b, h * SH:(h + 1) * SH],
                                               start=(b == first), stop=(b == end - 1))
                ins.then_inc(s_out, 1)


def steps_of_graph(nc, k):
    to_steps(nc, k, "ts_src", k.src.rearrange("(c p) -> c p", p=P), 1, [(0, k.src_step[:], 0.0)], True)
    with ExitStack() as ctx:
        dst = ctx.enter_context(nc.sbuf_tensor("sg_dst", [P, S], fp32))
        to_steps(nc, k, "ts_dst", k.dst_ext[1:1 + EP].rearrange("(c p) -> c p", p=P), 1,
                 [(0, dst[:], 0.0)], True)
        sem = lambda n: (k.semaphore(n))
        s_ch, s_ps = sem("sg_ch"), sem("sg_ps")
        ps = ctx.enter_context(nc.psum_tensor("sg_ps", [P, 2, 512], fp32))
        block = ctx.enter_context(nc.Block())

        @block.tensor
        def _(pe):
            for h in range(2):
                for b in range(CB):
                    ins = nc.tensor.matmul(ps[:, h, 0:SH], k.ones[:], k.pick[:, b, h * SH:(h + 1) * SH],
                                           start=(b == 0), stop=(b == CB - 1))
            ins.then_inc(s_ps, 1)

        @block.vector
        def _(dve):
            link = chained(dve, s_ch)
            link(nc.vector.tensor_tensor(k.place[:], dst[:], k.place[:], ALU.subtract))
            dve.wait_ge(s_ps, 1)
            o = k.place[:].rearrange("p (a s) -> p a s", a=2)
            link(nc.vector.tensor_tensor(o, o, ps[:, :, 0:SH], ALU.add))



def sort_positions(nc, k):
    with ExitStack() as ctx:
        sb = lambda n, s, d=fp32: ctx.enter_context(nc.sbuf_tensor("so_" + n, s, d))
        sem = lambda n: (k.semaphore("so_" + n))
        vals = sb("vals", [P, 5, J])
        same = sb("same", [P, 2, J])
        hot = sb("hot", [P, RELS + 1, J])
        fwd = sb("fwd", [P, RELS + 1, J])
        bwd = sb("bwd", [P, RELS, J])
        ints = fwd[:, 0:5, :].bitcast(i32)
        tmp = sb("tmp", [P, J])
        sum_ = sb("sum", [P, J])
        s_in, s_ch, s_iota, s_out = sem("in"), sem("ch"), sem("iota"), sem("out")
        scan_f = segmented_scan(nc, k, ctx, "so_f", [(fwd[:, q, :], hot[:, q, :], same[:, 0, :], False)
                                                  for q in range(RELS + 1)], ALU.mult, ALU.add, 0.0)
        scan_b = segmented_scan(nc, k, ctx, "so_b", [(bwd[:, q, :], hot[:, q, :], same[:, 1, :], True)
                                                  for q in range(RELS)], ALU.mult, ALU.add, 0.0)
        block = ctx.enter_context(nc.Block())
        here, prev, nxt, rel, src = range(5)

        @block.gpsimd
        def _(pool):
            pool.iota(hot[:, RELS, :], [[1, J]], 0, J, allow_small_or_imprecise_dtypes=True).then_inc(s_iota, 1)

        @block.sync
        def _(sp):
            for q, view in ((here, k.dst_ext[1:1 + EP]), (prev, k.dst_ext[0:EP]), (nxt, k.dst_ext[2:2 + EP]),
                            (rel, k.rel), (src, k.src)):
                sp.dma_start(ints[:, q, :], view.rearrange("(p j) -> p j", j=J)).then_inc(s_in, 16)

        @block.tensor
        def _(pe):
            scan_f[1](k.ident[:])
            scan_b[1](k.ident[:])

        @block.vector
        def _(dve):
            link = chained(dve, s_ch)
            dve.wait_ge(s_in, 80)
            dve.wait_ge(s_iota, 1)
            v = nc.vector
            link(v.tensor_copy(vals[:], ints))
            link(v.tensor_tensor(same[:, 0, :], vals[:, here, :], vals[:, prev, :], ALU.is_equal))
            link(v.tensor_tensor(same[:, 1, :], vals[:, here, :], vals[:, nxt, :], ALU.is_equal))
            for r in range(RELS):
                link(v.tensor_scalar(hot[:, r, :], vals[:, rel, :], float(r), None, ALU.is_equal))
            link(v.tensor_tensor(tmp[:], hot[:, RELS, :], same[:, 0, :], ALU.mult))
            link(v.tensor_tensor(hot[:, RELS, :], hot[:, RELS, :], tmp[:], ALU.subtract))
            scan_f[0](link)
            scan_b[0](link)
            link(v.tensor_tensor(bwd[:], bwd[:], fwd[:, 0:RELS, :], ALU.add))
            link(v.tensor_tensor(bwd[:], bwd[:], hot[:, 0:RELS, :], ALU.subtract))
            link(v.tensor_copy(sum_[:], fwd[:, RELS, :]))
            link(v.memset(k.rows[:, :, 2], 0.0))
            for r in range(RELS):
                link(v.tensor_tensor(tmp[:], hot[:, r, :], fwd[:, r, :], ALU.mult))
                link(v.tensor_tensor(sum_[:], sum_[:], tmp[:], ALU.add))
                link(v.scalar_tensor_tensor(tmp[:], vals[:, rel, :], float(r), bwd[:, r, :], ALU.is_gt, ALU.mult))
                link(v.tensor_tensor(sum_[:], sum_[:], tmp[:], ALU.add))
                link(v.scalar_tensor_tensor(k.rows[:, :, 2], bwd[:, r, :], 0.0, k.rows[:, :, 2], ALU.is_gt, ALU.add))
            link(v.tensor_copy(k.position[:], sum_[:]))
            link(v.scalar_tensor_tensor(k.rows[:, :, 0], vals[:, src, :], float(RELS), vals[:, rel, :], ALU.mult, ALU.add))
            link(v.scalar_tensor_tensor(k.rows[:, :, 1], vals[:, here, :], float(RELS), vals[:, rel, :], ALU.mult, ALU.add))
            v.tensor_copy(k.rows[:, :, 3], vals[:, here, :])


def scatter_sorted(nc, k, ctx):
    sb = lambda n, s, d=fp32: ctx.enter_context(nc.sbuf_tensor("sc_" + n, s, d))
    sem = lambda n: (k.semaphore("sc_" + n))
    at = sb("at", [P, 2, GW], i32)
    row = sb("row", [P, 2, GW, 4])
    edge = sb("edge", [1, 4])
    s_staged, s_edge, s_ends, s_go = sem("staged"), sem("edge"), sem("ends"), sem("go")
    s_wrote = [sem(f"wrote{g}") for g in range(2)]
    groups, rest = J // GW, J % GW

    def sp_part():
        nc.sync.wait_ge(s_edge, 1)
        nc.sync.dma_start(k.sorted_rows[0:1, :], edge[:]).then_inc(s_ends, 16)
        nc.sync.dma_start(k.sorted_rows[EP + 1:EP + 2, :], edge[:]).then_inc(s_ends, 16)
        nc.sync.wait_ge(s_ends, 32)

    def pool_part():
        pool = nc.gpsimd
        pool.memset(edge[:], -1.0).then_inc(s_edge, 1)

        def write(kk, g, turn, n=GW):
            if after(kk, 2):
                pool.wait_ge(s_wrote[g], turn * (16 * GW))
            pool.tensor_copy(at[:, g, 0:n], k.position[:, ds(kk * GW, n)])
            pool.tensor_copy(row[:, g, 0:n, :], k.rows[:, ds(kk * GW, n), :]).then_inc(s_staged, 1)
            pool.wait_ge(s_staged, kk + 1)
            pool.sem_inc(s_go, 1)
            for q in range(n):
                pool.indirect_dma_start(k.sorted_rows, bass.IndirectOffsetOnAxis(ap=at[:, g, q:q + 1], axis=0),
                                        row[:, g, q, :], None).then_inc(s_wrote[g], 16)

        grouped(pool, groups, write)
        write(groups, groups % 2, groups // 2, rest)
        turns = [(groups + 1 - g) // 2 for g in range(2)]
        for g in range(2):
            extra = 16 * rest if groups % 2 == g else 0
            pool.wait_ge(s_wrote[g], 16 * GW * turns[g] + extra)

    return sp_part, pool_part



def hgt_tables(nc, k):
    FQ = 3 * D
    BANKS = 4
    with ExitStack() as ctx:
        sb = lambda n, s, d=fp32: ctx.enter_context(nc.sbuf_tensor("ht_" + n, s, d))
        ps = lambda n, s: ctx.enter_context(nc.psum_tensor("ht_" + n, s, fp32))
        sem = lambda n: (k.semaphore("ht_" + n))
        scatter_sp, scatter_pool = scatter_sorted(nc, k, ctx)
        w = sb("w", [P, 2 * TYPES, FQ])
        bias = sb("bias", [TYPES, FQ])
        rel_w = sb("rel_w", [P, 2, 2, RELS, P])
        pri = sb("pri", [P, RELS, HEADS])
        xt = sb("xt", [P, 2, D])
        s_xt = [sem(f"xt{g}") for g in range(2)]
        types_in = sb("types_in", [P, 2, P], i32)
        types = sb("types", [P, P])
        s_type = [sem(f"type{g}") for g in range(2)]
        xT = sb("xT", [P, 2, 2 * TYPES, P])
        maskT = sb("maskT", [TYPES, 2, P])
        q_out = sb("q_out", [P, 2, D])
        kv = sb("kv", [P, 2, 2 * D])
        kvT = sb("kvT", [P, 2, 4, P])
        rel_out = sb("rel_out", [P, 2, 2, RELS, D])
        p_turn = ps("p_turn", [P, 512])
        p_qkv = ps("p_qkv", [P, 2, 512])
        p_kvT = ps("p_kvT", [P, 512])
        p_rel = ps("p_rel", [P, BANKS, 512])
        s_x, s_zero, s_w, s_ch = (sem(n) for n in ("x", "zero", "w", "ch"))
        s_types, s_turn, s_xT, s_qkv, s_q, s_kv, s_kvT, s_kvTs, s_rel, s_even, s_odd = (
            sem(n) for n in ("types", "turn", "xT", "qkv", "q", "kv", "kvT", "kvTs", "rel", "even", "odd"))
        s_qout = [sem(f"qout{g}") for g in range(2)]
        s_relout = [sem(f"relout{g}") for g in range(2)]
        block = ctx.enter_context(nc.Block())

        def rel_piece(g, m):
            kind, half, rh = m // 4, (m // 2) % 2, m % 2
            return rel_out[:, g, kind, 4 * rh:4 * rh + 4, half * P:(half + 1) * P]

        @block.gpsimd
        def _(pool):
            scatter_pool()

        @block.sync
        def _(sp):
            with nc.allow_non_contiguous_dma(reason="a type for each node"):
                sp.dma_start(k.type_int[:], k.node_type.rearrange("(t p) -> p t", p=P)).then_inc(s_x, 16)
            for n, (wt, bt) in enumerate(((k.L0_Wk, k.L0_bk), (k.L0_Wv, k.L0_bv), (k.L0_Wq, k.L0_bq))):
                sp.dma_start(w[:, :, n * D:(n + 1) * D], wt.rearrange("t (h i) o -> i (t h) o", i=P)).then_inc(s_w, 16)
                sp.dma_start(bias[:, n * D:(n + 1) * D], bt).then_inc(s_w, 16)
            sp.wait_ge(s_zero, 1)
            for m, mat in enumerate((k.L0_rel_att, k.L0_rel_msg)):
                for h in range(HEADS):
                    b = DK * (h % 4)
                    sp.dma_start(rel_w[b:b + DK, m, h // 4, :, b:b + DK],
                                 mat[:, h, :, :].rearrange("r d e -> d r e")).then_inc(s_w, 16)
            sp.dma_start(pri[:], k.L0_rel_pri.partition_broadcast(P)).then_inc(s_w, 16)
            scatter_sp()

            def store(u, g, turn):
                sp.wait_ge(s_q, u + 1)
                sp.dma_start(k.q_table[ds(u * P, P), :], q_out[:, g, :]).then_inc(s_qout[g], 16)
                sp.wait_ge(s_even, u * 4 + 4)
                sp.wait_ge(s_odd, u * 4 + 4)
                for m, table in enumerate((k.kr_table, k.vr_table)):
                    sp.dma_start(table.rearrange("(n r) d -> n r d", r=RELS)[ds(u * P, P), :, :],
                                 rel_out[:, g, m, :, :]).then_inc(s_relout[g], 16)

            grouped(sp, T, store, last=3)
            for g in range(2):
                sp.wait_ge(s_qout[g], 16 * ((T + 1 - g) // 2))
                sp.wait_ge(s_relout[g], 32 * ((T + 1 - g) // 2))

        @block.vector
        def _(dve):
            v = nc.vector
            link = chained(dve, s_ch)
            v.memset(rel_w[:], 0.0).then_inc(s_zero, 1)
            dve.wait_ge(s_x, 16)
            link(v.tensor_copy(k.type_mask[:, :, 0], k.type_int[:]))
            for t in range(TYPES - 1, -1, -1):
                link(v.tensor_scalar(k.type_mask[:, :, t], k.type_mask[:, :, 0], float(t), None, ALU.is_equal))
            dve.wait_ge(s_w, 16 * (6 + 2 * HEADS + 1))
            for half in range(2):
              for r in range(RELS):
                a = rel_w[:, 0, half, r, :].rearrange("p (h e) -> p h e", e=DK)
                f = col(pri[:, r, 4 * half:4 * half + 4], DK)
                link(v.scalar_tensor_tensor(a, a, float(DK) ** -0.5, f, ALU.mult, ALU.mult))

            def mask(u, g, turn):
                dve.wait_ge(s_type[g], turn * 16 + 16)
                if after(u, 1):
                    dve.wait_ge(s_xT, u)
                v.tensor_copy(types[:], types_in[:, g, :]).then_inc(s_types, 1)
                dve.wait_ge(s_types, u + 1)
                if after(u, 2):
                    dve.wait_ge(s_qkv, u - 1)
                v.tensor_scalar(maskT[:, g, :], types[0:TYPES, :], k.part[0:TYPES, 0:1], None, ALU.is_equal)
                dve.wait_ge(s_turn, u + 1)
                for t in range(TYPES):
                    ins = v.scalar_tensor_tensor(xT[:, g, 2 * t:2 * t + 2, :], types[:].unsqueeze(1).to_broadcast([P, 2, P]), float(t),
                                                 p_turn[:, 0:D].rearrange("p (c n) -> p c n", n=P), ALU.is_equal, ALU.mult)
                ins.then_inc(s_xT, 1)

            mask(0, 0, 0)

            def tile(u, g, turn):
                if before(u, T - 1):
                    mask(u + 1, 1 - g, turn + g)
                if before(u, T):
                    dve.wait_ge(s_qkv, u + 1)
                    if after(u, 2):
                        dve.wait_ge(s_kvT, u - 1)
                    v.tensor_copy(kv[:, g, :], p_qkv[:, 0, :]).then_inc(s_kv, 1)
                if after(u, 1):
                    o = 1 - g
                    if after(u, 3):
                        dve.wait_ge(s_relout[o], (turn if g == 1 else turn - 1) * 32)
                    for m in range(0, 8, 2):
                        dve.wait_ge(s_rel, u * 8 + (m - 7))
                        v.tensor_copy(rel_piece(o, m), p_rel[:, m % BANKS, :].rearrange("p (r e) -> p r e", e=P)).then_inc(s_even, 1)

            grouped(dve, T + 1, tile, last=2)

        @block.scalar
        def _(act):
            def copy(o, i):
                return nc.scalar.activation(o, i, ACT.Copy)

            def load(u, g, turn):
                if after(u, 2):
                    act.wait_ge(s_turn, u - 1)
                    act.wait_ge(s_types, u - 1)
                act.dma_start(xt[:, g, :], k.x[ds(u * P, P), :]).then_inc(s_xt[g], 16)
                act.dma_start(types_in[:, g, :], k.node_type[ds(u * P, P)].partition_broadcast(P)).then_inc(s_type[g], 16)

            load(0, 0, 0)
            load(1, 1, 0)

            def tile(u, g, turn):
                if before(u, T - 2):
                    load(u + 2, g, turn + 1)
                if before(u, T):
                    act.wait_ge(s_qkv, u + 1)
                    if after(u, 2):
                        act.wait_ge(s_qout[g], turn * 16)
                    copy(q_out[:, g, :], p_qkv[:, 1, 0:D]).then_inc(s_q, 1)
                if after(u, 1):
                    o = 1 - g
                    if after(u, 3):
                        act.wait_ge(s_relout[o], (turn if g == 1 else turn - 1) * 32)
                    for m in range(1, 8, 2):
                        act.wait_ge(s_rel, u * 8 + (m - 7))
                        copy(rel_piece(o, m), p_rel[:, m % BANKS, :].rearrange("p (r e) -> p r e", e=P)).then_inc(s_odd, 1)
                if before(u, T):
                    act.wait_ge(s_kvT, u + 1)
                    if after(u, 2):
                        act.wait_ge(s_rel, u * 8 - 8)
                    copy(kvT[:, g, :, :], p_kvT[:].rearrange("p (c n) -> p c n", n=P)).then_inc(s_kvTs, 1)

            grouped(act, T + 1, tile, last=3)

        @block.tensor
        def _(pe):
            mm, tr = nc.tensor.matmul, nc.tensor.transpose

            def turn_x(u, g, turn):
                pe.wait_ge(s_xt[g], turn * 16 + 16)
                if after(u, 1):
                    pe.wait_ge(s_xT, u)
                for c in range(2):
                    ins = tr(p_turn[:, c * P:(c + 1) * P], xt[:, g, c * P:(c + 1) * P], k.ident[:])
                ins.then_inc(s_turn, 1)

            pe.wait_ge(s_w, 16 * (6 + 2 * HEADS + 1))
            turn_x(0, 0, 0)

            def tile(u, g, turn):
                if before(u, T - 1):
                    turn_x(u + 1, 1 - g, turn + g)
                if before(u, T):
                    pe.wait_ge(s_xT, u + 1)
                    if after(u, 1):
                        pe.wait_ge(s_q, u)
                        pe.wait_ge(s_kv, u)
                    for lo, hi in ((0, 512), (512, FQ)):
                        o = p_qkv[:, lo // 512, 0:hi - lo]
                        for c in range(2 * TYPES):
                            mm(o, xT[:, g, c, :], w[:, c, lo:hi], start=(c == 0), stop=False)
                        ins = mm(o, maskT[:, g, :], bias[:, lo:hi], start=False, stop=True)
                    ins.then_inc(s_qkv, 1)
                if after(u, 1):
                    o = 1 - g
                    pe.wait_ge(s_kvTs, u)
                    for m in range(8):
                        if m >= BANKS:
                            j = m - BANKS
                            pe.wait_ge(s_odd if j % 2 else s_even, u * 4 + (j // 2 - 3))
                        elif after(u, 2):
                            j = max(i for i in range(8) if i % BANKS == m)
                            pe.wait_ge(s_odd if j % 2 else s_even, u * 4 + (j // 2 - 7))
                        kind, half, rh = m // 4, (m // 2) % 2, m % 2
                        mm(p_rel[:, m % BANKS, :], kvT[:, o, 2 * kind + half, :],
                           rel_w[:, kind, half, 4 * rh:4 * rh + 4, :].rearrange("p r e -> p (r e)"),
                           start=True, stop=True).then_inc(s_rel, 1)
                if before(u, T):
                    pe.wait_ge(s_kv, u + 1)
                    if after(u, 1):
                        pe.wait_ge(s_kvTs, u)
                    for c in range(4):
                        ins = tr(p_kvT[:, c * P:(c + 1) * P], kv[:, g, c * P:(c + 1) * P], k.ident[:])
                    ins.then_inc(s_kvT, 1)

            grouped(pe, T + 1, tile, last=2)





def place_rows(nc, k):
    blocks = -(-S // P)
    with ExitStack() as ctx:
        sem = lambda n: k.semaphore("pr_" + n)
        turned = ctx.enter_context(nc.sbuf_tensor("pr_turned", [P, blocks, P], fp32))
        ps = ctx.enter_context(nc.psum_tensor("pr_ps", [P, 2, 512], fp32))
        s_turn, s_kept, s_out = sem("turn"), sem("kept"), sem("out")
        block = ctx.enter_context(nc.Block())
        last = S - (blocks - 1) * P

        @block.tensor
        def _(pe):
            for b in range(blocks):
                n = P if b < blocks - 1 else last
                ins = nc.tensor.transpose(ps[0:n, b // 4, (b % 4) * P:(b % 4 + 1) * P], k.place[:, b * P:b * P + n], k.ident[:])
            ins.then_inc(s_turn, 1)

        @block.vector
        def _(dve):
            dve.wait_ge(s_turn, 1)
            nc.vector.tensor_copy(turned[:, 0:4, :], ps[:, 0, :].rearrange("p (b n) -> p b n", n=P))
            nc.vector.tensor_copy(turned[:, 4:blocks - 1, :], ps[:, 1, 0:(blocks - 5) * P].rearrange("p (b n) -> p b n", n=P))
            nc.vector.tensor_copy(turned[0:last, blocks - 1, :], ps[0:last, 1, (blocks - 5) * P:(blocks - 4) * P]).then_inc(s_kept, 1)

        @block.sync
        def _(sp):
            sp.wait_ge(s_kept, 1)
            rows = k.place_row.rearrange("(s p) -> s p", p=P)
            for b in range(blocks):
                n = P if b < blocks - 1 else last
                sp.dma_start(rows[b * P:b * P + n, :], turned[0:n, b, :]).then_inc(s_out, 16)
            sp.wait_ge(s_out, 16 * blocks)


def hgt_scores(nc, k):
    with ExitStack() as ctx:
        sb = lambda n, s, d=fp32: ctx.enter_context(nc.sbuf_tensor("hs_" + n, s, d))
        sem = lambda n: k.semaphore("hs_" + n)
        q_rows = sb("q_rows", [P, T, D])
        at = sb("at", [P, WAYS, GW], i32)
        key = sb("key", [P, WAYS, GW, D])
        place = sb("place", [P, WAYS, GW * P])
        hot = sb("hot", [P, 2, GW * P])
        product = sb("product", [P, GW, D])
        part = sb("part", [P, 1])
        ps = ctx.enter_context(nc.psum_tensor("hs_ps", [P, 2, GW, D], fp32))
        s_q, s_iota, s_staged, s_go, s_hot, s_query, s_product, s_score = (
            sem(n) for n in ("q", "iota", "staged", "go", "hot_s", "query", "product_s", "score"))
        s_got = [sem(f"got{g}") for g in range(WAYS)]
        s_place = [sem(f"place{g}") for g in range(WAYS)]
        block = ctx.enter_context(nc.Block())
        groups = S // GW

        @block.sync
        def _(sp):
            sp.dma_start(q_rows[:], k.q_table.rearrange("(t p) d -> p t d", p=P)).then_inc(s_q, 16)

            def load(kk, g, turn):
                if after(kk, WAYS):
                    sp.wait_ge(s_hot, kk - (WAYS - 1))
                sp.dma_start(place[:, g, :], k.place_row[ds(kk * GW * P, GW * P)].partition_broadcast(P)).then_inc(s_place[g], 16)

            grouped(sp, groups, load, ways=WAYS)

        @block.scalar
        def _(act):
            def stage(kk, g, turn):
                if after(kk, WAYS):
                    act.wait_ge(s_got[g], turn * (16 * GW))
                nc.scalar.activation(at[:, g, :], k.pair_step[:, ds(kk * GW, GW)], ACT.Copy).then_inc(s_staged, 1)

            grouped(act, groups, stage, ways=WAYS)

        @block.gpsimd
        def _(pool):
            pool.iota(part[:], [[0, 1]], 0, 1, allow_small_or_imprecise_dtypes=True).then_inc(s_iota, 1)

            def gather(kk, g, turn):
                pool.wait_ge(s_staged, kk + 1)
                if after(kk, WAYS):
                    pool.wait_ge(s_product, kk - (WAYS - 1))
                pool.sem_inc(s_go, 1)
                for q in range(GW):
                    pool.indirect_dma_start(key[:, g, q, :], None, k.kr_table,
                                            bass.IndirectOffsetOnAxis(ap=at[:, g, q:q + 1], axis=0)).then_inc(s_got[g], 16)

            grouped(pool, groups, gather, ways=WAYS)

        @block.tensor
        def _(pe):
            registers = [nc.tensor.alloc_register(f"hs_window{q}") for q in range(GW)]
            pe.wait_ge(s_q, 16)

            def query(kk, way, turn):
                g = way % 2
                windows = four(nc.tensor, registers, k.step_window, kk, T - 1)
                pe.wait_ge(s_hot, kk + 1)
                if after(kk, 2):
                    pe.wait_ge(s_product, kk - 1)
                for q in range(GW):
                    ins = nc.tensor.matmul(ps[:, g, q, :], hot[:, g, q * P:(q + 1) * P],
                                           q_rows[:, ds(windows[q], 1), :].squeeze(1), start=True, stop=True)
                ins.then_inc(s_query, 1)

            grouped(pe, groups, query, ways=WAYS)

        @block.vector
        def _(dve):
            v = nc.vector
            dve.wait_ge(s_iota, 1)

            def compare(kk, way, turn):
                if after(kk, 2):
                    dve.wait_ge(s_query, kk - 1)
                dve.wait_ge(s_place[way], turn * 16 + 16)
                v.tensor_scalar(hot[:, way % 2, :], place[:, way, :], part[:, 0:1], None, ALU.is_equal).then_inc(s_hot, 1)

            compare(0, 0, 0)

            def dot(kk, way, turn):
                if before(kk, groups - 1):
                    compare(kk + 1, (way + 1) % WAYS, turn + (way == WAYS - 1))
                if after(kk, 1):
                    dve.wait_ge(s_score, kk)
                dve.wait_ge(s_got[way], turn * (16 * GW) + 16 * GW)
                dve.wait_ge(s_query, kk + 1)
                v.tensor_tensor(product[:], ps[:, way % 2, :, :], key[:, way, :, :], ALU.mult).then_inc(s_product, 1)
                dve.wait_ge(s_product, kk + 1)
                v.tensor_reduce(k.step_w[:, ds(kk * GW, GW), :], product[:].rearrange("p n (h d) -> p n h d", d=DK),
                                AX.X, ALU.add).then_inc(s_score, 1)

            grouped(dve, groups, dot, last=WAYS, ways=WAYS)


def scores_to_edges(nc, k, score):
    blocks = -(-S // P)
    last = S - (blocks - 1) * P
    H = HEADS
    with ExitStack() as ctx:
        sb = lambda n, s: ctx.enter_context(nc.sbuf_tensor("se_" + n, s, fp32))
        ps = lambda n, s: ctx.enter_context(nc.psum_tensor("se_ps_" + n, s, fp32))
        sem = lambda n: k.semaphore("se_" + n)
        by_step = sb("by_step", [P, blocks, P, H])
        pickT = sb("pickT", [P, CB, 2, P])
        tiles = sb("tiles", [P, 2, P * H])
        p_turn, p_pick, p_out = ps("turn", [P, 2, 4, P]), ps("pick", [P, 2, P]), ps("out", [P, 2, 2, 512])
        s_turn, s_kept, s_pick, s_pickT, s_out, s_tiles, s_loaded = (
            sem(n) for n in ("turn", "kept", "pick", "pickT_s", "out", "tiles_s", "loaded"))
        s_stored = [sem(f"stored{g}") for g in range(2)]
        block = ctx.enter_context(nc.Block())
        rows_of = lambda b: P if b < blocks - 1 else last
        tiles_of = lambda b: min(P, C - b * P)
        steps_for = lambda b: [i for i in range(2) if b + i < blocks]
        units = [(b, h) for b in range(blocks) for h in range(0, H, 4)]

        @block.tensor
        def _(pe):
            for n, (b, h) in enumerate(units):
                if n >= 2:
                    pe.wait_ge(s_kept, n - 1)
                for i in range(4):
                    ins = nc.tensor.transpose(p_turn[0:rows_of(b), n % 2, i, :],
                                              k.step_w[:, b * P:b * P + rows_of(b), h + i], k.ident[:])
                ins.then_inc(s_turn, 1)
            for b in range(CB):
                if b >= 1:
                    pe.wait_ge(s_pickT, b)
                for i in steps_for(b):
                    r = rows_of(b + i)
                    ins = nc.tensor.transpose(p_pick[0:r, i, :], k.pick[:, b, (b + i) * P:(b + i) * P + r], k.ident[:])
                ins.then_inc(s_pick, 1)
            pe.wait_ge(s_kept, len(units))
            pe.wait_ge(s_pickT, CB)
            for b in range(CB):
                if b >= 2:
                    pe.wait_ge(s_tiles, b - 1)
                m = tiles_of(b)
                for half in range(2):
                    todo = steps_for(b)
                    for i in todo:
                        r = rows_of(b + i)
                        ins = nc.tensor.matmul(p_out[0:m, b % 2, half, :], pickT[0:r, b, i, 0:m],
                                               by_step[0:r, b + i, half * 64:(half + 1) * 64, :].rearrange("s p h -> s (p h)"),
                                               start=(i == 0), stop=(i == todo[-1]))
                ins.then_inc(s_out, 1)

        @block.vector
        def _(dve):
            v = nc.vector
            for n, (b, h) in enumerate(units):
                r = rows_of(b)
                dve.wait_ge(s_turn, n + 1)
                v.tensor_copy(by_step[0:r, b, :, h:h + 4].rearrange("s p h -> s h p"), p_turn[0:r, n % 2, :, :]).then_inc(s_kept, 1)
            for b in range(CB):
                dve.wait_ge(s_pick, b + 1)
                for i in steps_for(b):
                    r = rows_of(b + i)
                    ins = v.tensor_copy(pickT[0:r, b, i, :], p_pick[0:r, i, :])
                ins.then_inc(s_pickT, 1)

        @block.scalar
        def _(act):
            for b in range(CB):
                m = tiles_of(b)
                act.wait_ge(s_out, b + 1)
                if b >= 2:
                    act.wait_ge(s_stored[b % 2], 16 * (b // 2))
                nc.scalar.activation(tiles[0:m, b % 2, :].rearrange("c (a w) -> c a w", a=2), p_out[0:m, b % 2, :, :], ACT.Copy).then_inc(s_tiles, 1)

        @block.sync
        def _(sp):
            rows = k.weight_dram.rearrange("(c p) h -> c (p h)", p=P)
            for b in range(CB):
                m = tiles_of(b)
                sp.wait_ge(s_tiles, b + 1)
                sp.dma_start(rows[b * P:b * P + m, :], tiles[0:m, b % 2, :]).then_inc(s_stored[b % 2], 16)
            for g in range(2):
                sp.wait_ge(s_stored[g], 16 * ((CB + 1 - g) // 2))
            sp.dma_start(score, k.weight_dram.rearrange("(p j) h -> p j h", j=J)).then_inc(s_loaded, 16)
            sp.wait_ge(s_loaded, 16)


def hgt_softmax(nc, k, score):
    with ExitStack() as ctx:
        sb = lambda n, s, d=fp32: ctx.enter_context(nc.sbuf_tensor("sm_" + n, s, d))
        sem = lambda n: (k.semaphore("sm_" + n))
        rows = sb("rows", [P, 3, J, 4])
        fwd = sb("fwd", [P, J, HEADS])
        bwd = rows[:].rearrange("p a j w -> p (a j w)")[:, 0:J * HEADS].rearrange("p (j h) -> p j h", h=HEADS)
        present = sb("present", [P, J])
        same = sb("same", [P, 2, J])
        gate = sb("gate", [P, 2, J])
        s_in, s_ch, s_shift, s_exp, s_w, s_out = (sem(n) for n in ("in", "ch", "shift", "exp", "w", "out"))
        heads = range(HEADS)
        scans = []
        for name, g, ops, init in (("m", gate, (ALU.add, ALU.max), -BIG), ("s", same, (ALU.mult, ALU.add), 0.0)):
            for way, out, back in ((0, fwd, False), (1, bwd, True)):
                scans.append(segmented_scan(nc, k, ctx, f"sm_{name}{way}",
                             [(out[:, :, h], score[:, :, h], g[:, way, :], back) for h in heads], *ops, init))
        block = ctx.enter_context(nc.Block())

        @block.sync
        def _(sp):
            for q, first in enumerate((1, 0, 2)):
                sp.dma_start(rows[:, q, :, :], k.sorted_rows[first:first + EP, :].rearrange("(p j) w -> p j w", j=J)).then_inc(s_in, 16)
            sp.wait_ge(s_w, 1)
            sp.dma_start(k.weight_dram.rearrange("(p j) h -> p j h", j=J), score).then_inc(s_out, 16)
            sp.wait_ge(s_out, 16)

        @block.tensor
        def _(pe):
            for s in scans:
                s[1](k.ident[:])

        @block.scalar
        def _(act):
            act.wait_ge(s_shift, 1)
            nc.scalar.activation(score, score, ACT.Exp).then_inc(s_exp, 1)

        @block.vector
        def _(dve):
            v = nc.vector
            link = chained(dve, s_ch)
            dve.wait_ge(s_in, 48)
            for way in range(2):
                link(v.tensor_tensor(same[:, way, :], rows[:, 0, :, 1], rows[:, 1 + way, :, 1], ALU.is_equal))
            link(v.tensor_scalar(gate[:], same[:], -1.0, BIG, ALU.add, ALU.mult))
            link(v.tensor_scalar(present[:], rows[:, 0, :, 2], 1.0, None, ALU.max))
            scans[0][0](link)
            scans[1][0](link)
            link(v.tensor_tensor(fwd[:], fwd[:], bwd, ALU.max))
            v.tensor_tensor(score, score, fwd[:], ALU.subtract).then_inc(s_shift, 1)
            dve.wait_ge(s_exp, 1)
            scans[2][0](link)
            scans[3][0](link)
            link(v.tensor_tensor(fwd[:], fwd[:], bwd, ALU.add))
            link(v.tensor_tensor(fwd[:], fwd[:], score, ALU.subtract))
            link(v.tensor_tensor(fwd[:], fwd[:], col(present[:], HEADS), ALU.mult))
            link(v.reciprocal(fwd[:], fwd[:]))
            v.tensor_tensor(score, score, fwd[:], ALU.mult).then_inc(s_w, 1)



def aggregate(nc, k, name, table, table_row, numbers, width, weights=None, heads=0, extra=0, count=False):
    row = D + extra + count
    with ExitStack() as ctx:
        sb = lambda n, s, d=fp32: ctx.enter_context(nc.sbuf_tensor(f"{name}_{n}", s, d))
        sem = lambda n: (k.semaphore(f"{name}_{n}"))
        at = sb("at", [P, WAYS, GW], i32)
        got = sb("got", [P, WAYS, GW, max(table_row, row)])
        hot = sb("hot", [P, WAYS, GW, P])
        p_sum = ctx.enter_context(nc.psum_tensor(f"{name}_sum", [P, 2, GW, 512], fp32))
        s_staged, s_go, s_ready, s_summed, s_added = (sem(n) for n in ("staged", "go", "ready", "summed", "added"))
        s_zero = sem("zero")
        s_got = [sem(f"got{g}") for g in range(WAYS)]
        block = ctx.enter_context(nc.Block())
        groups = S // GW

        @block.gpsimd
        def _(pool):
            def gather(kk, g, turn):
                pool.wait_ge(s_staged, kk + 1)
                if after(kk, WAYS):
                    pool.wait_ge(s_summed, (kk - (WAYS - 1)) * GW)
                pool.sem_inc(s_go, 1)
                for q in range(GW):
                    pool.indirect_dma_start(got[:, g, q, 0:table_row], None, table,
                                            bass.IndirectOffsetOnAxis(ap=at[:, g, q:q + 1], axis=0)).then_inc(s_got[g], 16)

            grouped(pool, groups, gather, ways=WAYS)

        @block.scalar
        def _(act):
            def stage(kk, g, turn):
                if after(kk, WAYS):
                    act.wait_ge(s_got[g], turn * (16 * GW))
                nc.scalar.activation(at[:, g, :], numbers[:, ds(kk * GW, GW)], ACT.Copy).then_inc(s_staged, 1)

            grouped(act, groups, stage, ways=WAYS)

        @block.tensor
        def _(pe):
            def sums(kk, way, turn):
                g = way % 2
                pe.wait_ge(s_ready, kk + 1)
                if weights is None:
                    pe.wait_ge(s_got[way], turn * (16 * GW) + 16 * GW)
                if after(kk, 2):
                    pe.wait_ge(s_added, kk * GW - GW)
                for q in range(GW):
                    nc.tensor.matmul(p_sum[:, g, q, 0:row], hot[:, way, q, :], got[:, way, q, 0:row],
                                     start=True, stop=True).then_inc(s_summed, 1)

            grouped(pe, groups, sums, ways=WAYS)

        @block.vector
        def _(dve):
            v = nc.vector
            if count:
                v.memset(got[:, :, :, D:D + 1], 1.0)
            v.memset(k.acc[:], 0.0).then_inc(s_zero, 1)
            dve.wait_ge(s_zero, 1)

            def ready(kk, way, turn):
                if after(kk, WAYS):
                    dve.wait_ge(s_summed, (kk - (WAYS - 1)) * GW)
                ins = v.tensor_tensor(hot[:, way, :, :], k.window_iota[:],
                                      col(k.place[:, ds(kk * GW, GW)], P), ALU.is_equal)
                if weights is not None:
                    dve.wait_ge(s_got[way], turn * (16 * GW) + 16 * GW)
                    if extra:
                        v.tensor_copy(got[:, way, :, D:D + extra], weights[:, ds(kk * GW, GW), 0:extra])
                    hd = D // heads
                    for q in range(GW):
                        heads_of = got[:, way, q, 0:D].rearrange("p (h d) -> p h d", d=hd)
                        factor = weights[:, ds(kk * GW + q, 1), 0:heads].squeeze(1).unsqueeze(2).to_broadcast([P, heads, hd])
                        ins = v.tensor_tensor(heads_of, heads_of, factor, ALU.mult)
                ins.then_inc(s_ready, 1)

            registers = [v.alloc_register(f"{name}_window{q}") for q in range(GW)]

            def add(kk, g):
                windows = four(v, registers, k.step_window, kk, T - 1)
                for q in range(GW):
                    dve.wait_ge(s_summed, kk * GW + (q + 1))
                    if after(kk, 1) or q:
                        dve.wait_ge(s_added, kk * GW + q)
                    o = k.acc[:, ds(windows[q], 1), 0:row].squeeze(1)
                    v.tensor_tensor(o, o, p_sum[:, g, q, 0:row], ALU.add).then_inc(s_added, 1)

            ready(0, 0, 0)

            def body(kk, way, turn):
                if before(kk, groups - 1):
                    ready(kk + 1, (way + 1) % WAYS, turn + (way == WAYS - 1))
                if after(kk, 1):
                    add(kk - 1, 1 - way % 2)

            grouped(dve, groups, body, last=WAYS, ways=WAYS)
            add(groups - 1, (groups - 1) % 2)



def hgt_update(nc, k):
    with ExitStack() as ctx:
        sb = lambda n, s, d=fp32: ctx.enter_context(nc.sbuf_tensor("hu_" + n, s, d))
        ps = lambda n, s: ctx.enter_context(nc.psum_tensor("hu_ps_" + n, s, fp32))
        sem = lambda n: (k.semaphore("hu_" + n))
        w = sb("w", [P, 2 * TYPES, D])
        bias = sb("bias", [TYPES, D])
        skip = sb("skip", [P, TYPES])
        share = sb("share", [P, T])
        rest = sb("rest", [P, T])
        sums = sb("sums", [P, 2, D])
        types_in = sb("types_in", [P, 2, P], i32)
        types = sb("types", [P, P])
        s_type = [sem(f"type{g}") for g in range(2)]
        xT = sb("xT", [P, 2, 2 * TYPES, P])
        maskT = sb("maskT", [TYPES, 2, P])
        p_turn, p_out = ps("turn", [P, 2, 512]), ps("out", [P, 2, 512])
        s_x, s_w, s_ch, s_skip, s_sig = (sem(n) for n in ("x", "w", "ch", "skip", "sig"))
        s_sums, s_types, s_turn, s_xT, s_out, s_added = (sem(n) for n in ("sums", "types", "turn", "xT", "out", "added"))
        block = ctx.enter_context(nc.Block())

        @block.sync
        def _(sp):
            sp.dma_start(skip[:], k.L0_skip.partition_broadcast(P)).then_inc(s_skip, 16)
            sp.dma_start(w[:], k.L0_Wa.rearrange("t (h i) o -> i (t h) o", i=P)).then_inc(s_w, 16)
            sp.dma_start(bias[:], k.L0_ba).then_inc(s_w, 16)
            sp.dma_start(k.x_now[:], k.x.rearrange("(t p) d -> p t d", p=P)).then_inc(s_x, 16)

            def load(u, g, turn):
                if after(u, 2):
                    sp.wait_ge(s_types, u - 1)
                sp.dma_start(types_in[:, g, :], k.node_type[ds(u * P, P)].partition_broadcast(P)).then_inc(s_type[g], 16)

            grouped(sp, T, load)

        @block.vector
        def _(dve):
            v = nc.vector
            link = chained(dve, s_ch)
            dve.wait_ge(s_sig, 1)
            link(v.tensor_scalar(share[:], k.type_mask[:, :, 0], skip[:, 0:1], None, ALU.mult))
            for t in range(1, TYPES):
                link(v.scalar_tensor_tensor(share[:], k.type_mask[:, :, t], skip[:, t:t + 1], share[:], ALU.mult, ALU.add))
            link(v.tensor_scalar(rest[:], share[:], -1.0, 2.0, ALU.mult, ALU.add))
            dve.wait_ge(s_x, 16)
            link(v.tensor_tensor(k.x_now[:], k.x_now[:], col(rest[:], D), ALU.mult))

            def mask(u, g, turn):
                dve.wait_ge(s_type[g], turn * 16 + 16)
                if after(u, 1):
                    dve.wait_ge(s_xT, u)
                v.tensor_copy(types[:], types_in[:, g, :]).then_inc(s_types, 1)
                dve.wait_ge(s_types, u + 1)
                if after(u, 2):
                    dve.wait_ge(s_out, u - 1)
                v.tensor_scalar(maskT[:, g, :], types[0:TYPES, :], k.part[0:TYPES, 0:1], None, ALU.is_equal)
                dve.wait_ge(s_turn, u + 1)
                for t in range(TYPES):
                    ins = v.scalar_tensor_tensor(xT[:, g, 2 * t:2 * t + 2, :], types[:].unsqueeze(1).to_broadcast([P, 2, P]), float(t),
                                                 p_turn[:, g, 0:D].rearrange("p (c n) -> p c n", n=P), ALU.is_equal, ALU.mult)
                ins.then_inc(s_xT, 1)

            mask(0, 0, 0)

            def tile(u, g, turn):
                if before(u, T - 1):
                    mask(u + 1, 1 - g, turn + g)
                dve.wait_ge(s_out, u + 1)
                o = k.x_now[:, ds(u, 1), :].squeeze(1)
                v.scalar_tensor_tensor(o, p_out[:, g, 0:D], share[:, ds(u, 1)], o, ALU.mult, ALU.add).then_inc(s_added, 1)

            grouped(dve, T, tile, last=1)

        @block.scalar
        def _(act):
            act.wait_ge(s_skip, 16)
            nc.scalar.activation(skip[:], skip[:], ACT.Sigmoid).then_inc(s_sig, 1)

            def take(u, g, turn):
                if after(u, 2):
                    act.wait_ge(s_turn, u - 1)
                nc.scalar.activation(sums[:, g, :], k.acc[:, ds(u, 1), 0:D].squeeze(1), ACT.Copy).then_inc(s_sums, 1)

            grouped(act, T, take)

        @block.tensor
        def _(pe):
            mm, tr = nc.tensor.matmul, nc.tensor.transpose

            def turn_x(u, g):
                pe.wait_ge(s_sums, u + 1)
                if after(u, 2):
                    pe.wait_ge(s_xT, u - 1)
                for c in range(2):
                    ins = tr(p_turn[:, g, c * P:(c + 1) * P], sums[:, g, c * P:(c + 1) * P], k.ident[:])
                ins.then_inc(s_turn, 1)

            pe.wait_ge(s_w, 32)
            turn_x(0, 0)
            turn_x(1, 1)

            def tile(u, g, turn):
                if before(u, T - 2):
                    turn_x(u + 2, g)
                pe.wait_ge(s_xT, u + 1)
                if after(u, 2):
                    pe.wait_ge(s_added, u - 1)
                for c in range(2 * TYPES):
                    mm(p_out[:, g, 0:D], xT[:, g, c, :], w[:, c, :], start=(c == 0), stop=False)
                mm(p_out[:, g, 0:D], maskT[:, g, :], bias[:], start=False, stop=True).then_inc(s_out, 1)

            grouped(pe, T, tile, last=3)


def node_products(nc, k, name, x, weight, cols, table, bias=None, attention=None):
    W = 512
    pieces = -(-cols // W)
    width = min(W, cols)
    extra = 2 * GHEADS if attention else 0
    with ExitStack() as ctx:
        sb = lambda n, s, d=fp32: ctx.enter_context(nc.sbuf_tensor(f"{name}_{n}", s, d))
        ps = lambda n, s: ctx.enter_context(nc.psum_tensor(f"{name}_ps_{n}", s, fp32))
        sem = lambda n: (k.semaphore(f"{name}_{n}"))
        w = sb("w", [P, 2, cols])
        xs = sb("xs", [P, 2, D])
        xT = sb("xT", [P, 2, 2, P])
        out = sb("out", [P, 2, cols + extra])
        b = sb("b", [1, cols]) if bias is not None else None
        if attention:
            vecs = sb("vecs", [P, 2, D])
            product = sb("product", [P, 2, D])
        p_turn, p_out = ps("turn", [P, 2, 512]), ps("out_ps", [P, 2, 512])
        s_w, s_xs, s_turn, s_xT, s_out, s_kept, s_prod, s_sum, s_row = (
            sem(n) for n in ("s_w", "s_xs", "s_turn", "s_xT", "s_out", "s_kept", "s_prod", "s_sum", "s_row"))
        s_stored = [sem(f"s_stored{g}") for g in range(2)]
        loads = len(weight) * 2 + (bias is not None) + (2 if attention else 0)
        block = ctx.enter_context(nc.Block())

        @block.sync
        def _(sp):
            for view, first in weight:
                for h in range(2):
                    sp.dma_start(w[:, h, first:first + view.shape[1]], view[h * P:(h + 1) * P, :]).then_inc(s_w, 16)
            if bias is not None:
                sp.dma_start(b[:], bias.unsqueeze(0)).then_inc(s_w, 16)
            if attention:
                for m, a in enumerate(attention):
                    sp.dma_start(vecs[:, m, :], a.rearrange("h d -> (h d)").partition_broadcast(P)).then_inc(s_w, 16)

            def store(u, g, turn):
                if attention:
                    sp.wait_ge(s_row, u + 1)
                else:
                    sp.wait_ge(s_kept, u * pieces + pieces)
                sp.dma_start(table[ds(u * P, P), :], out[:, g, :]).then_inc(s_stored[g], 16)

            grouped(sp, T, store)
            for g in range(2):
                sp.wait_ge(s_stored[g], 16 * ((T + 1 - g) // 2))

        @block.scalar
        def _(act):
            copy = lambda o, i: nc.scalar.activation(o, i, ACT.Copy)

            def take(u, g):
                if after(u, 2):
                    act.wait_ge(s_turn, u - 1)
                copy(xs[:, g, :], x[:, ds(u, 1), :].squeeze(1)).then_inc(s_xs, 1)

            def turned(u, g):
                act.wait_ge(s_turn, u + 1)
                if after(u, 2):
                    act.wait_ge(s_out, u * pieces - pieces)
                copy(xT[:, g, :, :], p_turn[:, g, 0:2 * P].rearrange("p (c n) -> p c n", n=P)).then_inc(s_xT, 1)

            take(0, 0)
            take(1, 1)
            turned(0, 0)

            def tile(u, g, turn):
                if before(u, T - 1):
                    turned(u + 1, 1 - g)
                if before(u, T - 2):
                    take(u + 2, g)
                if after(u, 2):
                    act.wait_ge(s_stored[g], turn * 16)
                for m in range(pieces):
                    bank = m % 2 if pieces > 1 else g
                    act.wait_ge(s_out, u * pieces + (m + 1))
                    copy(out[:, g, m * W:m * W + width], p_out[:, bank, 0:width]).then_inc(s_kept, 1)

            grouped(act, T, tile, last=3)

        @block.vector
        def _(dve):
            if not attention:
                return
            v = nc.vector
            dve.wait_ge(s_w, 16 * loads)

            def tile(u, g, turn):
                dve.wait_ge(s_kept, u + 1)
                if after(u, 1):
                    dve.wait_ge(s_row, u)
                v.tensor_tensor(product[:], out[:, g, 0:D].unsqueeze(1).to_broadcast([P, 2, D]), vecs[:], ALU.mult).then_inc(s_prod, 1)
                dve.wait_ge(s_prod, u + 1)
                heads = product[:].rearrange("p a (h d) -> p (a h) d", d=GHID)
                v.tensor_reduce(k.node8[:, ds(u, 1), :].squeeze(1), heads, AX.X, ALU.add).then_inc(s_sum, 1)
                dve.wait_ge(s_sum, u + 1)
                v.tensor_scalar(out[:, g, D:D + extra], k.node8[:, ds(u, 1), :].squeeze(1), 1.0, None, ALU.mult).then_inc(s_row, 1)

            grouped(dve, T, tile)

        @block.tensor
        def _(pe):
            def turn_x(u, g):
                pe.wait_ge(s_xs, u + 1)
                if after(u, 2):
                    pe.wait_ge(s_xT, u - 1)
                for c in range(2):
                    ins = nc.tensor.transpose(p_turn[:, g, c * P:(c + 1) * P], xs[:, g, c * P:(c + 1) * P], k.ident[:])
                ins.then_inc(s_turn, 1)

            pe.wait_ge(s_w, 16 * loads)
            turn_x(0, 0)

            def tile(u, g, turn):
                if before(u, T - 1):
                    turn_x(u + 1, 1 - g)
                pe.wait_ge(s_xT, u + 1)
                for m in range(pieces):
                    bank = m % 2 if pieces > 1 else g
                    if after(u, 1) or m >= 2:
                        if pieces > 1 or after(u, 2):
                            pe.wait_ge(s_kept, u * pieces + (m - 1))
                    o = p_out[:, bank, 0:width]
                    for c in range(2):
                        ins = nc.tensor.matmul(o, xT[:, g, c, :], w[:, c, m * W:m * W + width],
                                               start=(c == 0), stop=(c == 1 and bias is None))
                    if bias is not None:
                        ins = nc.tensor.matmul(o, k.ones[0:1, :], b[:, m * W:m * W + width], start=False, stop=True)
                    ins.then_inc(s_out, 1)

            grouped(pe, T, tile, last=1)


def norm_rows(nc, k, name, x, eps, other=None, scale=None, store=None):
    CH = 7
    chunks = T // CH
    with ExitStack() as ctx:
        sb = lambda n, s, d=fp32: ctx.enter_context(nc.sbuf_tensor(f"{name}_{n}", s, d))
        sem = lambda n: (k.semaphore(f"{name}_{n}"))
        square = sb("square", [P, 2, CH, D])
        total = sb("total", [P, T])
        var = sb("var", [P, T])
        eps_col = sb("eps", [P, 1])
        s_ch, s_centred, s_square, s_var, s_root, s_scale, s_done, s_stored, s_eps = (
            sem(n) for n in ("ch", "centred", "squared", "vars", "root", "sc", "done", "stored", "epss"))
        if scale:
            both = sb("both", [P, 2, D])
        block = ctx.enter_context(nc.Block())

        @block.sync
        def _(sp):
            if scale:
                for m, a in enumerate(scale):
                    sp.dma_start(both[:, m, :], a.partition_broadcast(P)).then_inc(s_scale, 16)
            if store is not None:
                full = N // P
                for c in range(chunks):
                    sp.wait_ge(s_done, c + 1)
                    lo, hi = c * CH, min((c + 1) * CH, full)
                    sp.dma_start(store[lo * P:hi * P, :].rearrange("(t p) d -> p t d", p=P), x[:, lo:hi, :]).then_inc(s_stored, 16)
                sp.dma_start(store[full * P:N, :], x[0:N - full * P, full, :]).then_inc(s_stored, 16)
                sp.wait_ge(s_stored, 16 * (chunks + 1))

        @block.scalar
        def _(act):
            for c in range(chunks):
                act.wait_ge(s_centred, c + 1)
                if c >= 2:
                    act.wait_ge(s_var, c - 1)
                nc.scalar.activation(square[:, c % 2, :, :], x[:, c * CH:(c + 1) * CH, :], ACT.Square).then_inc(s_square, 1)
            act.wait_ge(s_var, chunks)
            act.wait_ge(s_eps, 1)
            nc.scalar.activation(var[:], var[:], ACT.Sqrt, bias=eps_col[:], scale=1.0 / D).then_inc(s_root, 1)

        @block.vector
        def _(dve):
            v = nc.vector
            link = chained(dve, s_ch)
            v.memset(eps_col[:], eps).then_inc(s_eps, 1)

            def variance(c):
                dve.wait_ge(s_square, c + 1)
                v.tensor_reduce(var[:, c * CH:(c + 1) * CH], square[:, c % 2, :, :], AX.X, ALU.add).then_inc(s_var, 1)

            for c in range(chunks):
                t = slice(c * CH, (c + 1) * CH)
                if other is not None:
                    link(v.tensor_tensor(x[:, t, :], x[:, t, :], other[:, t, :], ALU.add))
                link(v.tensor_reduce(total[:, t], x[:, t, :], AX.X, ALU.add))
                link(v.tensor_scalar(total[:, t], total[:, t], 1.0 / D, None, ALU.mult))
                v.tensor_tensor(x[:, t, :], x[:, t, :], col(total[:, t], D), ALU.subtract).then_inc(s_centred, 1)
                if c:
                    variance(c - 1)
            variance(chunks - 1)
            dve.wait_ge(s_root, 1)
            link(v.reciprocal(var[:], var[:]))
            if scale:
                dve.wait_ge(s_scale, 32)
            for c in range(chunks):
                t = slice(c * CH, (c + 1) * CH)
                ins = v.tensor_tensor(x[:, t, :], x[:, t, :], col(var[:, t], D), ALU.mult)
                if scale:
                    link(ins)
                    for m, op in ((0, ALU.mult), (1, ALU.add)):
                        ins = v.tensor_tensor(x[:, t, :], x[:, t, :], both[:, m, :].unsqueeze(1).to_broadcast([P, CH, D]), op)
                        if m == 0:
                            link(ins)
                ins.then_inc(s_done, 1)



def segment_starts(nc, k):
    with ExitStack() as ctx:
        sb = lambda n, s, d=fp32: ctx.enter_context(nc.sbuf_tensor("st_" + n, s, d))
        sem = lambda n: (k.semaphore("st_" + n))
        part = sb("part", [P, 1])
        node = sb("node", [P, T])
        lower = sb("lower", [P, P])
        degree = sb("degree", [P, T])
        whole = sb("whole", [P, T])
        upto = sb("upto", [P, T])
        tmp = sb("tmp", [P, T])
        zeros = sb("zeros", [P, J])
        ps = ctx.enter_context(nc.psum_tensor("st_ps", [P, 512], fp32))
        s_iota, s_in, s_ps, s_ch, s_zero, s_clear = (sem(n) for n in ("iota", "in", "ps", "ch", "zero", "clear"))
        block = ctx.enter_context(nc.Block())

        @block.gpsimd
        def _(pool):
            pool.iota(part[:], [[0, 1]], 0, 1, allow_small_or_imprecise_dtypes=True).then_inc(s_iota, 1)
            pool.iota(node[:], [[P, T]], EP, 1, allow_small_or_imprecise_dtypes=True).then_inc(s_iota, 1)

        @block.sync
        def _(sp):
            sp.wait_ge(s_zero, 1)
            to = k.edge_node[0:EP, :].rearrange("(p j) h -> p (j h)", j=J)
            for h in range(8):
                sp.dma_start(to[:, h * J:(h + 1) * J], zeros[:]).then_inc(s_clear, 16)
            sp.wait_ge(s_clear, 128)

        @block.tensor
        def _(pe):
            pe.wait_ge(s_in, 1)
            nc.tensor.matmul(ps[:, 0:T], lower[:], degree[:], start=True, stop=True)
            nc.tensor.matmul(ps[:, 64:64 + T], k.ones[:], degree[:], start=True, stop=True).then_inc(s_ps, 1)

        @block.vector
        def _(dve):
            v = nc.vector
            link = chained(dve, s_ch)
            v.memset(zeros[:], 0.0).then_inc(s_zero, 1)
            dve.wait_ge(s_iota, 2)
            link(v.tensor_scalar(lower[:], k.window_iota[:, 0, :], part[:, 0:1], None, ALU.is_gt))
            v.tensor_copy(degree[:], k.acc[:, :, D]).then_inc(s_in, 1)
            dve.wait_ge(s_ps, 1)
            link(v.tensor_copy(whole[:], ps[:, 64:64 + T]))
            link(v.tensor_tensor_scan(upto[:], k.ones[:, 0:T], whole[:], 0.0, ALU.mult, ALU.add))
            link(v.tensor_tensor(upto[:], upto[:], whole[:], ALU.subtract))
            link(v.tensor_tensor(upto[:], upto[:], ps[:, 0:T], ALU.add))
            link(v.tensor_scalar(k.alone[:], degree[:], 0.0, None, ALU.is_equal))
            link(v.tensor_tensor(tmp[:], node[:], upto[:], ALU.subtract))
            link(v.tensor_tensor(tmp[:], tmp[:], k.alone[:], ALU.mult))
            link(v.tensor_tensor(k.first_edge[:], upto[:], tmp[:], ALU.add))


def source_parts(nc, k):
    with ExitStack() as ctx:
        sb = lambda n, s, d=fp32: ctx.enter_context(nc.sbuf_tensor("sr_" + n, s, d))
        sem = lambda n: k.semaphore("sr_" + n)
        ints = sb("ints", [P, 2, J], i32)
        vals = sb("vals", [P, 2, J])
        s_in, s_ch, s_out, s_done = sem("in"), sem("ch"), sem("out"), sem("done")
        block = ctx.enter_context(nc.Block())
        flat = lambda a: a.rearrange("(p j) -> p j", j=J)

        @block.sync
        def _(sp):
            sp.dma_start(ints[:, 0, :], flat(k.src_by_column)).then_inc(s_in, 16)
            sp.dma_start(ints[:, 1, :], flat(k.src)).then_inc(s_in, 16)
            sp.wait_ge(s_out, 1)
            sp.dma_start(flat(k.src_low), vals[:, 0, :]).then_inc(s_done, 16)
            sp.dma_start(flat(k.src_high), vals[:, 1, :]).then_inc(s_done, 16)
            sp.wait_ge(s_done, 32)

        @block.vector
        def _(dve):
            v = nc.vector
            link = chained(dve, s_ch)
            dve.wait_ge(s_in, 32)
            link(v.tensor_scalar(ints[:, 0, :], ints[:, 0, :], P - 1, None, ALU.bitwise_and))
            link(v.tensor_scalar(ints[:, 1, :], ints[:, 1, :], 7, None, ALU.arith_shift_right))
            v.tensor_copy(vals[:], ints[:]).then_inc(s_out, 1)


def gat_lookup(nc, k, name, es):
    H, W = GHEADS, T * GHEADS
    with ExitStack() as ctx:
        sb = lambda n, s, d=fp32: ctx.enter_context(nc.sbuf_tensor(f"{name}_{n}", s, d))
        sem = lambda n: (k.semaphore(f"{name}_{n}"))
        low = sb("low", [P, WAYS, GW * P])
        hot = sb("hot", [P, 2, GW * P], bf16)
        pick = sb("pick", [P, 2, GW, T])
        product = sb("product", [P, 2, GW, W])
        part = sb("part", [P, 1])
        parts = sb("parts", [P, 3, W], bf16)
        left = sb("left", [P, W])
        whole = sb("whole", [P, W])
        high = sb("high", [P, J])
        to = sb("to", [P, 1], i32)
        node = sb("node", [P, 8])
        ps = ctx.enter_context(nc.psum_tensor(f"{name}_ps", [P, 2, 2, 512], fp32))
        s_high, s_iota, s_ch, s_parts, s_hot, s_rows, s_product, s_es, s_go, s_node = (
            sem(n) for n in ("s_high", "s_iota", "s_ch", "s_parts", "s_hot", "s_rows", "s_product", "s_es", "s_go", "s_node"))
        s_pick = sem("s_pick")
        s_low = [sem(f"s_low{g}") for g in range(WAYS)]
        s_put = sem("s_put")
        block = ctx.enter_context(nc.Block())
        groups, rest = J // GW, J % GW

        @block.sync
        def _(sp):
            sp.dma_start(high[:], k.src_high.rearrange("(p j) -> p j", j=J)).then_inc(s_high, 16)

            def load(kk, g, turn, n=GW):
                if after(kk, WAYS):
                    sp.wait_ge(s_hot, kk - (WAYS - 1))
                sp.dma_start(low[:, g, 0:n * P], k.src_low[ds(kk * GW * P, n * P)].partition_broadcast(P)).then_inc(s_low[g], 16)

            grouped(sp, groups, load, ways=WAYS)
            load(groups, groups % WAYS, groups // WAYS, rest)

        @block.gpsimd
        def _(pool):
            pool.iota(part[:], [[0, 1]], 0, 1, allow_small_or_imprecise_dtypes=True).then_inc(s_iota, 1)

            pool.wait_ge(s_iota, 1)

            def put(u):
                if after(u, 1):
                    pool.wait_ge(s_put, u * 16)
                pool.tensor_copy(to[:], k.first_edge[:, ds(u, 1)])
                pool.tensor_copy(node[:], k.node8[:, ds(u, 1), :].squeeze(1)).then_inc(s_node, 1)
                pool.wait_ge(s_node, u + 1)
                pool.sem_inc(s_go, 1)
                pool.indirect_dma_start(k.edge_node, bass.IndirectOffsetOnAxis(ap=to[:, 0:1], axis=0),
                                        node[:], None).then_inc(s_put, 16)

            def compare(kk, way, turn, n=GW):
                g = way % 2
                if after(kk, 2):
                    pool.wait_ge(s_rows, kk - 1)
                pool.wait_ge(s_low[way], turn * 16 + 16)
                pool.sem_inc(s_go, 1)
                pool.tensor_scalar(hot[:, g, 0:n * P], low[:, way, 0:n * P], part[:, 0:1], None, ALU.is_equal).then_inc(s_hot, 1)
                if way == 0:
                    put(turn)

            assert groups // WAYS == T - 1
            grouped(pool, groups, compare, ways=WAYS)
            compare(groups, groups % WAYS, groups // WAYS, rest)
            pool.wait_ge(s_put, 16 * T)

        @block.tensor
        def _(pe):
            pe.wait_ge(s_parts, 1)

            def rows(kk, way, turn, n=GW):
                g = way % 2
                pe.wait_ge(s_hot, kk + 1)
                if after(kk, 2):
                    pe.wait_ge(s_product, kk - 1)
                for q in range(n):
                    for m in range(3):
                        ins = nc.tensor.matmul(ps[:, g, q // 2, (q % 2) * W:(q % 2 + 1) * W], hot[:, g, q * P:(q + 1) * P],
                                               parts[:, m, :], start=(m == 0), stop=(m == 2))
                ins.then_inc(s_rows, 1)

            grouped(pe, groups, rows, ways=WAYS)
            rows(groups, groups % WAYS, groups // WAYS, rest)

        @block.vector
        def _(dve):
            v = nc.vector
            link = chained(dve, s_ch)
            link(v.tensor_copy(whole[:].rearrange("p (t h) -> p t h", h=H), k.node8[:, :, 0:H]))
            link(v.tensor_copy(left[:], whole[:]))
            for m in range(3):
                link(v.tensor_copy(parts[:, m, :], left[:]))
                link(v.tensor_tensor(left[:], left[:], parts[:, m, :], ALU.subtract))
            v.tensor_copy(whole[:], left[:]).then_inc(s_parts, 1)
            dve.wait_ge(s_high, 16)

            def pick_window(kk, g, n=GW):
                if after(kk, 2):
                    dve.wait_ge(s_product, kk - 1)
                v.tensor_tensor(pick[:, g, 0:n, :], k.window_iota[:, 0:n, 0:T], col(high[:, ds(kk * GW, n)], T), ALU.is_equal).then_inc(s_pick, 1)

            def multiply(kk, g, n=GW):
                if after(kk, 2):
                    dve.wait_ge(s_es, kk - 1)
                dve.wait_ge(s_pick, kk + 1)
                dve.wait_ge(s_rows, kk + 1)
                for b in range(-(-n // 2)):
                    c = min(2, n - 2 * b)
                    ins = v.tensor_tensor(product[:, g, 2 * b:2 * b + c, :].rearrange("p q (t h) -> p (q t) h", h=H),
                                          ps[:, g, b, 0:c * W].rearrange("p (a h) -> p a h", h=H),
                                          col(pick[:, g, 2 * b:2 * b + c, :].rearrange("p q t -> p (q t)"), H), ALU.mult)
                ins.then_inc(s_product, 1)

            def add(kk, g, n=GW):
                dve.wait_ge(s_product, kk + 1)
                v.tensor_reduce(es[:, ds(kk * GW, n), :], product[:, g, 0:n, :].rearrange("p q (t h) -> p q h t", h=H),
                                AX.X, ALU.add).then_inc(s_es, 1)

            pick_window(0, 0)

            def choose(kk, way, turn):
                multiply(kk, way % 2)
                if before(kk, groups - 1):
                    pick_window(kk + 1, 1 - way % 2)
                add(kk, way % 2)

            grouped(dve, groups, choose, last=WAYS + 1, ways=WAYS)
            pick_window(groups, groups % 2, rest)
            multiply(groups, groups % 2, rest)
            add(groups, groups % 2, rest)


def gat_softmax(nc, k, name, es):
    H = GHEADS
    with ExitStack() as ctx:
        sb = lambda n, s, d=fp32: ctx.enter_context(nc.sbuf_tensor(f"{name}_{n}", s, d))
        sem = lambda n: (k.semaphore(f"{name}_{n}"))
        flat = k.acc[:].rearrange("p t w -> p (t w)")
        cut = lambda lo, w: flat[:, lo * J:(lo + w) * J].rearrange("p (j w) -> p j w", w=w)
        out, fwd, bwd = cut(0, 8), cut(8, H), cut(12, H)
        ints = k.step_w[:].rearrange("p s h -> p (s h)")[:, 0:3 * J].rearrange("p (q j) -> p q j", j=J).bitcast(i32)
        node = k.step_w[:].rearrange("p s h -> p (s h)")[:, 0:8 * J].rearrange("p (j w) -> p j w", w=8)
        tmp = sb("tmp", [P, J, H])
        same = sb("same", [P, 2, J])
        gate = tmp[:].rearrange("p j h -> p (j h)")[:, 0:2 * J].rearrange("p (w j) -> p w j", j=J)
        s_in, s_ch, s_shift, s_exp, s_w, s_out = (sem(n) for n in ("s_in", "s_ch", "s_shift", "s_exp", "s_w", "s_out"))
        spread = segmented_scan(nc, k, ctx, name + "_n", [(node[:, :, q], out[:, :, q], same[:, 0, :], False) for q in range(8)],
                                ALU.mult, ALU.add, 0.0)
        tops = [segmented_scan(nc, k, ctx, f"{name}_m{way}", [(o[:, :, h], es[:, :, h], gate[:, way, :], way == 1) for h in range(H)],
                               ALU.add, ALU.max, -BIG) for way, o in enumerate((fwd, bwd))]
        block = ctx.enter_context(nc.Block())

        @block.sync
        def _(sp):
            for q, first in enumerate((1, 0, 2)):
                sp.dma_start(ints[:, q, :], k.dst_ext[first:first + EP].rearrange("(p j) -> p j", j=J)).then_inc(s_in, 16)
            sp.dma_start(out, k.edge_node[0:EP, :].rearrange("(p j) h -> p j h", j=J)).then_inc(s_in, 16)
            sp.wait_ge(s_w, 1)
            sp.dma_start(k.weight_dram.rearrange("(p j) h -> p j h", j=J), out).then_inc(s_out, 16)
            sp.wait_ge(s_out, 16)

        @block.tensor
        def _(pe):
            spread[1](k.ident[:])
            for s in tops:
                s[1](k.ident[:])

        @block.scalar
        def _(act):
            act.wait_ge(s_shift, 1)
            nc.scalar.activation(out, out, ACT.Exp).then_inc(s_exp, 1)

        @block.vector
        def _(dve):
            v = nc.vector
            link = chained(dve, s_ch)
            dve.wait_ge(s_in, 64)
            for way in range(2):
                link(v.tensor_tensor(same[:, way, :], ints[:, 0, :], ints[:, 1 + way, :], ALU.is_equal))
            link(v.tensor_scalar(gate, same[:], -1.0, BIG, ALU.add, ALU.mult))
            spread[0](link)
            for s in tops:
                s[0](link)
            own, to = node[:, :, 0:H], node[:, :, H:2 * H]

            def leaky(o, a):
                link(v.tensor_tensor(tmp[:], a, to, ALU.add))
                link(v.scalar_tensor_tensor(o, tmp[:], 0.2, tmp[:], ALU.mult, ALU.max))

            link(v.tensor_tensor(fwd, fwd, bwd, ALU.max))
            link(v.tensor_tensor(fwd, fwd, own, ALU.max))
            leaky(bwd, fwd)
            leaky(fwd, es)
            link(v.tensor_tensor(out[:, :, 0:H], fwd, bwd, ALU.subtract))
            leaky(fwd, own)
            v.tensor_tensor(out[:, :, H:2 * H], fwd, bwd, ALU.subtract).then_inc(s_shift, 1)
            link(v.tensor_scalar(same[:, 1, :], same[:, 1, :], -1.0, 1.0, ALU.mult, ALU.add))
            dve.wait_ge(s_exp, 1)
            v.tensor_tensor(out[:, :, H:2 * H], out[:, :, H:2 * H], col(same[:, 1, :], H), ALU.mult).then_inc(s_w, 1)


def gat_update(nc, k, name, bias, residual):
    H = GHEADS
    CH = 7
    chunks = T // CH
    with ExitStack() as ctx:
        sb = lambda n, s, d=fp32: ctx.enter_context(nc.sbuf_tensor(f"{name}_{n}", s, d))
        sem = lambda n: (k.semaphore(f"{name}_{n}"))
        own = sb("own", [P, T, H])
        inverse = sb("inverse", [P, T, H])
        b = sb("b", [P, D])
        row = sb("row", [P, 2, CH, D])
        s_b, s_ch, s_done = sem("s_b"), sem("s_ch"), sem("s_done")
        s_row = [sem(f"s_row{g}") for g in range(2)]
        block = ctx.enter_context(nc.Block())

        @block.sync
        def _(sp):
            sp.dma_start(b[:], bias.partition_broadcast(P)).then_inc(s_b, 16)

            rows = k.h_table.rearrange("(t p) w -> p t w", p=P)
            for c in range(chunks):
                if c >= 2:
                    sp.wait_ge(s_done, c - 1)
                sp.dma_start(row[:, c % 2, :, :], rows[:, c * CH:(c + 1) * CH, 0:D]).then_inc(s_row[c % 2], 16)

        @block.vector
        def _(dve):
            v = nc.vector
            link = chained(dve, s_ch)
            link(v.tensor_tensor(own[:], k.acc[:, :, D + H:D + 2 * H], col(k.alone[:], H), ALU.add))
            link(v.tensor_tensor(inverse[:], own[:], k.acc[:, :, D:D + H], ALU.add))
            link(v.tensor_scalar(inverse[:], inverse[:], 1e-16, None, ALU.add))
            link(v.reciprocal(inverse[:], inverse[:]))
            dve.wait_ge(s_b, 16)

            heads = lambda a: a.rearrange("p t (h d) -> p (t h) d", d=GHID)
            per = lambda a, t: col(a[:, t, :].rearrange("p t h -> p (t h)"), GHID)
            for c in range(chunks):
                t = slice(c * CH, (c + 1) * CH)
                dve.wait_ge(s_row[c % 2], (c // 2) * 16 + 16)
                r = row[:, c % 2, :, :]
                link(v.tensor_tensor(heads(r), heads(r), per(own, t), ALU.mult))
                link(v.tensor_tensor(r, r, k.acc[:, t, 0:D], ALU.add))
                link(v.tensor_tensor(heads(r), heads(r), per(inverse, t), ALU.mult))
                link(v.tensor_tensor(r, r, b[:].unsqueeze(1).to_broadcast([P, CH, D]), ALU.add))
                if residual:
                    v.scalar_tensor_tensor(k.x_now[:, t, :], r, 0.0, k.x_now[:, t, :], ALU.max, ALU.add).then_inc(s_done, 1)
                else:
                    v.tensor_scalar(k.acc[:, t, 0:D], r, 0.0, None, ALU.max).then_inc(s_done, 1)



def mlp_aggregate(nc, k):
    with ExitStack() as ctx:
        sb = lambda n, s, d=fp32: ctx.enter_context(nc.sbuf_tensor("ml_" + n, s, d))
        ps = lambda n, s: ctx.enter_context(nc.psum_tensor("ml_ps_" + n, s, fp32))
        sem = lambda n: (k.semaphore("ml_" + n))
        w = sb("w", [DE, D])
        tile_of = sb("tile_of", [1, S], i32)
        s_tiles, s_go_sp, s_go_pe = sem("tiles"), sem("go_sp"), sem("go_pe")
        at = sb("at", [P, WAYS, GW], i32)
        got = sb("got", [P, WAYS, GW, D])
        attr = sb("attr", [P, WAYS, GW, DE])
        attrT = sb("attrT", [DE, 2, GW, P])
        hot = sb("hot", [P, WAYS, GW, P])
        p_turn = ps("turn", [P, 512])
        p_edge = ps("edge", [P, GW, D])
        p_sum = ps("sum", [P, 2, GW, D])
        s_w, s_staged, s_go, s_turn, s_turned, s_edge, s_pre, s_hot, s_message, s_summed, s_added, s_zero = (
            sem(n) for n in ("s_w", "staged", "go", "turn_s", "turned", "edge_s", "pre", "hot_s", "message_s", "summed", "added", "zero"))
        s_got = [sem(f"got{g}") for g in range(WAYS)]
        s_attr = [sem(f"attr{g}") for g in range(WAYS)]
        block = ctx.enter_context(nc.Block())
        groups = S // GW

        @block.sync
        def _(sp):
            sp.dma_start(w[:], k.L2_W[D:D + DE, :]).then_inc(s_w, 16)
            sp.dma_start(tile_of[:], k.step_tile).then_inc(s_tiles, 16)
            sp.wait_ge(s_tiles, 16)
            registers = [sp.alloc_register(f"ml_tile{q}") for q in range(GW)]

            def load(kk, g, turn):
                if after(kk, WAYS):
                    sp.wait_ge(s_turn, kk - (WAYS - 1))
                    sp.sem_inc(s_go_sp, 1)
                tiles = four(sp, registers, tile_of, kk, C - 1)
                for q in range(GW):
                    sp.dma_start(attr[:, g, q, :], k.edge_attr[ds(tiles[q] * P, P), :]).then_inc(s_attr[g], 16)

            grouped(sp, groups, load, ways=WAYS)

        @block.gpsimd
        def _(pool):
            def gather(kk, g, turn):
                pool.wait_ge(s_staged, kk + 1)
                if after(kk, WAYS):
                    pool.wait_ge(s_summed, (kk - (WAYS - 1)) * GW)
                pool.sem_inc(s_go, 1)
                for q in range(GW):
                    pool.indirect_dma_start(got[:, g, q, :], None, k.p_table,
                                            bass.IndirectOffsetOnAxis(ap=at[:, g, q:q + 1], axis=0)).then_inc(s_got[g], 16)

            grouped(pool, groups, gather, ways=WAYS)

        @block.scalar
        def _(act):
            def stage(kk, g, turn):
                if after(kk, WAYS):
                    act.wait_ge(s_got[g], turn * (16 * GW))
                nc.scalar.activation(at[:, g, :], k.src_step[:, ds(kk * GW, GW)], ACT.Copy).then_inc(s_staged, 1)

            def turned(kk, g):
                act.wait_ge(s_turn, kk + 1)
                if after(kk, 2):
                    act.wait_ge(s_edge, kk - 1)
                nc.scalar.activation(attrT[:, g, :, :], p_turn[0:DE, :].rearrange("p (q n) -> p q n", n=P), ACT.Copy).then_inc(s_turned, 1)

            for kk in range(WAYS - 1):
                stage(kk, kk, 0)
            turned(0, 0)

            def silu(kk, way, turn):
                g = way % 2
                if before(kk, groups - (WAYS - 1)):
                    stage(kk + (WAYS - 1), (way - 1) % WAYS, turn + (way > 0))
                if before(kk, groups - 1):
                    turned(kk + 1, 1 - g)
                act.wait_ge(s_pre, kk + 1)
                nc.scalar.activation(got[:, way, :, :], got[:, way, :, :], ACT.Silu).then_inc(s_message, 1)

            grouped(act, groups, silu, last=WAYS, ways=WAYS)

        @block.tensor
        def _(pe):
            def turn_attr(kk, way, turn):
                pe.wait_ge(s_attr[way], turn * (16 * GW) + 16 * GW)
                if after(kk, 1):
                    pe.wait_ge(s_turned, kk)
                pe.sem_inc(s_go_pe, 1)
                for q in range(GW):
                    ins = nc.tensor.transpose(p_turn[0:DE, q * P:(q + 1) * P], attr[:, way, q, :], k.ident[:])
                ins.then_inc(s_turn, 1)

            def edge(kk, g):
                pe.wait_ge(s_turned, kk + 1)
                if after(kk, 1):
                    pe.wait_ge(s_pre, kk)
                for q in range(GW):
                    ins = nc.tensor.matmul(p_edge[:, q, :], attrT[:, g, q, :], w[:], start=True, stop=True)
                ins.then_inc(s_edge, 1)

            def sums(kk, way):
                g = way % 2
                pe.wait_ge(s_message, kk + 1)
                pe.wait_ge(s_hot, kk + 1)
                if after(kk, 2):
                    pe.wait_ge(s_added, kk * GW - GW)
                for q in range(GW):
                    nc.tensor.matmul(p_sum[:, g, q, :], hot[:, way, q, :], got[:, way, q, :],
                                     start=True, stop=True).then_inc(s_summed, 1)

            pe.wait_ge(s_w, 16)
            turn_attr(0, 0, 0)

            def body(kk, way, turn):
                g = way % 2
                edge(kk, g)
                if before(kk, groups - 1):
                    turn_attr(kk + 1, (way + 1) % WAYS, turn + (way == WAYS - 1))
                if after(kk, 1):
                    sums(kk - 1, (way - 1) % WAYS)

            grouped(pe, groups, body, last=WAYS, ways=WAYS)
            sums(groups - 1, (groups - 1) % WAYS)

        @block.vector
        def _(dve):
            v = nc.vector
            v.memset(k.acc[:], 0.0).then_inc(s_zero, 1)
            dve.wait_ge(s_zero, 1)

            def pre(kk, way, turn):
                if after(kk, WAYS):
                    dve.wait_ge(s_summed, (kk - (WAYS - 1)) * GW)
                v.tensor_tensor(hot[:, way, :, :], k.window_iota[:],
                                col(k.place[:, ds(kk * GW, GW)], P), ALU.is_equal).then_inc(s_hot, 1)
                dve.wait_ge(s_edge, kk + 1)
                dve.wait_ge(s_got[way], turn * (16 * GW) + 16 * GW)
                v.tensor_tensor(got[:, way, :, :], got[:, way, :, :], p_edge[:], ALU.add).then_inc(s_pre, 1)

            registers = [v.alloc_register(f"ml_window{q}") for q in range(GW)]

            def add(kk, g):
                windows = four(v, registers, k.step_window, kk, T - 1)
                for q in range(GW):
                    dve.wait_ge(s_summed, kk * GW + (q // 2 * 2 + 2))
                    if after(kk, 1) or q:
                        dve.wait_ge(s_added, kk * GW + q)
                    o = k.acc[:, ds(windows[q], 1), 0:D].squeeze(1)
                    v.tensor_tensor(o, o, p_sum[:, g, q, :], ALU.add).then_inc(s_added, 1)

            pre(0, 0, 0)

            def body(kk, way, turn):
                if before(kk, groups - 1):
                    pre(kk + 1, (way + 1) % WAYS, turn + (way == WAYS - 1))
                if after(kk, 1):
                    add(kk - 1, 1 - way % 2)

            grouped(dve, groups, body, last=WAYS, ways=WAYS)
            add(groups - 1, (groups - 1) % 2)



def norm_columns(nc, k):
    CH = 7
    chunks = T // CH
    full = N // P
    with ExitStack() as ctx:
        sb = lambda n, s, d=fp32: ctx.enter_context(nc.sbuf_tensor("bn_" + n, s, d))
        sem = lambda n: (k.semaphore("bn_" + n))
        square = sb("square", [P, 2, CH, D])
        both = sb("both", [P, 2, D])
        mean = sb("mean", [P, D])
        factor = sb("factor", [P, D])
        eps_col = sb("eps", [P, 1])
        ps = ctx.enter_context(nc.psum_tensor("bn_ps", [P, 2, 512], fp32))
        s_scale, s_ch, s_sum, s_var, s_centred, s_square, s_squares, s_root, s_eps = (
            sem(n) for n in ("scale", "ch", "sum", "var", "centred", "squared", "squares", "root", "epss"))
        acc = k.acc[:, :, 0:D]
        block = ctx.enter_context(nc.Block())

        @block.sync
        def _(sp):
            sp.dma_start(both[:, 0, :], k.L3_gamma.partition_broadcast(P)).then_inc(s_scale, 16)
            sp.dma_start(both[:, 1, :], k.L3_beta.partition_broadcast(P)).then_inc(s_scale, 16)

        @block.tensor
        def _(pe):
            def add(o, view, t):
                rows = N - full * P if t == full else P
                return nc.tensor.matmul(o, k.ones[0:rows, :], view[0:rows, :], start=(t == 0), stop=(t == T - 1))

            for t in range(T):
                ins = add(ps[:, 0, 0:D], acc[:, t, :], t)
            ins.then_inc(s_sum, 1)
            for c in range(chunks):
                pe.wait_ge(s_square, c + 1)
                for t in range(CH):
                    ins = add(ps[:, 1, 0:D], square[:, c % 2, t, :], c * CH + t)
                ins.then_inc(s_squares, 1)

        @block.scalar
        def _(act):
            for c in range(chunks):
                act.wait_ge(s_centred, c + 1)
                if c >= 2:
                    act.wait_ge(s_squares, c - 1)
                nc.scalar.activation(square[:, c % 2, :, :], acc[:, c * CH:(c + 1) * CH, :], ACT.Square).then_inc(s_square, 1)
            act.wait_ge(s_squares, chunks)
            act.wait_ge(s_eps, 1)
            nc.scalar.activation(factor[:], ps[:, 1, 0:D], ACT.Sqrt, bias=eps_col[:], scale=1.0 / N).then_inc(s_root, 1)

        @block.vector
        def _(dve):
            v = nc.vector
            link = chained(dve, s_ch)
            v.memset(eps_col[:], 1e-5).then_inc(s_eps, 1)
            wide = lambda a: a.unsqueeze(1).to_broadcast([P, CH, D])
            dve.wait_ge(s_sum, 1)
            link(v.tensor_scalar(mean[:], ps[:, 0, 0:D], 1.0 / N, None, ALU.mult))
            for c in range(chunks):
                t = slice(c * CH, (c + 1) * CH)
                v.tensor_tensor(acc[:, t, :], acc[:, t, :], wide(mean[:]), ALU.subtract).then_inc(s_centred, 1)
            dve.wait_ge(s_root, 1)
            link(v.reciprocal(factor[:], factor[:]))
            dve.wait_ge(s_scale, 32)
            link(v.tensor_tensor(factor[:], factor[:], both[:, 0, :], ALU.mult))
            dve.wait_ge(s_squares, chunks)
            for c in range(chunks):
                t = slice(c * CH, (c + 1) * CH)
                link(v.tensor_tensor(acc[:, t, :], acc[:, t, :], wide(factor[:]), ALU.mult))
                link(v.tensor_tensor(acc[:, t, :], acc[:, t, :], wide(both[:, 1, :]), ALU.add))


def build(nc, a, out, upto=99):
    k = Shared(nc)
    with ExitStack() as ctx:
        sb = lambda n, s, d=fp32: ctx.enter_context(nc.sbuf_tensor(n, s, d))
        dram = lambda n, s, d=fp32: nc.dram_tensor(n, s, d, kind="Internal").ap()
        k.x = a["x"]
        k.dst_ext = a["dst_ext"]
        k.src = a["src"]
        k.src_by_column = a["src_by_column"]
        k.src_low = nc.dram_tensor("src_low", [EP], fp32, kind="Internal").ap()
        k.src_high = nc.dram_tensor("src_high", [EP], fp32, kind="Internal").ap()
        k.rel = a["rel"]
        k.node_type = a["node_type"]
        k.edge_attr = a["edge_attr"]
        k.L0_Wk = a["L0_Wk"]
        k.L0_bk = a["L0_bk"]
        k.L0_Wq = a["L0_Wq"]
        k.L0_bq = a["L0_bq"]
        k.L0_Wv = a["L0_Wv"]
        k.L0_bv = a["L0_bv"]
        k.L0_Wa = a["L0_Wa"]
        k.L0_ba = a["L0_ba"]
        k.L0_rel_att = a["L0_rel_att"]
        k.L0_rel_msg = a["L0_rel_msg"]
        k.L0_rel_pri = a["L0_rel_pri"]
        k.L0_skip = a["L0_skip"]
        k.L1_W0 = a["L1_W0"]
        k.L1_a_src0 = a["L1_a_src0"]
        k.L1_a_dst0 = a["L1_a_dst0"]
        k.L1_b0 = a["L1_b0"]
        k.L1_W1 = a["L1_W1"]
        k.L1_a_src1 = a["L1_a_src1"]
        k.L1_a_dst1 = a["L1_a_dst1"]
        k.L1_b1 = a["L1_b1"]
        k.L2_W = a["L2_W"]
        k.L2_b = a["L2_b"]
        k.L2_gamma = a["L2_gamma"]
        k.L2_beta = a["L2_beta"]
        k.L3_weight = a["L3_weight"]
        k.L3_gamma = a["L3_gamma"]
        k.L3_beta = a["L3_beta"]
        k.out = out
        k.ident = sb("ident", [P, P])
        k.ones = sb("ones", [P, P])
        k.window_iota = sb("window_iota", [P, GW, P])
        k.pick = sb("pick", [P, CB, S])
        k.step_window = sb("step_window", [1, S], i32)
        k.src_step = sb("src_step", [P, S])
        k.pair_step = sb("pair_step", [P, S])
        k.place = sb("place", [P, S])
        k.type_int = sb("type_int", [P, T], i32)
        k.part = sb("part", [P, 1])
        k.type_mask = sb("type_mask", [P, T, TYPES])
        k.step_w = sb("step_w", [P, S, HEADS])
        flat = k.step_w[:].rearrange("p s h -> p (s h)")
        k.rows = flat[:, 0:4 * J].rearrange("p (j w) -> p j w", w=4)
        k.position = flat[:, 4 * J:5 * J]
        k.sorted_rows = dram("sorted_rows", [EP + 2, 4])
        k.place_row = dram("place_row", [S * P])
        k.step_tile = dram("step_tile", [1, S], i32)
        k.q_table = dram("q_table", [NP, D])
        k.kr_table = dram("kr_table", [NP * RELS, D])
        k.vr_table = dram("vr_table", [NP * RELS, D])
        k.weight_dram = dram("weight_dram", [EP, HEADS])

        for stage in (constants, plan_steps, steps_of_graph, sort_positions, hgt_tables):
            stage(nc, k)
        if upto < 1: return
        to_steps(nc, k, "ts_pair", k.sorted_rows[1:1 + EP, :].rearrange("(c p) w -> c (p w)", p=P), 4,
                 [(0, k.pair_step[:], 0.0)], False)
        place_rows(nc, k)
        hgt_scores(nc, k)
        with ExitStack() as scan:
            score = scan.enter_context(nc.sbuf_tensor("score", [P, J, HEADS], fp32))[:]
            scores_to_edges(nc, k, score)
            hgt_softmax(nc, k, score)
        to_steps(nc, k, "ts_w", k.weight_dram.rearrange("(c p) h -> c (p h)", p=P), HEADS,
                 [(h, k.step_w[:, :, h], 0.0) for h in range(HEADS)], False)
        if upto < 2: return
        k.acc = sb("acc", [P, T, HROW])
        aggregate(nc, k, "ag0", k.vr_table, D, k.pair_step[:], D, k.step_w[:], HEADS, count=True)
        if upto < 3: return
        k.x_now = sb("x_now", [P, T, D])
        k.node8 = sb("node8", [P, T, 8])
        k.first_edge = sb("first_edge", [P, T])
        k.alone = sb("alone", [P, T])
        k.h_table = dram("h_table", [NP, HROW])
        k.p_table = dram("p_table", [NP, D])
        k.edge_node = dram("edge_node", [EP + NP, 8])
        acc = k.acc[:, :, 0:D]
        k.recycle()
        source_parts(nc, k)
        hgt_update(nc, k)
        if upto < 3.5: return
        segment_starts(nc, k)
        norm_rows(nc, k, "n0", k.x_now[:], 1e-5)
        if upto < 4: return
        for n, (x, w, a_src, a_dst, bias) in enumerate(((k.x_now[:], k.L1_W0, k.L1_a_src0, k.L1_a_dst0, k.L1_b0),
                                                         (acc, k.L1_W1, k.L1_a_src1, k.L1_a_dst1, k.L1_b1))):
            node_products(nc, k, f"gp{n}", x, [(w, 0)], D, k.h_table, attention=(a_src, a_dst))
            with ExitStack() as scan:
                es = scan.enter_context(nc.sbuf_tensor(f"es{n}", [P, J, GHEADS], fp32))[:]
                gat_lookup(nc, k, f"gg{n}", es)
                gat_softmax(nc, k, f"gs{n}", es)
            to_steps(nc, k, f"tw{n}", k.weight_dram.rearrange("(c p) h -> c (p h)", p=P), HEADS,
                     [(h, k.step_w[:, :, h], 0.0) for h in range(HEADS)], False)
            aggregate(nc, k, f"ag{n + 1}", k.h_table, HROW, k.src_step[:], D, k.step_w[:], GHEADS, extra=8)
            gat_update(nc, k, f"gu{n}", bias, n == 1)
            if upto < 5 + n: return
            k.recycle()
        norm_rows(nc, k, "n1", k.x_now[:], 1e-5)
        node_products(nc, k, "mp", k.x_now[:], [(k.L2_W[0:D, :], 0)], D, k.p_table, bias=k.L2_b)
        mlp_aggregate(nc, k)
        if upto < 7: return
        norm_rows(nc, k, "n2", acc, 1e-3, scale=(k.L2_gamma, k.L2_beta))
        norm_rows(nc, k, "n3", k.x_now[:], 1e-5, other=acc)
        if upto < 8: return
        node_products(nc, k, "rp", k.x_now[:], [(k.L3_weight[r], r * D) for r in range(RELS)], RELS * D,
                      k.kr_table.rearrange("(n r) d -> n (r d)", r=RELS))
        aggregate(nc, k, "ag3", k.kr_table, D, k.pair_step[:], D)
        norm_columns(nc, k)
        norm_rows(nc, k, "n4", k.x_now[:], 1e-5, other=acc, store=k.out)


def lay_out(inputs):
    import numpy as np
    a = {n: np.ascontiguousarray(np.asarray(v)) for n, v in inputs.items()}
    ints = lambda v: np.ascontiguousarray(v, dtype=np.int32) if v.dtype == np.int32 else v
    pad = lambda v, n, fill: np.concatenate([v, np.full((n - v.shape[0],) + v.shape[1:], fill, v.dtype)])
    one = lambda x: np.full((1,), x, a["dst"].dtype)
    out = {
        "x": pad(a["x"], NP, 0),
        "dst_ext": np.concatenate([one(-1), pad(a["dst"], EP, NP - 1), one(-2)]),
        "src": pad(a["src"], EP, 0),
        "src_by_column": np.ascontiguousarray(pad(a["src"], EP, 0).reshape(P, J).T).reshape(-1),
        "rel": pad(a["edge_type_8"], EP, 0),
        "node_type": pad(a["node_type_4"], NP, 0),
        "edge_attr": pad(a["edge_attr_64"], EP, 0),
    }
    for n, v in a.items():
        if n.startswith("L"):
            out[n.replace("_gnn_", "_")] = v
    return out


def kernel(**inputs):
    import concourse.bacc as bacc
    from concourse.bass_utils import run_bass_kernel_spmd as run

    nc = bacc.Bacc("TRN2", target_bir_lowering=False, num_devices=1)
    arrays = {"in_" + n: v for n, v in lay_out(inputs).items()}
    aps = {n[3:]: nc.dram_tensor(n, v.shape, mybir.dt.from_np(v.dtype), kind="ExternalInput").ap()
           for n, v in arrays.items()}
    out = nc.dram_tensor("out_0", (N, D), fp32, kind="ExternalOutput").ap()
    build(nc, aps, out)
    r = run(nc, [arrays], core_ids=[0])
    return r.results[0]["out_0"]
```
